# Optimizing a Trainium2 kernel written in Bass

```python
import numpy as np
import jax
import jax.numpy as jnp

def _softmax(x, axis=-1):
    return jax.nn.softmax(x, axis=axis)

def _gelu(x):
    return jax.nn.gelu(x, approximate=True)

def _silu(x):
    return jax.nn.silu(x)

def _sigmoid(x):
    return jax.nn.sigmoid(x)

def _layernorm(x, axis=-1, eps=1e-05):
    m = jnp.mean(x, axis=axis, keepdims=True)
    v = jnp.var(x, axis=axis, keepdims=True)
    return (x - m) / jnp.sqrt(v + eps)

def _scatter_add(tgt, idx, src, axis=0):
    return tgt.at[idx].add(src)

def _segment_sum(src, seg, n):
    return jax.ops.segment_sum(src, seg, n)
kernel_name = 'mk_cond_resid_d4_seqx_r8_0f6c89'

def setup_inputs(seed: int=0):
    np.random.seed(seed)
    _w = jnp.asarray

    def _rec_inputs():
        import jax
        import jax.numpy as jnp
        _rk = jax.random.key(seed)
        x = 7.22e-05 + 1 * jax.random.normal(jax.random.fold_in(_rk, 1), (16, 128, 256), jnp.float32)
        _lenS = 128 - jax.random.randint(jax.random.fold_in(_rk, 7), (16,), 0, max(1, 128 // 4) + 1, jnp.int32)
        _lenS2 = 128 - jax.random.randint(jax.random.fold_in(_rk, 8), (16,), 0, max(1, 128 // 4) + 1, jnp.int32)
        cond_2048 = jax.random.bernoulli(jax.random.fold_in(_rk, 11), 0.8975, (16, 256)).astype(jnp.float32)
        return (x, cond_2048)
    x, cond_2048 = _rec_inputs()

    def _L0_cond_setup():
        import jax, jax.numpy as jnp
        import numpy as np
        import math
        D_MODEL = 128
        NUM_HEAD = 16
        NEG_INF = -1e+30
        key = jax.random.key(seed)
        k_x, k_m, k_q, k_k, k_v = jax.random.split(key, 5)
        B, C, T = (4, D_MODEL, 256)
        x = jax.random.normal(k_x, (B, C, T), dtype=jnp.float32)
        mask = (jax.random.uniform(k_m, (B, T)) < 0.9).astype(jnp.float32)
        limit = math.sqrt(6.0 / (C + C))
        Wq = jax.random.uniform(k_q, (C, C), minval=-limit, maxval=limit, dtype=jnp.float32)
        Wk = jax.random.uniform(k_k, (C, C), minval=-limit, maxval=limit, dtype=jnp.float32)
        Wv = jax.random.uniform(k_v, (C, C), minval=-limit, maxval=limit, dtype=jnp.float32)
        b = jnp.zeros((1,), dtype=jnp.float32)
        return {'x': x, 'mask': mask, 'Wq': Wq, 'Wk': Wk, 'Wv': Wv, 'b': b}
    _L0_cond_all = _L0_cond_setup()
    _L0_cond_in = {k: v for k, v in _L0_cond_all.items() if k in ('Wq', 'Wk', 'Wv', 'b')}
    del _L0_cond_all

    def _L1_cond_setup():
        import jax, jax.numpy as jnp
        import numpy as np
        B, T, D = (16, 128, 256)
        key = jax.random.key(seed)
        k0, k1, k2, k3 = jax.random.split(key, 4)
        scale = 1.0 / np.sqrt(D)
        return {'initial_state': jax.random.normal(k0, (B, D), jnp.float32), 'inputs': jax.random.normal(k1, (B, T, D), jnp.float32), 'W_ih': jax.random.normal(k2, (D, 3 * D), jnp.float32) * scale, 'W_hh': jax.random.normal(k3, (D, 3 * D), jnp.float32) * scale, 'b_ih': jnp.zeros((3 * D,), jnp.float32), 'b_hh': jnp.zeros((3 * D,), jnp.float32)}
    _L1_cond_all = _L1_cond_setup()
    _L1_cond_in = {k: v for k, v in _L1_cond_all.items() if k in ('W_ih', 'W_hh', 'b_ih', 'b_hh')}
    del _L1_cond_all

    def _L2_cond_setup():
        import jax, jax.numpy as jnp
        import numpy as np
        DT = 0.01
        EPSILON = 0.08
        ALPHA = 0.7
        BETA = 0.8
        CLAMP = 20.0
        B, T, N = (32, 128, 256)

        def _derivative(q, p, drive, coupling, bias):
            i_couple = jnp.tanh(q) @ coupling.T
            dq = q - q ** 3 / 3.0 - p + drive + i_couple + bias
            dp = EPSILON * (q + ALPHA - BETA * p)
            return (dq, dp)

        def _rk4_step(q, p, drive, coupling, bias):
            dq1, dp1 = _derivative(q, p, drive, coupling, bias)
            dq2, dp2 = _derivative(q + 0.5 * DT * dq1, p + 0.5 * DT * dp1, drive, coupling, bias)
            dq3, dp3 = _derivative(q + 0.5 * DT * dq2, p + 0.5 * DT * dp2, drive, coupling, bias)
            dq4, dp4 = _derivative(q + DT * dq3, p + DT * dp3, drive, coupling, bias)
            q_next = q + DT / 6.0 * (dq1 + 2 * dq2 + 2 * dq3 + dq4)
            p_next = p + DT / 6.0 * (dp1 + 2 * dp2 + 2 * dp3 + dp4)
            q_next = jnp.clip(q_next, -CLAMP, CLAMP)
            p_next = jnp.clip(p_next, -CLAMP, CLAMP)
            return (q_next, p_next)
        key = jax.random.key(seed)
        k1, k2, k3, k4 = jax.random.split(key, 4)
        return {'q0': jax.random.normal(k1, (B, N), dtype=jnp.float32), 'p0': jax.random.normal(k2, (B, N), dtype=jnp.float32), 'input_drive_seq': jax.random.normal(k3, (B, T, N), dtype=jnp.float32), 'coupling': jax.random.normal(k4, (N, N), dtype=jnp.float32) * 0.01, 'bias': jnp.zeros((N,), dtype=jnp.float32)}
    _L2_cond_all = _L2_cond_setup()
    _L2_cond_in = {k: v for k, v in _L2_cond_all.items() if k in ('coupling', 'bias')}
    del _L2_cond_all

    def _L3_cond_setup():
        import jax, jax.numpy as jnp
        import numpy as np
        HEADS = 16
        EPS = 1e-06

        def _rms_norm(x, g):
            xf = x.astype(jnp.float32)
            y = xf * jax.lax.rsqrt(jnp.mean(xf * xf, axis=-1, keepdims=True) + EPS)
            return y.astype(x.dtype) * g
        key = jax.random.key(seed)
        ks = jax.random.split(key, 6)
        b, n, dim, emb_dim = (4, 256, 256, 256)
        d_head = dim // HEADS
        return {'x': jax.random.normal(ks[0], (b, n, dim), jnp.float32), 'emb': jax.random.normal(ks[1], (b, 1, emb_dim), jnp.float32), 'W_emb': jax.random.normal(ks[2], (emb_dim, 2 * dim), jnp.float32) * emb_dim ** (-0.5), 'b_emb': jnp.zeros((2 * dim,), jnp.float32), 'g_norm': jnp.ones((dim,), jnp.float32), 'W_qkv': jax.random.normal(ks[3], (dim, 3 * dim), jnp.float32) * dim ** (-0.5), 'g_q': jnp.ones((d_head,), jnp.float32), 'g_k': jnp.ones((d_head,), jnp.float32), 'W_out': jax.random.normal(ks[4], (dim, dim), jnp.float32) * dim ** (-0.5)}
    _L3_cond_all = _L3_cond_setup()
    _L3_cond_in = {k: v for k, v in _L3_cond_all.items() if k in ('W_emb', 'b_emb', 'g_norm', 'W_qkv', 'g_q', 'g_k', 'W_out')}
    del _L3_cond_all
    return {'x': x, 'cond_2048': cond_2048, 'L0_cond_Wq': _L0_cond_in['Wq'], 'L0_cond_Wk': _L0_cond_in['Wk'], 'L0_cond_Wv': _L0_cond_in['Wv'], 'L0_cond_b': _L0_cond_in['b'], 'L1_cond_W_ih': _L1_cond_in['W_ih'], 'L1_cond_W_hh': _L1_cond_in['W_hh'], 'L1_cond_b_ih': _L1_cond_in['b_ih'], 'L1_cond_b_hh': _L1_cond_in['b_hh'], 'L2_cond_coupling': _L2_cond_in['coupling'], 'L2_cond_bias': _L2_cond_in['bias'], 'L3_cond_W_emb': _L3_cond_in['W_emb'], 'L3_cond_b_emb': _L3_cond_in['b_emb'], 'L3_cond_g_norm': _L3_cond_in['g_norm'], 'L3_cond_W_qkv': _L3_cond_in['W_qkv'], 'L3_cond_g_q': _L3_cond_in['g_q'], 'L3_cond_g_k': _L3_cond_in['g_k'], 'L3_cond_W_out': _L3_cond_in['W_out']}

def reference(x, cond_2048, L0_cond_Wq, L0_cond_Wk, L0_cond_Wv, L0_cond_b, L1_cond_W_ih, L1_cond_W_hh, L1_cond_b_ih, L1_cond_b_hh, L2_cond_coupling, L2_cond_bias, L3_cond_W_emb, L3_cond_b_emb, L3_cond_g_norm, L3_cond_W_qkv, L3_cond_g_q, L3_cond_g_k, L3_cond_W_out):
    import jax
    import jax.numpy as jnp

    def _L0_cond_ref(x, mask, Wq, Wk, Wv, b):
        import jax, jax.numpy as jnp
        import numpy as np
        import math
        D_MODEL = 128
        NUM_HEAD = 16
        NEG_INF = -1e+30
        B, C, T = x.shape
        H = NUM_HEAD
        Dh = C // H

        def proj(W):
            y = jnp.einsum('oc,bct->bto', W, x)
            return y.reshape(B, T, H, Dh).transpose(0, 2, 1, 3)
        Q, K, V = (proj(Wq), proj(Wk), proj(Wv))
        att = jnp.einsum('bhqd,bhkd->bhqk', Q, K) * (1.0 / math.sqrt(Dh))
        att = att + b[0]
        m = mask[:, None, None, :]
        att = att * m + (1.0 - m) * NEG_INF
        att = jax.nn.softmax(att, axis=-1)
        y = jnp.einsum('bhqk,bhkd->bhqd', att, V)
        y = y.transpose(0, 2, 1, 3).reshape(B, T, C)
        return y.transpose(0, 2, 1)

    def _L1_cond_ref(initial_state, inputs, W_ih, W_hh, b_ih, b_hh):
        import jax, jax.numpy as jnp
        import numpy as np
        B, T, D = (16, 128, 256)
        "ScanOverTime(GRU cell): sequential per-timestep module call with\n            dict-state passing; merge_dict_trees stacks the per-step\n            'state_predicted' tensors along axis=1 -> [B, T, D]."

        def cell(h, x):
            gi = x @ W_ih + b_ih
            gh = h @ W_hh + b_hh
            i_r, i_z, i_n = jnp.split(gi, 3, axis=-1)
            h_r, h_z, h_n = jnp.split(gh, 3, axis=-1)
            r = jax.nn.sigmoid(i_r + h_r)
            z = jax.nn.sigmoid(i_z + h_z)
            n = jnp.tanh(i_n + r * h_n)
            h_new = (1.0 - z) * n + z * h
            return (h_new, h_new)
        xs = jnp.swapaxes(inputs, 0, 1)
        _, hs = jax.lax.scan(cell, initial_state, xs)
        return jnp.swapaxes(hs, 0, 1)

    def _L2_cond_ref(q0, p0, input_drive_seq, coupling, bias):
        import jax, jax.numpy as jnp
        import numpy as np
        DT = 0.01
        EPSILON = 0.08
        ALPHA = 0.7
        BETA = 0.8
        CLAMP = 20.0
        B, T, N = (32, 128, 256)

        def _derivative(q, p, drive, coupling, bias):
            i_couple = jnp.tanh(q) @ coupling.T
            dq = q - q ** 3 / 3.0 - p + drive + i_couple + bias
            dp = EPSILON * (q + ALPHA - BETA * p)
            return (dq, dp)

        def _rk4_step(q, p, drive, coupling, bias):
            dq1, dp1 = _derivative(q, p, drive, coupling, bias)
            dq2, dp2 = _derivative(q + 0.5 * DT * dq1, p + 0.5 * DT * dp1, drive, coupling, bias)
            dq3, dp3 = _derivative(q + 0.5 * DT * dq2, p + 0.5 * DT * dp2, drive, coupling, bias)
            dq4, dp4 = _derivative(q + DT * dq3, p + DT * dp3, drive, coupling, bias)
            q_next = q + DT / 6.0 * (dq1 + 2 * dq2 + 2 * dq3 + dq4)
            p_next = p + DT / 6.0 * (dp1 + 2 * dp2 + 2 * dp3 + dp4)
            q_next = jnp.clip(q_next, -CLAMP, CLAMP)
            p_next = jnp.clip(p_next, -CLAMP, CLAMP)
            return (q_next, p_next)
        drive_tbn = jnp.swapaxes(input_drive_seq, 0, 1)

        def scan_fn(carry, drive):
            q, p = carry
            q, p = _rk4_step(q, p, drive, coupling, bias)
            return ((q, p), q)
        (_, _), q_trace_tbn = jax.lax.scan(scan_fn, (q0, p0), drive_tbn)
        return jnp.swapaxes(q_trace_tbn, 0, 1)

    def _L3_cond_ref(x, emb, W_emb, b_emb, g_norm, W_qkv, g_q, g_k, W_out):
        import jax, jax.numpy as jnp
        import numpy as np
        HEADS = 16
        EPS = 1e-06

        def _rms_norm(x, g):
            xf = x.astype(jnp.float32)
            y = xf * jax.lax.rsqrt(jnp.mean(xf * xf, axis=-1, keepdims=True) + EPS)
            return y.astype(x.dtype) * g
        b, n, dim = x.shape
        h = HEADS
        d = dim // h
        scale_shift = emb @ W_emb + b_emb
        scale, shift = jnp.split(scale_shift, 2, axis=-1)
        xn = _rms_norm(x, g_norm) * (1.0 + scale) + shift
        qkv = xn @ W_qkv
        qkv = qkv.reshape(b, n, 3, h, d)
        q, k, v = jnp.moveaxis(qkv, 2, 0)
        q = jnp.swapaxes(q, 1, 2)
        k = jnp.swapaxes(k, 1, 2)
        v = jnp.swapaxes(v, 1, 2)
        q = _rms_norm(q, g_q)
        k = _rms_norm(k, g_k)
        logits = jnp.einsum('bhqd,bhkd->bhqk', q, k) * d ** (-0.5)
        attn = jax.nn.softmax(logits, axis=-1)
        o = jnp.einsum('bhqk,bhkd->bhqd', attn, v)
        o = jnp.swapaxes(o, 1, 2).reshape(b, n, dim)
        return o + o @ W_out
    x = x + _L0_cond_ref(x, cond_2048, L0_cond_Wq, L0_cond_Wk, L0_cond_Wv, L0_cond_b)
    x = x + _L1_cond_ref(cond_2048, x, L1_cond_W_ih, L1_cond_W_hh, L1_cond_b_ih, L1_cond_b_hh)
    x = x + _L2_cond_ref(cond_2048, cond_2048, x, L2_cond_coupling, L2_cond_bias)
    x = x + _L3_cond_ref(x, cond_2048[:, None, :], L3_cond_W_emb, L3_cond_b_emb, L3_cond_g_norm, L3_cond_W_qkv, L3_cond_g_q, L3_cond_g_k, L3_cond_W_out)
    return x

_drawn_inputs = setup_inputs


def setup_inputs(seed=0):
    import zlib

    import numpy as np

    out = dict(_drawn_inputs(seed))
    spreads = {'L1_cond_b_ih': (0.0, 0.1),
     'L1_cond_b_hh': (0.0, 0.1),
     'L2_cond_bias': (0.0, 0.1),
     'L3_cond_b_emb': (0.0, 0.1),
     'L3_cond_g_norm': (1.0, 0.2),
     'L3_cond_g_q': (1.0, 0.6),
     'L3_cond_g_k': (1.0, 0.6)}
    factors = {}
    for name, (base, spread) in spreads.items():
        noise = np.random.default_rng([zlib.crc32(name.encode()), seed]).standard_normal(out[name].shape)
        drawn = base * np.exp(spread * noise) if base else spread * noise
        out[name] = jnp.asarray(drawn.astype(out[name].dtype))
    for name, factor in factors.items():
        out[name] = (out[name] * factor).astype(out[name].dtype)
    return out
```

```python
import numpy as np
import concourse.bass as bass
import concourse.mybir as mybir
from contextlib import ExitStack

FP32 = mybir.dt.float32
BF16 = mybir.dt.bfloat16
FP16 = mybir.dt.float16
ALU = mybir.AluOpType
ACT = mybir.ActivationFunctionType
AXIS_X = mybir.AxisListType.X

B = 16
T = 128
N = 256
KC = N // 128
SLOT = KC * B
HEADS = 16
D0 = T // HEADS
D3 = N // HEADS
GROUPS = 4
NEG = -1e30
EPS = 1e-6
CLAMP = 20.0
P_SHIFT = 0.7 / 0.8


def rk4_coefficients():
    dt, eps, beta = 0.01, 0.08, 0.8
    a = [dt / 2, dt / 2, dt, dt / 6]

    def unit(i):
        return [1.0 if j == i else 0.0 for j in range(5)]

    p_stage = [unit(0)]
    for s in range(3):
        c = a[s] * eps
        p_stage.append([unit(0)[i] + c * (unit(s + 1)[i] - beta * p_stage[s][i]) for i in range(5)])
    p_next = unit(0)
    for s, w in enumerate((1, 2, 2, 1)):
        p_next = [p_next[i] + dt * eps / 6 * w * (unit(s + 1)[i] - beta * p_stage[s][i]) for i in range(5)]
    rows = []
    for s in range(4):
        if s < 3:
            own = unit(1)
        else:
            own = [(-unit(1)[i] + unit(2)[i] + 2 * unit(3)[i] + unit(4)[i]) / 3 for i in range(5)]
        rows.append([own[i] - a[s] * p_stage[s][i] + a[s] * unit(s + 1)[i] for i in range(5)])
    return a, rows, p_next


def cond_resid_kernel(nc, x_cbn, x_seq, cond_rows, cond_t, wq_pad, wk_pad, wv_t, b0, w_ih, w_hh, b_ih, b_hh, b_hn,
                      coupling_t, bias_t, w_emb, b_emb, g_norm, w_qkv, g_q, g_k, w_out, identity_in, row_consts_in, out):
    ctx = ExitStack()
    with ctx:
        def sb(name, shape, dtype=FP32):
            return ctx.enter_context(nc.sbuf_tensor(name, shape, dtype))

        def sem(name):
            return ctx.enter_context(nc.semaphore(name))

        bank = [ctx.enter_context(nc.psum_tensor(f"bank{i}", [128, 512], FP32)) for i in range(8)]

        SEQ = sb("SEQ", [128, (T + 1) * SLOT])
        GI = sb("GI", [128, T * 96])
        seq = SEQ[:].rearrange("p (s k b) -> p s k b", k=KC, b=B)
        gi4 = GI[:].rearrange("p (t j b) -> p t j b", j=6, b=B)
        x_b0 = sb("x_b0", [128, N])
        identity = sb("identity", [128, 128])
        row_consts = sb("row_consts", [128, 5])
        wq_sb = sb("wq_sb", [128, GROUPS, 128]); wk_sb = sb("wk_sb", [128, GROUPS, 128]); wv_sb = sb("wv_sb", [128, T])
        b0_sb = sb("b0_sb", [128, 1]); k_const = sb("k_const", [128, 1])
        mask_rows = sb("mask_rows", [128, B, N])
        w_ih_sb = sb("w_ih_sb", [128, KC, 3 * N]); b_ih_sb = sb("b_ih_sb", [128, 6]); b_hh_sb = sb("b_hh_sb", [128, 6]); gate_bias = sb("gate_bias", [128, 6])
        WHHf = sb("WHHf", [128, KC, 3 * N]); WCf = sb("WCf", [128, KC, N])
        WHH = sb("WHH", [128, 3, KC, 3 * N], BF16); WC = sb("WC", [128, 3, KC, N], BF16)
        condT = sb("condT", [128, SLOT]); biasT = sb("biasT", [128, SLOT])
        bhn = sb("bhn", [1, N]); bhnp = sb("bhnp", [1, 3, N], BF16); bhn3 = sb("bhn3", [128, N], BF16); ones16 = sb("ones16", [128, B], BF16)
        w_emb_sb = sb("w_emb_sb", [128, KC, 2 * N]); b_emb_sb = sb("b_emb_sb", [128, 4]); b_emb1 = sb("b_emb1", [128, 4]); g_norm_sb = sb("g_norm_sb", [128, KC])
        gain_shift = sb("gain_shift", [128, 4, B])
        w_qkv_sb = sb("w_qkv_sb", [128, KC, 3 * N]); g_qk_sb = sb("g_qk_sb", [128, 2, HEADS, D3])
        w_out_sb = sb("w_out_sb", [128, KC, N]); mean_ones = sb("mean_ones", [128, 128]); minus_half = sb("minus_half", [128, 128])

        q_rows = sb("q_rows", [128, GROUPS, N]); k_rows = sb("k_rows", [128, GROUPS, N])
        v_sb = sb("v_sb", [128, KC, T])
        negmax0 = sb("negmax0", [128, 2, KC]); esum0 = sb("esum0", [128, KC, HEADS]); rsum0 = sb("rsum0", [128, KC, HEADS])
        probs0 = sb("probs0", [128, 2, KC, N]); probs0_t = sb("probs0_t", [128, 2, KC, N])
        y_sb = sb("y_sb", [128, KC, T])

        q_tile = sb("q_tile", [128, 4, 32]); q_clip = sb("q_clip", [128, 32])
        th_hi = sb("th_hi", [128, 2, 32], FP16); th_lo = sb("th_lo", [128, 2, 32], FP16)
        qsq = sb("qsq", [128, 2, 32]); qcube = sb("qcube", [128, 2, 32]); base = sb("base", [128, 2, 32])
        rlin = sb("rlin", [128, 4, 32]); rinit = sb("rinit", [128, 4, 32]); kp = sb("kp", [128, 5, 32])
        pacc = sb("pacc", [128, 4, 32]); pterm = sb("pterm", [128, 4, 32]); p_tile = sb("p_tile", [128, 32])
        drive = sb("drive", [128, 32]); dscaled = sb("dscaled", [128, 3, 32])
        h_tile = sb("h_tile", [128, 2, 16]); h_split = sb("h_split", [128, 2, 2, 16], FP16)
        gsum = sb("gsum", [128, 2, 64]); trz = sb("trz", [128, 64]); nmul = sb("nmul", [128, 32]); npre = sb("npre", [128, 32])
        ncand = sb("ncand", [128, 32]); hdiff = sb("hdiff", [128, 32]); hz = sb("hz", [128, 32]); omz = sb("omz", [128, 32])

        r1=sb("r1",[128,2])
        sq3 = sb("sq3", [128, KC, T]); x3_b = sb("x3_b", [128, KC, T]); mean_eps = sb("mean_eps", [128, T]); rstd3 = sb("rstd3", [128, T])
        xg = sb("xg", [128, KC, T]); xn = sb("xn", [128, KC, T])
        qk_sq = sb("qk_sq", [128, 2, HEADS, D3]); qk_sum = sb("qk_sum", [128, 2, HEADS]); qk_mean = sb("qk_mean", [128, 2, HEADS]); qk_rstd = sb("qk_rstd", [128, 2, HEADS])
        qk_n = sb("qk_n", [128, 2, HEADS, D3]); qk_pad = sb("qk_pad", [128, 2, HEADS, 32])
        v3_sb = sb("v3_sb", [128, N])
        q3_rows = sb("q3_rows", [128, GROUPS, T]); k3_rows = sb("k3_rows", [128, GROUPS, T])
        negmax3 = sb("negmax3", [128, 2, 4]); esum3 = sb("esum3", [128, HEADS]); rsum3 = sb("rsum3", [128, HEADS])
        probs3 = sb("probs3", [128, 2, 4, T]); probs3_t = sb("probs3_t", [128, 2, 4, T])
        o_sb = sb("o_sb", [128, N]); o_t = sb("o_t", [128, KC, T]); out_sb = sb("out_sb", [128, N])

        a2_ready = sem("a2_ready")
        base_done = sem("base_done")
        bias3 = sem("bias3")
        c_ready = sem("c_ready")
        cube_ready = sem("cube_ready")
        drive_ready = sem("drive_ready")
        dsc_ready = sem("dsc_ready")
        dve_setup = sem("dve_setup")
        emb_ready = sem("emb_ready")
        final_ready = sem("final_ready")
        first_loaded = sem("first_loaded")
        ga_done = sem("ga_done")
        gate_bias_ready = sem("gate_bias_ready")
        gi_a = sem("gi_a")
        gi_d = sem("gi_d")
        gi_ready = sem("gi_ready")
        gn_ready = sem("gn_ready")
        grz_ready = sem("grz_ready")
        h_ready = sem("h_ready")
        hh_ready = sem("hh_ready")
        hs_ready = sem("hs_ready")
        hz_done = sem("hz_done")
        init = sem("init")
        k0_copied = sem("k0_copied")
        k3_copied = sem("k3_copied")
        kp_ready = sem("kp_ready")
        kr0_ready = sem("kr0_ready")
        l0_tail = sem("l0_tail")
        m0_ready = sem("m0_ready")
        m3_ready = sem("m3_ready")
        mask_loaded = sem("mask_loaded")
        me3_ready = sem("me3_ready")
        ms3_ready = sem("ms3_ready")
        n_ready = sem("n_ready")
        nmul_done = sem("nmul_done")
        npre_ready = sem("npre_ready")
        o3_ready = sem("o3_ready")
        omz_ready = sem("omz_ready")
        ot3_copied = sem("ot3_copied")
        ot3_ready = sem("ot3_ready")
        out_ready = sem("out_ready")
        out_stored = sem("out_stored")
        p0_ready = sem("p0_ready")
        p3_ready = sem("p3_ready")
        p_ready = sem("p_ready")
        pool_done = sem("pool_done")
        pool_setup = sem("pool_setup")
        psum_done = sem("psum_done")
        pt0_a = sem("pt0_a")
        pt0_d = sem("pt0_d")
        pt3_copied = sem("pt3_copied")
        pterm_ready = sem("pterm_ready")
        pv0_ready = sem("pv0_ready")
        pv3_ready = sem("pv3_ready")
        q0_copied = sem("q0_copied")
        q3_copied = sem("q3_copied")
        q_ready = sem("q_ready")
        qc_ready = sem("qc_ready")
        qk3_ready = sem("qk3_ready")
        qk_mean_ready = sem("qk_mean_ready")
        qk_n_ready = sem("qk_n_ready")
        qk_rstd_ready = sem("qk_rstd_ready")
        qk_sq_ready = sem("qk_sq_ready")
        qk_sum_ready = sem("qk_sum_ready")
        qkt3_ready = sem("qkt3_ready")
        qkv3_ready = sem("qkv3_ready")
        qr0_ready = sem("qr0_ready")
        qs_ready = sem("qs_ready")
        ready = sem("ready")
        rinit0 = sem("rinit0")
        rinit_a = sem("rinit_a")
        rinit_b = sem("rinit_b")
        rs3_ready = sem("rs3_ready")
        rs_done = sem("rs_done")
        rsum3_ready = sem("rsum3_ready")
        s0_ready = sem("s0_ready")
        s3_ready = sem("s3_ready")
        seq_loaded = sem("seq_loaded")
        splits_ready = sem("splits_ready")
        sq3_ready = sem("sq3_ready")
        sq_done = sem("sq_done")
        t0_ready = sem("t0_ready")
        t3_ready = sem("t3_ready")
        t_ready = sem("t_ready")
        terms0 = sem("terms0")
        terms1 = sem("terms1")
        terms2 = sem("terms2")
        terms3 = sem("terms3")
        terms4 = sem("terms4")
        terms5 = sem("terms5")
        th_ready = sem("th_ready")
        tl_ready = sem("tl_ready")
        trz_ready = sem("trz_ready")
        v0_copied = sem("v0_copied")
        v0_ready = sem("v0_ready")
        v3_copied = sem("v3_copied")
        weights_loaded = sem("weights_loaded")
        x2_done = sem("x2_done")
        x3_done = sem("x3_done")
        x3_taken = sem("x3_taken")
        x_loaded = sem("x_loaded")
        xg_ready = sem("xg_ready")
        xn_ready = sem("xn_ready")
        y0_added = sem("y0_added")
        zh_done = sem("zh_done")
        a, Rc, Pc = rk4_coefficients()

        def C(s):
            return bank[s % 2][:, 0:32]
        Grz = bank[2][:, 0:128].rearrange("p (j w b) -> p j w b", j=4, w=2)
        Gn = bank[3][:, 0:32]

        def QP(s):
            return bank[4 + s % 2][:, 0:32]
        th_ps = bank[6][:, 0:64].rearrange("p (s n) -> p s n", s=2)

        with nc.Block() as block:
            @block.sync
            def _(sp):
                sp.dma_start(row_consts[:], row_consts_in).then_inc(first_loaded, 16)
                sp.dma_start(b0_sb[:], b0.broadcast_to([128, 1])).then_inc(first_loaded, 16)
                sp.dma_start(wq_sb[:], wq_pad).then_inc(first_loaded, 16)
                sp.dma_start(wk_sb[:], wk_pad).then_inc(first_loaded, 16)
                sp.dma_start(wv_sb[:], wv_t).then_inc(first_loaded, 16)
                sp.dma_start(identity[:], identity_in).then_inc(first_loaded, 16)
                sp.dma_start(x_b0[:], x_cbn[:, 0]).then_inc(x_loaded, 16)
                for i in range(4):
                    sp.dma_start(mask_rows[:, 4 * i:4 * i + 4], cond_rows[:, 4 * i:4 * i + 4].broadcast_to([128, 4, N])).then_inc(mask_loaded, 16)
                sp.dma_start(SEQ[:, SLOT:], x_seq).then_inc(seq_loaded, 16)
                for tile, source in ((condT, cond_t), (biasT, bias_t), (bhn, b_hn), (b_ih_sb, b_ih), (b_hh_sb, b_hh),
                                     (b_emb_sb, b_emb), (g_norm_sb, g_norm)):
                    sp.dma_start(tile[:], source).then_inc(weights_loaded, 16)
                for tile, source in ((WHHf, w_hh), (WCf, coupling_t), (w_ih_sb, w_ih), (w_emb_sb, w_emb), (w_qkv_sb, w_qkv), (w_out_sb, w_out)):
                    sp.dma_start(tile[:], source).then_inc(weights_loaded, 16)
                for i, gain in enumerate((g_q, g_k)):
                    sp.dma_start(g_qk_sb[:, i], gain.broadcast_to([128, HEADS, D3])).then_inc(weights_loaded, 16)
                with nc.Fori(0, B - 1, engines=(mybir.EngineType.SP,)) as b:
                    sp.wait_ge(v0_ready, b + 1)
                    sp.dma_start(x_b0[:].unsqueeze(1), x_cbn[:, bass.ds(b + 1, 1)]).then_inc(x_loaded, 16)
                sp.wait_ge(pool_setup, 16)
                sp.dma_start(bhn3[0:3, :], bhnp[:].rearrange("p w n -> p (w n)")).then_inc(bias3, 16)
                with nc.Fori(0, B, engines=(mybir.EngineType.SP,)) as b:
                    sp.wait_ge(out_ready, b + 1)
                    sp.dma_start(out[:, bass.ds(b, 1), :], out_sb[:].unsqueeze(1)).then_inc(out_stored, 16)
                sp.wait_ge(out_stored, 16 * B)

            @block.tensor
            def _(pe):
                mm = nc.tensor.matmul
                pe.wait_ge(first_loaded, 96)

                def l0_scores(b, h):
                    n = b * HEADS + h
                    g, j = h // 4, h % 4
                    if j == 0:
                        pe.wait_ge(q0_copied, b * 2 + g // 2 + 1)
                        pe.wait_ge(k0_copied, b * 2 + g // 2 + 1)
                    pe.wait_ge(p0_ready, n - 1 if h >= 2 else b * HEADS)
                    rows = slice(32 * j, 32 * j + 32)
                    for qc in range(KC):
                        i = mm(bank[h % 2][:, qc * N:(qc + 1) * N], q_rows[rows, g, qc * 128:(qc + 1) * 128], k_rows[rows, g], start=(qc == 0), stop=True, skip_group_check=True)
                    i.then_inc(s0_ready, 1)

                def l0_transposes(b, h):
                    n = b * HEADS + h
                    pe.wait_ge(p0_ready, n + 1)
                    pe.wait_ge(pt0_d if h % 2 else pt0_a, b * 8 + h // 2)
                    for kc in range(KC):
                        for qc in range(KC):
                            i = nc.tensor.transpose(bank[2 + h % 2][:, kc * N + qc * 128:kc * N + qc * 128 + 128], probs0[:, h % 2, qc, kc * 128:kc * 128 + 128], identity[:])
                    i.then_inc(t0_ready, 1)

                def l0_values(b, h):
                    n = b * HEADS + h
                    pe.wait_ge(pt0_d if h % 2 else pt0_a, b * 8 + h // 2 + 1)
                    if h == 0:
                        pe.wait_ge(v0_copied, b + 1)
                        pe.wait_ge(y0_added, b)
                    for qc in range(KC):
                        for kc in range(KC):
                            i = mm(bank[7][:, qc * T + h * D0:qc * T + h * D0 + D0], probs0_t[:, h % 2, kc, qc * 128:qc * 128 + 128], v_sb[:, kc, h * D0:h * D0 + D0],
                                   start=(h == 0 and qc == 0 and kc == 0), stop=(kc == KC - 1), skip_group_check=True)
                    i.then_inc(pv0_ready, 1)

                with nc.Fori(0, B, engines=(mybir.EngineType.PE,)) as b:
                    pe.wait_ge(x_loaded, (b + 1) * 16)
                    xb = x_b0[:]
                    for pair in range(2):
                        pe.wait_ge(q0_copied, b * 2 + pair)
                        pe.wait_ge(k0_copied, b * 2 + pair)
                        for w_sb, to, ready in ((wq_sb, 4, qr0_ready), (wk_sb, 5, kr0_ready)):
                            for i in range(2):
                                product = mm(bank[to][:, i * N:(i + 1) * N], w_sb[:, 2 * pair + i], xb, start=(i == 0), stop=True, skip_group_check=True)
                            product.then_inc(ready, 1)
                        if pair == 1:
                            pe.wait_ge(v0_copied, b)
                            for kc in range(KC):
                                i = mm(bank[6][:, kc * T:kc * T + T], x_b0[:, kc * 128:kc * 128 + 128], wv_sb[:], start=(kc == 0), stop=True, skip_group_check=True)
                            i.then_inc(v0_ready, 1)
                    for h in range(HEADS + 2):
                        if h < HEADS:
                            l0_scores(b, h)
                        if 1 <= h <= HEADS:
                            l0_transposes(b, h - 1)
                        if h >= 2:
                            l0_values(b, h - 2)

                pe.wait_ge(weights_loaded, 15 * 16)
                pe.wait_ge(v0_copied, B)
                for j in range(4):
                    for k in range(KC):
                        i = mm(bank[6][:, j * B:(j + 1) * B], w_emb_sb[:, k, j * 128:(j + 1) * 128], condT[:, k * B:(k + 1) * B], start=(j == 0 and k == 0), stop=(k == KC - 1), skip_group_check=True)
                i.then_inc(emb_ready, 1)
                pe.wait_ge(y0_added, B)
                with nc.Fori(0, 4, engines=(mybir.EngineType.PE,)) as c:
                    for j in range(6):
                        pe.wait_ge(gi_a if j % 2 == 0 else gi_d, c * 3)
                        for k in range(KC):
                            i = mm(bank[j][:].rearrange("p (t b) -> p t b", b=B), w_ih_sb[:, k, j * 128:(j + 1) * 128], seq[:, bass.ds(c * 32 + 1, 32), k, :], start=(k == 0), stop=(k == KC - 1), skip_group_check=True)
                        i.then_inc(gi_ready, 1)

                pe.wait_ge(splits_ready, 1)
                pe.wait_ge(gi_a, 12)
                pe.wait_ge(gi_d, 12)
                def coupling(t,s,parts,src,first,last):
                    i=0; n=len(parts)*4
                    for w in parts:
                        for m in range(2):
                            for k in range(2):
                                mm=nc.tensor.matmul(bank[s%2][:,m*16:m*16+16],WC[:,w,k,m*128:m*128+128],src[:,s%2,k*16:k*16+16],
                                    start=(first and i==0),stop=(last and i==n-1),skip_group_check=True)
                                i+=1
                    return mm
                def gru_products(dst,chunks,j0):
                    i=0
                    for j in chunks:
                        for w in range(3):
                            for k in range(2):
                                mm=nc.tensor.matmul(dst[:,j-j0],WHH[:,w,k,j*128:j*128+128],h_split[:,k],start=(i==0),stop=(i==len(chunks)*6-1),skip_group_check=True)
                                i+=1
                    return mm
                def gru(tau):
                    pe.wait_ge(hs_ready,tau+1)
                    gru_products(Grz,range(4),0).then_inc(grz_ready,1)
                def gru_n(tau):
                    for j in range(2):
                        dst=Gn[:,j*16:j*16+16]
                        nc.tensor.matmul(dst,bhn3[:,j*128:j*128+128],ones16[:],start=(j==0),stop=False,skip_group_check=True)
                        for w,half in ((0,0),(1,0),(2,0),(0,1),(1,1)):
                            for k in range(2):
                                mm=nc.tensor.matmul(dst,WHH[:,w,k,(4+j)*128:(5+j)*128],h_split[:,k,half],start=False,stop=(j==1 and k==1 and w==1 and half==1),skip_group_check=True)
                    mm.then_inc(gn_ready,1)
                def step(t,g):
                    for s in range(4):
                        pe.wait_ge(th_ready,t*4+s+1)
                        coupling(t,s,(0,1,2),th_hi,True,False)
                        pe.wait_ge(tl_ready,t*4+s+1)
                        coupling(t,s,(0,1),th_lo,False,True).then_inc(c_ready,1)
                        if g and s==0: gru(t+2)
                        if g and s==1: gru_n(t+2)
                pe.wait_ge(bias3,16)
                for tau in range(2):
                    gru(tau); gru_n(tau)
                with nc.Fori(0,(T-2)//2,engines=(mybir.EngineType.PE,)) as t:
                    for uu in range(2): step(t*2+uu,True)
                step(T-2,False); step(T-1,False)
                pe.wait_ge(qc_ready, T + 1)

                def l3_scores(b, g):
                    n = b * GROUPS + g
                    pe.wait_ge(p3_ready, n - 1 if g >= 2 else b * GROUPS)
                    rows = slice(32 * g, 32 * g + 32)
                    for j in range(4):
                        i = mm(bank[4 + g % 2][:, j * T:(j + 1) * T], q3_rows[rows, j], k3_rows[rows, j], start=(j == 0), stop=True, skip_group_check=True)
                    i.then_inc(s3_ready, 1)

                def l3_transposes(b, g):
                    n = b * GROUPS + g
                    pe.wait_ge(p3_ready, n + 1)
                    pe.wait_ge(pt3_copied, n - 1 if g >= 2 else b * GROUPS)
                    for j in range(4):
                        i = nc.tensor.transpose(bank[6 + g % 2][:, j * T:(j + 1) * T], probs3[:, g % 2, j], identity[:])
                    i.then_inc(t3_ready, 1)

                def l3_values(b, g):
                    n = b * GROUPS + g
                    pe.wait_ge(pt3_copied, n + 1)
                    for j in range(4):
                        h = 4 * j + g
                        i = mm(bank[2][:, h * D3:(h + 1) * D3], probs3_t[:, g % 2, j], v3_sb[:, h * D3:(h + 1) * D3], start=(h == 0), stop=True, skip_group_check=True)
                    i.then_inc(pv3_ready, 1)

                with nc.Fori(0, B, engines=(mybir.EngineType.PE,)) as b:
                    pe.wait_ge(sq3_ready, b + 1)
                    pe.wait_ge(v3_copied, b)
                    for k in range(KC):
                        i = mm(bank[0][:, 0:T], mean_ones[:], sq3[:, k], start=(k == 0), stop=(k == KC - 1), skip_group_check=True)
                    i.then_inc(ms3_ready, 1)
                    pe.wait_ge(xn_ready, b + 1)
                    pe.wait_ge(out_ready, b)
                    for k in range(KC):
                        mm(bank[1][:], xn[:, k], w_qkv_sb[:, k, 0:2 * N], start=(k == 0), stop=(k == KC - 1), skip_group_check=True)
                    for k in range(KC):
                        i = mm(bank[0][:, T:T + N], xn[:, k], w_qkv_sb[:, k, 2 * N:], start=(k == 0), stop=(k == KC - 1), skip_group_check=True)
                    i.then_inc(qkv3_ready, 1)
                    pe.wait_ge(qk3_ready, b + 1)
                    pe.wait_ge(o3_ready, b)
                    for w in range(2):
                        for g in range(GROUPS):
                            i = nc.tensor.transpose(bank[2 + w][:, g * T:(g + 1) * T], qk_pad[:, w, 4 * g:4 * g + 4].rearrange("p h d -> p (h d)"), identity[:])
                        i.then_inc(qkt3_ready, 1)
                    pe.wait_ge(q3_copied, b + 1)
                    pe.wait_ge(k3_copied, b + 1)
                    for g in range(GROUPS + 2):
                        if g < GROUPS:
                            l3_scores(b, g)
                        if 1 <= g <= GROUPS:
                            l3_transposes(b, g - 1)
                        if g >= 2:
                            l3_values(b, g - 2)
                    for k in range(KC):
                        mm(bank[1][:, k * 128:(k + 1) * 128], x3_b[:, k], identity[:], start=(k == 0), stop=False, skip_group_check=True)
                    pe.wait_ge(o3_ready, b + 1)
                    for k in range(KC):
                        i = nc.tensor.transpose(bank[3][:, k * 128:(k + 1) * 128], o_sb[:, k * 128:(k + 1) * 128], identity[:])
                    i.then_inc(ot3_ready, 1)
                    pe.wait_ge(ot3_copied, b + 1)
                    for k in range(KC):
                        i = mm(bank[1][:, 0:N], o_t[:, k], w_out_sb[:, k], start=False, stop=(k == KC - 1), skip_group_check=True)
                    i.then_inc(final_ready, 1)

            @block.scalar
            def _(act):
                with nc.Fori(0, B, engines=(mybir.EngineType.Activation,)) as b:
                    for pair in range(2):
                        act.wait_ge(qr0_ready, b * 2 + pair + 1)
                        act.wait_ge(s0_ready, b * HEADS)
                        nc.scalar.activation(q_rows[:, 2 * pair:2 * pair + 2].rearrange("p g n -> p (g n)"), bank[4][:], ACT.Identity, scale=1.0 / float(np.sqrt(D0)), bias=row_consts[:, 0:1]).then_inc(q0_copied, 1)
                    for h in range(HEADS + 1):
                        if h < HEADS:
                            n = b * HEADS + h
                            act.wait_ge(m0_ready, n + 1)
                            act.wait_ge(t0_ready, n - 1 if h >= 2 else b * HEADS)
                            if h == 0:
                                act.wait_ge(y0_added, b)
                            for qc in range(KC):
                                i = nc.scalar.activation(probs0[:, h % 2, qc], bank[h % 2][:, qc * N:(qc + 1) * N], ACT.Exp, bias=negmax0[:, h % 2, qc:qc + 1], accum_out=esum0[:, qc, h:h + 1])
                            i.then_inc(p0_ready, 1)
                        if h % 2 == 1:
                            n = b * HEADS + h - 1
                            act.wait_ge(t0_ready, n + 1)
                            act.wait_ge(pv0_ready, n - 1 if h >= 3 else b * HEADS)
                            nc.scalar.activation(probs0_t[:, 0].rearrange("p c k -> p (c k)"), bank[2][:], ACT.Copy).then_inc(pt0_a, 1)

                act.wait_ge(gate_bias_ready, 1)
                with nc.Fori(0, 4, engines=(mybir.EngineType.Activation,)) as c:
                    for j in (0, 2, 4):
                        act.wait_ge(gi_ready, c * 6 + j + 1)
                        nc.scalar.activation(gi4[:, bass.ds(c * 32, 32), j, :], bank[j][:].rearrange("p (t b) -> p t b", b=B), ACT.Identity, bias=gate_bias[:, j:j + 1]).then_inc(gi_a, 1)

                A=nc.scalar.activation
                def gates(tau):
                    act.wait_ge(a2_ready,tau+1)
                    A(trz[:],gsum[:,1],ACT.Tanh,scale=0.5).then_inc(trz_ready,1)
                def omzs(tau):
                    act.wait_ge(trz_ready,tau+1)
                    A(omz[:],trz[:,32:64],ACT.Copy,scale=-0.5,bias=0.5).then_inc(omz_ready,1)
                def cand(tau):
                    act.wait_ge(npre_ready,tau+1)
                    A(ncand[:],npre[:],ACT.Tanh).then_inc(n_ready,1)
                def hhi(tau):
                    act.wait_ge(h_ready,tau+2)
                    A(h_split[:,:,0,:],h_tile[:],ACT.Copy).then_inc(hh_ready,1)
                def drives(t):
                    act.wait_ge(drive_ready,t+1)
                    for i,c in enumerate((a[0],a[2],a[3])):
                        x=A(dscaled[:,i],drive[:],ACT.Copy,scale=c)
                    x.then_inc(dsc_ready,1)
                def step(t,g,prep):
                    for s in range(4):
                        act.wait_ge(q_ready,t*4+s+1)
                        A(th_hi[:,s%2],QP(s),ACT.Tanh).then_inc(th_ready,1)
                        A(th_ps[:,s%2],QP(s),ACT.Tanh).then_inc(t_ready,1)
                        if s==0:
                            if g: hhi(t+1)
                            act.wait_ge(qc_ready,t+1)
                            qv=q_clip[:]
                        else: qv=QP(s)
                        A(qsq[:,s%2],qv,ACT.Square).then_inc(sq_done,1)
                        if s==0:
                            act.wait_ge(p_ready,t+1)
                            A(kp[:,1],p_tile[:],ACT.Copy,scale=Rc[1][0]).then_inc(kp_ready,1)
                            A(kp[:,2],p_tile[:],ACT.Copy,scale=Rc[2][0])
                            A(kp[:,3],p_tile[:],ACT.Copy,scale=Rc[3][0]).then_inc(kp_ready,1)
                            A(kp[:,4],p_tile[:],ACT.Copy,scale=Pc[0])
                        if s==3 and g: cand(t+2)
                        A(pterm[:,s],qv,ACT.Copy,scale=Pc[s+1]).then_inc(pterm_ready,1)
                        if s==2 and g:
                            gates(t+2)
                            omzs(t+2)
                        if s==3 and prep: drives(t+1)
                act.wait_ge(init,1)
                for tau in range(2):
                    hhi(tau-1); gates(tau); omzs(tau); cand(tau)
                drives(0)
                with nc.Fori(0,(T-2)//2,engines=(mybir.EngineType.Activation,)) as t:
                    for uu in range(2): step(t*2+uu,True,True)
                step(T-2,False,True); step(T-1,False,False)
                with nc.Fori(0, B, engines=(mybir.EngineType.Activation,)) as b:
                    act.wait_ge(xg_ready, b + 1)
                    act.wait_ge(qkv3_ready, b)
                    for k in range(KC):
                        i = nc.scalar.activation(xn[:, k], xg[:, k], ACT.Identity, scale=gain_shift[:, k, bass.ds(b, 1)], bias=gain_shift[:, 2 + k, bass.ds(b, 1)])
                    i.then_inc(xn_ready, 1)
                    act.wait_ge(qkv3_ready, b + 1)
                    act.wait_ge(qk_sum_ready, b)
                    nc.scalar.activation(qk_sq[:].rearrange("p w h d -> p (w h d)"), bank[1][:], ACT.Square).then_inc(qk_sq_ready, 1)
                    act.wait_ge(pv3_ready, b * GROUPS)
                    nc.scalar.activation(v3_sb[:], bank[0][:, T:T + N], ACT.Copy).then_inc(v3_copied, 1)
                    act.wait_ge(qkt3_ready, 2 * b + 1)
                    nc.scalar.activation(q3_rows[:].rearrange("p g t -> p (g t)"), bank[2][:], ACT.Copy).then_inc(q3_copied, 1)
                    for g in range(GROUPS):
                        n = b * GROUPS + g
                        act.wait_ge(m3_ready, n + 1)
                        act.wait_ge(t3_ready, n - 1 if g >= 2 else b * GROUPS)
                        if g == 0:
                            act.wait_ge(o3_ready, b)
                        for j in range(4):
                            i = nc.scalar.activation(probs3[:, g % 2, j], bank[4 + g % 2][:, j * T:(j + 1) * T], ACT.Exp, bias=negmax3[:, g % 2, j:j + 1], accum_out=esum3[:, 4 * j + g:4 * j + g + 1])
                        i.then_inc(p3_ready, 1)
                    act.wait_ge(ot3_ready, b + 1)
                    nc.scalar.activation(o_t[:].rearrange("p k t -> p (k t)"), bank[3][:, 0:N], ACT.Copy).then_inc(ot3_copied, 1)

            @block.gpsimd
            def _(pool):
                nc.gpsimd.memset(SEQ[:, 0:SLOT], 0.0)
                nc.gpsimd.memset(ones16[:], 1.0)
                nc.gpsimd.memset(bhn3[:], 0.0)
                nc.gpsimd.memset(mean_ones[:], 1.0 / N)
                nc.gpsimd.memset(minus_half[:], -0.5)
                nc.gpsimd.memset(qk_pad[:], 0.0).then_inc(pool_setup, 1)
                pool.wait_ge(weights_loaded, 15 * 16)
                pool.wait_ge(pool_setup, 1)
                done = 1
                for source, parts in ((WHHf, WHH), (WCf, WC), (bhn, bhnp)):
                    for w in range(3):
                        part = parts[:, w]
                        nc.gpsimd.tensor_copy(part, source[:]).then_inc(pool_setup, 1)
                        done += 1
                        pool.wait_ge(pool_setup, done)
                        if w < 2:
                            nc.gpsimd.tensor_tensor(source[:], source[:], part, ALU.subtract).then_inc(pool_setup, 1)
                            done += 1
                            pool.wait_ge(pool_setup, done)
                nc.gpsimd.tensor_scalar(biasT[:], biasT[:], P_SHIFT, None, ALU.subtract)
                pool.wait_ge(first_loaded, 96)
                for k in range(KC):
                    diagonal = w_out_sb[:, k, k * 128:(k + 1) * 128]
                    i = nc.gpsimd.tensor_tensor(diagonal, diagonal, identity[:], ALU.add)
                i.then_inc(splits_ready, 1)
                nc.gpsimd.tensor_tensor(gate_bias[:, 0:4], b_ih_sb[:, 0:4], b_hh_sb[:, 0:4], ALU.add)
                nc.gpsimd.tensor_copy(gate_bias[:, 4:6], b_ih_sb[:, 4:6]).then_inc(gate_bias_ready, 1)
                pool.wait_ge(y0_added, B)
                pool.wait_ge(gi_ready, 24)

                G=nc.gpsimd.tensor_tensor
                def xs(t):
                    return SEQ[:,bass.ds((t+1)*32,32)]
                def hlo(tau):
                    pool.wait_ge(hh_ready,tau+2)
                    G(h_split[:,:,1,:],h_tile[:],h_split[:,:,0,:],ALU.subtract).then_inc(hs_ready,1)
                def ncomb(tau):
                    pool.wait_ge(omz_ready,tau+1); pool.wait_ge(n_ready,tau+1)
                    G(hz[:],ncand[:],omz[:],ALU.mult).then_inc(hz_done,1)
                def addh(tau):
                    G(xs(tau),xs(tau),h_tile[:],ALU.add).then_inc(x2_done,1)
                def mkdrive(t):
                    G(drive[:],xs(t),biasT[:],ALU.add).then_inc(drive_ready,1)
                def step(t,g,prep):
                    for s in range(4):
                        if s==3 and g: ncomb(t+2)
                        if s==0:
                            if g: hlo(t+1)
                            pool.wait_ge(kp_ready,t*2+1)
                            G(rinit[:,1],kp[:,1],dscaled[:,0],ALU.add).then_inc(rinit_a,1)
                            pool.wait_ge(kp_ready,t*2+2)
                            G(rinit[:,2],kp[:,2],dscaled[:,1],ALU.add)
                            G(rinit[:,3],kp[:,3],dscaled[:,2],ALU.add).then_inc(rinit_b,1)
                        pool.wait_ge(pterm_ready,t*4+s+1)
                        if s>0: pool.wait_ge(psum_done,t*4+s)
                        if s==2 and prep: pool.wait_ge(x2_done,t+2)
                        G(pacc[:,s],(kp[:,4] if s==0 else pacc[:,s-1]),pterm[:,s],ALU.add).then_inc(psum_done,1)
                        if s==1:
                            if prep: addh(t+1)
                        if s==2:
                            if prep: mkdrive(t+1)
                            G(xs(t-1),xs(t-1),q_clip[:],ALU.add).then_inc(x3_done,1)
                hlo(-1)
                ncomb(0); hlo(0); addh(0); ncomb(1)
                pool.wait_ge(x2_done,1)
                mkdrive(0)
                with nc.Fori(0,(T-2)//2,engines=(mybir.EngineType.Pool,)) as t:
                    for uu in range(2): step(t*2+uu,True,True)
                step(T-2,False,True); step(T-1,False,False)
                pool.wait_ge(qc_ready,T+1)
                G(xs(T-1),xs(T-1),q_clip[:],ALU.add).then_inc(x3_done,1)
                pool.wait_ge(x3_done, T + 1)
                with nc.Fori(0, B, engines=(mybir.EngineType.Pool,)) as b:
                    pool.wait_ge(ms3_ready, b)
                    pool.wait_ge(final_ready, b)
                    nc.gpsimd.tensor_copy(x3_b[:], seq[:, 1:, :, bass.ds(b, 1)].rearrange("p t k o -> p k (t o)")).then_inc(x3_taken, 1)
                    pool.wait_ge(x3_taken, b + 1)
                    nc.gpsimd.tensor_tensor(sq3[:], x3_b[:], x3_b[:], ALU.mult).then_inc(sq3_ready, 1)
                    pool.wait_ge(me3_ready, b + 1)
                    pool.wait_ge(xg_ready, b)
                    nc.gpsimd.tensor_tensor(rstd3[:], mean_eps[:], minus_half[:], ALU.pow).then_inc(rs3_ready, 1)
                    pool.wait_ge(rs3_ready, b + 1)
                    pool.wait_ge(xn_ready, b)
                    for k in range(KC):
                        i = nc.gpsimd.tensor_tensor(xg[:, k], x3_b[:, k], rstd3[:], ALU.mult)
                    i.then_inc(xg_ready, 1)
                    pool.wait_ge(qk_mean_ready, b + 1)
                    nc.gpsimd.tensor_tensor(qk_rstd[:].rearrange("p w h -> p (w h)"), qk_mean[:].rearrange("p w h -> p (w h)"), minus_half[:, 0:2 * HEADS], ALU.pow).then_inc(qk_rstd_ready, 1)
                    pool.wait_ge(qk_n_ready, b + 1)
                    pool.wait_ge(qkt3_ready, 2 * b)
                    nc.gpsimd.tensor_tensor(qk_pad[:, :, :, 0:D3].rearrange("p w h d -> p (w h) d"), qk_n[:].rearrange("p w h d -> p (w h) d"), g_qk_sb[:].rearrange("p w h d -> p (w h) d"), ALU.mult).then_inc(qk3_ready, 1)

            @block.vector
            def _(dve):
                dve.wait_ge(first_loaded, 96)
                nc.vector.tensor_scalar(k_const[:], b0_sb[:], row_consts[:, 1:2], row_consts[:, 2:3], ALU.mult, ALU.add).then_inc(dve_setup, 1)
                dve.wait_ge(mask_loaded, 64)
                for b in range(4):
                    i = nc.vector.tensor_scalar(mask_rows[:, 4 * b:4 * b + 4], mask_rows[:, 4 * b:4 * b + 4], row_consts[:, 3:4], row_consts[:, 4:5], ALU.mult, ALU.add)
                i.then_inc(dve_setup, 1)
                dve.wait_ge(dve_setup, 2)
                with nc.Fori(0, B, engines=(mybir.EngineType.DVE,)) as b:
                    for pair in range(2):
                        dve.wait_ge(kr0_ready, b * 2 + pair + 1)
                        dve.wait_ge(s0_ready, b * HEADS)
                        nc.vector.scalar_tensor_tensor(out=k_rows[:, 2 * pair:2 * pair + 2], in0=bank[5][:].rearrange("p (g n) -> p g n", g=2), scalar=k_const[:],
                                                       in1=mask_rows[:, bass.ds(b, 1), :].broadcast_to([128, 2, N]), op0=ALU.add, op1=ALU.mult).then_inc(k0_copied, 1)
                        if pair == 1:
                            dve.wait_ge(v0_ready, b + 1)
                            dve.wait_ge(pv0_ready, b * HEADS)
                            nc.vector.tensor_copy(v_sb[:].rearrange("p k t -> p (k t)"), bank[6][:, 0:KC * T]).then_inc(v0_copied, 1)
                    for h in range(HEADS + 1):
                        if h < HEADS:
                            dve.wait_ge(s0_ready, b * HEADS + h + 1)
                            nc.vector.tensor_reduce(negmax0[:, h % 2], bank[h % 2][:].rearrange("p (c k) -> p c k", c=KC), AXIS_X, ALU.max, negate=True).then_inc(m0_ready, 1)
                        if h >= 2 and h % 2 == 0:
                            n = b * HEADS + h - 1
                            dve.wait_ge(t0_ready, n + 1)
                            dve.wait_ge(pv0_ready, n - 1 if h >= 3 else b * HEADS)
                            nc.vector.tensor_copy(probs0_t[:, 1].rearrange("p c k -> p (c k)"), bank[3][:]).then_inc(pt0_d, 1)
                    dve.wait_ge(p0_ready, (b + 1) * HEADS)
                    dve.wait_ge(y0_added, b)
                    nc.vector.reciprocal(rsum0[:], esum0[:]).then_inc(l0_tail, 1)
                    dve.wait_ge(pv0_ready, (b + 1) * HEADS)
                    dve.wait_ge(l0_tail, b * 2 + 1)
                    for qc in range(KC):
                        i = nc.vector.tensor_tensor(y_sb[:, qc].rearrange("p (h d) -> p h d", d=D0), bank[7][:, qc * T:(qc + 1) * T].rearrange("p (h d) -> p h d", d=D0),
                                                    rsum0[:, qc].unsqueeze(2).broadcast_to([128, HEADS, D0]), ALU.mult)
                    i.then_inc(l0_tail, 1)
                    dve.wait_ge(l0_tail, b * 2 + 2)
                    dve.wait_ge(seq_loaded, 16)
                    x_b = seq[:, 1:, :, bass.ds(b, 1)].rearrange("p t k o -> p k (t o)")
                    nc.vector.tensor_tensor(x_b, x_b, y_sb[:], ALU.add).then_inc(y0_added, 1)

                dve.wait_ge(weights_loaded, 15 * 16)
                dve.wait_ge(emb_ready, 1)
                nc.vector.tensor_scalar(b_emb1[:], b_emb_sb[:], 1.0, None, ALU.add).then_inc(dve_setup, 1)
                dve.wait_ge(dve_setup, 3)
                for j in range(4):
                    if j < 2:
                        i = nc.vector.tensor_scalar(gain_shift[:, j], bank[6][:, j * B:(j + 1) * B], b_emb1[:, j:j + 1], g_norm_sb[:, j:j + 1], ALU.add, ALU.mult)
                    else:
                        i = nc.vector.tensor_scalar(gain_shift[:, j], bank[6][:, j * B:(j + 1) * B], b_emb_sb[:, j:j + 1], None, ALU.add)
                i.then_inc(dve_setup, 1)
                dve.wait_ge(gate_bias_ready, 1)
                with nc.Fori(0, 4, engines=(mybir.EngineType.DVE,)) as c:
                    for j in (1, 3, 5):
                        dve.wait_ge(gi_ready, c * 6 + j + 1)
                        nc.vector.tensor_scalar(gi4[:, bass.ds(c * 32, 32), j, :], bank[j][:].rearrange("p (t b) -> p t b", b=B), gate_bias[:, j:j + 1], None, ALU.add).then_inc(gi_d, 1)

                V=nc.vector
                stt=lambda o,i0,sc,i1,op0=ALU.mult,op1=ALU.add: V.scalar_tensor_tensor(out=o,in0=i0,scalar=sc,in1=i1,op0=op0,op1=op1)
                def gis(tau,j0,n): return GI[:,bass.ds(tau*96+j0*16,n*16)]
                def g_rz(tau):
                    dve.wait_ge(grz_ready,tau+1)
                    V.tensor_tensor(gsum[:,0].rearrange("p (j b)->p j b",b=16),Grz[:,:,0,:],gis(tau,0,4).rearrange("p (j b)->p j b",b=16),ALU.add).then_inc(ga_done,1)
                def g_rz2(tau):
                    dve.wait_ge(ga_done,tau+1)
                    V.tensor_tensor(gsum[:,1].rearrange("p (j b)->p j b",b=16),Grz[:,:,1,:],gsum[:,0].rearrange("p (j b)->p j b",b=16),ALU.add).then_inc(a2_ready,1)
                v3=lambda ap: ap.rearrange("p (j b)->p j b",b=16)
                def g_m(tau):
                    dve.wait_ge(gn_ready,tau+1); dve.wait_ge(trz_ready,tau+1)
                    stt(nmul[:],trz[:,0:32],1.0,Gn,ALU.add,ALU.mult).then_inc(nmul_done,1)
                def g_npre(tau):
                    dve.wait_ge(nmul_done,tau+1)
                    stt(npre[:],nmul[:],0.5,gis(tau,4,2)).then_inc(npre_ready,1)
                hv=h_tile[:].rearrange("p k b -> p (k b)")
                def g_zh(tau):
                    stt(hdiff[:],trz[:,32:64],1.0,hv,ALU.add,ALU.mult).then_inc(zh_done,1)
                def g_h(tau,first=False):
                    dve.wait_ge(zh_done,tau+1); dve.wait_ge(hz_done,tau+1)
                    if not first: dve.wait_ge(x2_done,tau)
                    stt(hv,hdiff[:],0.5,hz[:]).then_inc(h_ready,1)
                def r0init(t):
                    dve.wait_ge(p_ready,t+1); dve.wait_ge(dsc_ready,t+1)
                    stt(rinit[:,0],p_tile[:],Rc[0][0],dscaled[:,0]).then_inc(rinit0,1)
                def step(t,g,prep):
                    def tl(s):
                        dve.wait_ge(t_ready,t*4+s+1)
                        V.tensor_tensor(th_lo[:,s%2],th_ps[:,s%2],th_hi[:,s%2],ALU.subtract).then_inc(tl_ready,1)
                    def mkbase(s):
                        dve.wait_ge(rs_done,t*4+s+1); dve.wait_ge(cube_ready,t*4+s+1)
                        stt(base[:,s%2],qcube[:,s%2],-a[s]/3,rlin[:,s]).then_inc(base_done,1)
                    def cube(s):
                        dve.wait_ge(sq_done,t*4+s+1)
                        V.tensor_tensor(qcube[:,s%2],qsq[:,s%2],(q_clip[:] if s==0 else q_tile[:,s]),ALU.mult).then_inc(cube_ready,1)
                    def upd(s):
                        dve.wait_ge(base_done,t*4+s+1); dve.wait_ge(c_ready,t*4+s+1)
                        stt(QP(s+1),C(s),a[s],base[:,s%2]).then_inc(q_ready,1)
                        stt(q_tile[:,(s+1)%4],C(s),a[s],base[:,s%2]).then_inc(qs_ready,1)
                    def rt(j,i,src):
                        return stt(rlin[:,j],q_clip[:] if i==0 else q_tile[:,i],Rc[j][i+1],src[:,j])
                    dve.wait_ge(psum_done,t*4)
                    V.tensor_scalar(p_tile[:],pacc[:,3],20.-.875,-20.-.875,ALU.min,ALU.max).then_inc(p_ready,1)
                    dve.wait_ge(x3_done,t)
                    dve.wait_ge(qs_ready,t*4+1)
                    V.tensor_scalar(q_clip[:],q_tile[:,0],20.,-20.,ALU.min,ALU.max).then_inc(qc_ready,1)
                    r0init(t)
                    tl(0)
                    dve.wait_ge(qc_ready,t+1); dve.wait_ge(rinit0,t+1)
                    rt(0,0,rinit).then_inc(rs_done,1)
                    cube(0)
                    mkbase(0)
                    upd(0)
                    dve.wait_ge(rinit_a,t+1)
                    rt(1,0,rinit).then_inc(terms0,1)
                    tl(1)
                    dve.wait_ge(qs_ready,t*4+2); dve.wait_ge(terms0,t+1)
                    rt(1,1,rlin).then_inc(rs_done,1)
                    cube(1)
                    dve.wait_ge(rinit_b,t+1)
                    rt(2,0,rinit).then_inc(terms1,1)
                    mkbase(1)
                    rt(3,0,rinit).then_inc(terms2,1)
                    if g: g_rz(t+2)
                    upd(1)
                    if g: g_rz2(t+2)
                    dve.wait_ge(terms1,t+1)
                    rt(2,1,rlin).then_inc(terms3,1)
                    tl(2)
                    dve.wait_ge(qs_ready,t*4+3)
                    dve.wait_ge(terms3,t+1)
                    rt(2,2,rlin).then_inc(rs_done,1)
                    cube(2)
                    dve.wait_ge(terms2,t+1)
                    rt(3,1,rlin).then_inc(terms4,1)
                    mkbase(2)
                    if g: g_m(t+2)
                    upd(2)
                    if g: g_npre(t+2)
                    dve.wait_ge(terms4,t+1)
                    rt(3,2,rlin).then_inc(terms5,1)
                    if g: g_zh(t+2)
                    tl(3)
                    dve.wait_ge(qs_ready,t*4+4); dve.wait_ge(terms5,t+1)
                    rt(3,3,rlin).then_inc(rs_done,1)
                    cube(3)
                    mkbase(3)
                    if g: g_h(t+2)
                    upd(3)
                dve.wait_ge(gi_a, 12)
                dve.wait_ge(gi_d, 12)
                V.tensor_copy(QP(0),condT[:])
                V.tensor_scalar(pacc[:,3],condT[:],P_SHIFT,None,ALU.subtract)
                V.tensor_copy(q_tile[:,0],condT[:]).then_inc(qs_ready,1)
                V.tensor_copy(hv,condT[:]).then_inc(h_ready,1)
                dve.wait_ge(h_ready,1)
                V.tensor_copy(r1[:,0:1],condT[:,0:1]).then_inc(init,1)
                V.tensor_copy(r1[:,1:2],condT[:,0:1]).then_inc(q_ready,1)
                for tau in range(2):
                    g_rz(tau); g_rz2(tau); g_m(tau); g_npre(tau); g_zh(tau); g_h(tau,tau==0)
                with nc.Fori(0,(T-2)//14,engines=(mybir.EngineType.DVE,)) as t:
                    for uu in range(14): step(t*14+uu,True,True)
                step(T-2,False,True); step(T-1,False,False)
                dve.wait_ge(x3_done,T)
                dve.wait_ge(qs_ready,4*T+1)
                V.tensor_scalar(q_clip[:],q_tile[:,0],20.,-20.,ALU.min,ALU.max).then_inc(qc_ready,1)
                with nc.Fori(0, B, engines=(mybir.EngineType.DVE,)) as b:
                    dve.wait_ge(ms3_ready, b + 1)
                    dve.wait_ge(rs3_ready, b)
                    nc.vector.tensor_scalar(mean_eps[:], bank[0][:, 0:T], EPS, None, ALU.add).then_inc(me3_ready, 1)
                    dve.wait_ge(qk_sq_ready, b + 1)
                    nc.vector.tensor_reduce(qk_sum[:].rearrange("p w h -> p (w h)"), qk_sq[:].rearrange("p w h d -> p (w h) d"), AXIS_X, ALU.add).then_inc(qk_sum_ready, 1)
                    dve.wait_ge(qk_sum_ready, b + 1)
                    nc.vector.tensor_scalar(qk_mean[:], qk_sum[:], 1.0 / D3, EPS, ALU.mult, ALU.add).then_inc(qk_mean_ready, 1)
                    dve.wait_ge(qk_rstd_ready, b + 1)
                    dve.wait_ge(qk3_ready, b)
                    nc.vector.tensor_tensor(qk_n[:].rearrange("p w h d -> p (w h) d"), bank[1][:].rearrange("p (h d) -> p h d", d=D3),
                                            qk_rstd[:].rearrange("p w h -> p (w h)").unsqueeze(2).broadcast_to([128, 2 * HEADS, D3]), ALU.mult).then_inc(qk_n_ready, 1)
                    dve.wait_ge(qkt3_ready, 2 * b + 2)
                    nc.vector.tensor_scalar(k3_rows[:].rearrange("p g t -> p (g t)"), bank[3][:], float(D3 ** -0.5), None, ALU.mult).then_inc(k3_copied, 1)
                    for g in range(GROUPS + 1):
                        if g < GROUPS:
                            dve.wait_ge(s3_ready, b * GROUPS + g + 1)
                            nc.vector.tensor_reduce(negmax3[:, g % 2], bank[4 + g % 2][:].rearrange("p (c k) -> p c k", c=4), AXIS_X, ALU.max, negate=True).then_inc(m3_ready, 1)
                        if g >= 1:
                            n = b * GROUPS + g - 1
                            dve.wait_ge(t3_ready, n + 1)
                            dve.wait_ge(pv3_ready, n - 1 if g >= 3 else b * GROUPS)
                            nc.vector.tensor_copy(probs3_t[:, (g - 1) % 2].rearrange("p j t -> p (j t)"), bank[6 + (g - 1) % 2][:]).then_inc(pt3_copied, 1)
                    dve.wait_ge(p3_ready, (b + 1) * GROUPS)
                    nc.vector.reciprocal(rsum3[:], esum3[:]).then_inc(rsum3_ready, 1)
                    dve.wait_ge(rsum3_ready, b + 1)
                    dve.wait_ge(pv3_ready, (b + 1) * GROUPS)
                    nc.vector.tensor_tensor(o_sb[:].rearrange("p (h d) -> p h d", d=D3), bank[2][:, 0:N].rearrange("p (h d) -> p h d", d=D3),
                                            rsum3[:].unsqueeze(2).broadcast_to([128, HEADS, D3]), ALU.mult).then_inc(o3_ready, 1)
                    dve.wait_ge(final_ready, b + 1)
                    dve.wait_ge(out_stored, b * 16)
                    nc.vector.tensor_copy(out_sb[:], bank[1][:, 0:N]).then_inc(out_ready, 1)


def kernel(**inputs):
    import concourse.bacc as bacc
    from concourse.bass_utils import run_bass_kernel_spmd

    def by_feature(v):
        return v.reshape(KC, 128, -1).transpose(1, 0, 2)

    def padded(w):
        p = np.zeros((T, GROUPS, 4, 32), w.dtype)
        p[..., :D0] = w.T.reshape(T, GROUPS, 4, D0)
        return p.reshape(T, GROUPS, 128)

    v = {k: np.asarray(x) for k, x in inputs.items()}
    x, cond = v["x"], v["cond_2048"]
    rows = np.zeros((4, 32, 5), np.float32)
    rows[:, D0:D0 + 2, 0] = 1.0
    rows[:, D0, 1] = 1.0
    rows[:, D0 + 1, 2] = NEG
    rows[..., 3] = 1.0
    rows[:, D0 + 1, 3] = -1.0
    rows[:, D0 + 1, 4] = 1.0
    arrays = {
        "x_cbn": x.transpose(1, 0, 2),
        "x_seq": x.reshape(B, T, KC, 128).transpose(3, 1, 2, 0).reshape(128, T * SLOT),
        "cond_rows": cond[None],
        "cond_t": by_feature(cond.T).reshape(128, SLOT),
        "wq_pad": padded(v["L0_cond_Wq"]), "wk_pad": padded(v["L0_cond_Wk"]), "wv_t": v["L0_cond_Wv"].T,
        "b0": v["L0_cond_b"].reshape(1, 1),
        "w_ih": by_feature(v["L1_cond_W_ih"]), "w_hh": by_feature(v["L1_cond_W_hh"]),
        "b_ih": v["L1_cond_b_ih"].reshape(6, 128).T, "b_hh": v["L1_cond_b_hh"].reshape(6, 128).T,
        "b_hn": v["L1_cond_b_hh"][None, 2 * N:],
        "coupling_t": by_feature(v["L2_cond_coupling"].T),
        "bias_t": np.repeat(v["L2_cond_bias"].reshape(KC, 128).T, B, axis=1),
        "w_emb": by_feature(v["L3_cond_W_emb"]), "b_emb": v["L3_cond_b_emb"].reshape(4, 128).T,
        "g_norm": v["L3_cond_g_norm"].reshape(KC, 128).T,
        "w_qkv": by_feature(v["L3_cond_W_qkv"]),
        "g_q": v["L3_cond_g_q"].reshape(1, 1, D3), "g_k": v["L3_cond_g_k"].reshape(1, 1, D3),
        "w_out": by_feature(v["L3_cond_W_out"]),
        "identity_in": np.eye(128, dtype=np.float32), "row_consts_in": rows.reshape(128, 5),
    }
    nc = bacc.Bacc("TRN2", target_bir_lowering=False, num_devices=1)
    args, ins = {}, {}
    for name, a in arrays.items():
        ins[f"in_{name}_dram"] = np.ascontiguousarray(a)
        args[name] = nc.dram_tensor(f"in_{name}_dram", a.shape, mybir.dt.from_np(a.dtype), kind="ExternalInput").ap()
    out = nc.dram_tensor("out_0_dram", [B, T, N], FP32, kind="ExternalOutput").ap()
    cond_resid_kernel(nc, **args, out=out.rearrange("b t n -> t b n"))
    r = run_bass_kernel_spmd(nc, [ins], core_ids=[0])
    return r.results[0]["out_0_dram"]
```

```python
import numpy as np
import concourse.bass as bass
import concourse.mybir as mybir
from contextlib import ExitStack

FP32 = mybir.dt.float32
BF16 = mybir.dt.bfloat16
FP16 = mybir.dt.float16
ALU = mybir.AluOpType
ACT = mybir.ActivationFunctionType
AXIS_X = mybir.AxisListType.X

B = 16
T = 128
N = 256
KC = N // 128
SLOT = KC * B
HEADS = 16
D0 = T // HEADS
D3 = N // HEADS
GROUPS = 4
NEG = 60000.0
EPS = 1e-6
CLAMP = 20.0
L0_DRAIN = 5
P_SHIFT = 0.7 / 0.8


def rk4_coefficients():
    dt, eps, beta = 0.01, 0.08, 0.8
    a = [dt / 2, dt / 2, dt, dt / 6]

    def unit(i):
        return [1.0 if j == i else 0.0 for j in range(5)]

    p_stage = [unit(0)]
    for s in range(3):
        c = a[s] * eps
        p_stage.append([unit(0)[i] + c * (unit(s + 1)[i] - beta * p_stage[s][i]) for i in range(5)])
    p_next = unit(0)
    for s, w in enumerate((1, 2, 2, 1)):
        p_next = [p_next[i] + dt * eps / 6 * w * (unit(s + 1)[i] - beta * p_stage[s][i]) for i in range(5)]
    rows = []
    for s in range(4):
        if s < 3:
            own = unit(1)
        else:
            own = [(-unit(1)[i] + unit(2)[i] + 2 * unit(3)[i] + unit(4)[i]) / 3 for i in range(5)]
        rows.append([own[i] - a[s] * p_stage[s][i] + a[s] * unit(s + 1)[i] for i in range(5)])
    return a, rows, p_next


def cond_resid_kernel(nc, x_cbn, x_seq, cond_rows, cond_t, wq_pad, wk_pad, wv_t, b0, w_ih, w_hh, b_ih, b_hh, b_hn,
                      coupling_t, bias_t, w_emb, b_emb, g_norm, w_qkv, g_q, g_k, w_out, identity_in, row_consts_in, select_in, out):
    ctx = ExitStack()
    with ctx:
        def sb(name, shape, dtype=FP32):
            return ctx.enter_context(nc.sbuf_tensor(name, shape, dtype))

        def sem(name):
            return ctx.enter_context(nc.semaphore(name))

        bank = [ctx.enter_context(nc.psum_tensor(f"bank{i}", [128, 512], FP32)) for i in range(8)]

        SEQ = sb("SEQ", [128, (T + 1) * SLOT])
        GI = sb("GI", [128, T * 96])
        seq = SEQ[:].rearrange("p (s k b) -> p s k b", k=KC, b=B)
        gi4 = GI[:].rearrange("p (t j b) -> p t j b", j=6, b=B)
        x_b0 = sb("x_b0", [128, N])
        identity = sb("identity", [128, 128])
        row_consts = sb("row_consts", [128, 8])
        wq_sb = sb("wq_sb", [128, GROUPS, 128]); wk_sb = sb("wk_sb", [128, GROUPS, 128]); wv_sb = sb("wv_sb", [128, T])
        select_sb = sb("select_sb", [T // 8, T // 8, 128])
        b0_sb = sb("b0_sb", [128, 1]); k_const = sb("k_const", [128, 1])
        mask_rows = sb("mask_rows", [128, B, N])
        w_ih_sb = sb("w_ih_sb", [128, KC, 3 * N]); b_ih_sb = sb("b_ih_sb", [128, 6]); b_hh_sb = sb("b_hh_sb", [128, 6]); gate_bias = sb("gate_bias", [128, 6])
        WHHf = sb("WHHf", [128, KC, 3 * N]); WCf = sb("WCf", [128, KC, N])
        WHH = sb("WHH", [128, 3, KC, 3 * N], BF16); WC = sb("WC", [128, 3, KC, N], BF16)
        condT = sb("condT", [128, SLOT]); biasT = sb("biasT", [128, SLOT])
        bhn = sb("bhn", [1, N]); bhnp = sb("bhnp", [1, 3, N], BF16); bhn3 = sb("bhn3", [128, N], BF16); ones16 = sb("ones16", [128, B], BF16)
        w_emb_sb = sb("w_emb_sb", [128, KC, 2 * N]); b_emb_sb = sb("b_emb_sb", [128, 4]); b_emb1 = sb("b_emb1", [128, 4]); g_norm_sb = sb("g_norm_sb", [128, KC])
        gain_shift = sb("gain_shift", [128, 4, B])
        w_qkv_sb = sb("w_qkv_sb", [128, KC, 3 * N]); g_qk_sb = sb("g_qk_sb", [128, 2, HEADS, D3])
        w_out_sb = sb("w_out_sb", [128, KC, N]); mean_ones = sb("mean_ones", [128, 128]); minus_half = sb("minus_half", [128, 128])

        q_full = sb("q_full", [128, 2 * N]); q_hi_part = sb("q_hi_part", [128, 2 * N], FP16)
        k_full = sb("k_full", [128, 2 * N]); k_hi_part = sb("k_hi_part", [128, 2 * N], FP16)
        q_stack = sb("q_stack", [128, 2, GROUPS, N], FP16); k_stack = sb("k_stack", [128, 2, GROUPS, N], FP16)
        v_parts = sb("v_parts", [128, 2, KC, HEADS, 2, D0], FP16)
        negmax0 = sb("negmax0", [128, 4, KC]); esum0 = sb("esum0", [128, 2, KC, HEADS]); rsum0 = sb("rsum0", [128, KC, HEADS])
        probs0 = sb("probs0", [128, 4, KC, N]); probs0_t = sb("probs0_t", [128, 4, 2, KC, N], FP16)
        y_sum = sb("y_sum", [128, KC, T]); y_sb = sb("y_sb", [128, KC, T])

        q_tile = sb("q_tile", [128, 4, 32]); q_clip = sb("q_clip", [128, 32])
        th_hi = sb("th_hi", [128, 2, 32], FP16); th_lo = sb("th_lo", [128, 2, 32], FP16)
        qsq = sb("qsq", [128, 2, 32]); qcube = sb("qcube", [128, 2, 32]); base = sb("base", [128, 2, 32])
        rlin = sb("rlin", [128, 4, 32]); rinit = sb("rinit", [128, 4, 32]); kp = sb("kp", [128, 5, 32])
        pacc = sb("pacc", [128, 4, 32]); pterm = sb("pterm", [128, 4, 32]); p_tile = sb("p_tile", [128, 32])
        drive = sb("drive", [128, 32]); dscaled = sb("dscaled", [128, 3, 32])
        h_tile = sb("h_tile", [128, 2, 16]); h_split = sb("h_split", [128, 2, 2, 16], FP16)
        gsum = sb("gsum", [128, 2, 64]); trz = sb("trz", [128, 64]); nmul = sb("nmul", [128, 32]); npre = sb("npre", [128, 32])
        ncand = sb("ncand", [128, 32]); hdiff = sb("hdiff", [128, 32]); hz = sb("hz", [128, 32]); omz = sb("omz", [128, 32])

        r1=sb("r1",[128,2])
        mean_eps = sb("mean_eps", [128, T // 8]); rstd3 = sb("rstd3", [128, T // 8]); rstd_rows = sb("rstd_rows", [T // 8, 128])
        sq3 = GI[:, 0:T * SLOT].rearrange("p (k t b) -> p k t b", k=KC, b=B)
        xg = GI[:, T * SLOT:2 * T * SLOT].rearrange("p (t k b) -> p t k b", k=KC, b=B)
        x3_b = sb("x3_b", [128, KC, T]); xn = sb("xn", [128, KC, T])
        qk_sq = sb("qk_sq", [128, 2, HEADS, D3]); qk_sum = sb("qk_sum", [128, 2, HEADS]); qk_mean = sb("qk_mean", [128, 2, HEADS]); qk_rstd = sb("qk_rstd", [128, 2, HEADS])
        qk_n = sb("qk_n", [128, 2, HEADS, D3]); qk_pad = sb("qk_pad", [128, 2, HEADS, 32])
        v3_sb = sb("v3_sb", [128, N])
        q3_rows = sb("q3_rows", [128, GROUPS, T]); k3_rows = sb("k3_rows", [128, GROUPS, T])
        negmax3 = sb("negmax3", [128, 2, 4]); esum3 = sb("esum3", [128, HEADS]); rsum3 = sb("rsum3", [128, HEADS])
        probs3 = sb("probs3", [128, 2, 4, T]); probs3_t = sb("probs3_t", [128, 2, 4, T])
        o_sb = sb("o_sb", [128, N]); o_t = sb("o_t", [128, KC, T]); out_sb = sb("out_sb", [128, N])

        a2_ready = sem("a2_ready")
        base_done = sem("base_done")
        bias3 = sem("bias3")
        c_ready = sem("c_ready")
        cube_ready = sem("cube_ready")
        drive_ready = sem("drive_ready")
        dsc_ready = sem("dsc_ready")
        dve_setup = sem("dve_setup")
        emb_ready = sem("emb_ready")
        final_ready = sem("final_ready")
        first_loaded = sem("first_loaded")
        ga_done = sem("ga_done")
        gate_bias_ready = sem("gate_bias_ready")
        gi_a = sem("gi_a")
        gi_d = sem("gi_d")
        gi_ready = sem("gi_ready")
        gn_ready = sem("gn_ready")
        grz_ready = sem("grz_ready")
        h_ready = sem("h_ready")
        hh_ready = sem("hh_ready")
        hs_ready = sem("hs_ready")
        hz_done = sem("hz_done")
        init = sem("init")
        k3_copied = sem("k3_copied")
        k_copied = sem("k_copied")
        k_hi_ready = sem("k_hi_ready")
        k_stacked = sem("k_stacked")
        kp_ready = sem("kp_ready")
        kr0_ready = sem("kr0_ready")
        l0_tail = sem("l0_tail")
        m0_ready = sem("m0_ready")
        m3_ready = sem("m3_ready")
        mask_loaded = sem("mask_loaded")
        me3_ready = sem("me3_ready")
        ms3_ready = sem("ms3_ready")
        n_ready = sem("n_ready")
        nmul_done = sem("nmul_done")
        npre_ready = sem("npre_ready")
        o3_ready = sem("o3_ready")
        omz_ready = sem("omz_ready")
        ot3_copied = sem("ot3_copied")
        ot3_ready = sem("ot3_ready")
        out_ready = sem("out_ready")
        out_stored = sem("out_stored")
        p0_ready = sem("p0_ready")
        p3_ready = sem("p3_ready")
        p_hi_ready = sem("p_hi_ready")
        p_lo_ready = sem("p_lo_ready")
        p_ready = sem("p_ready")
        pool_done = sem("pool_done")
        pool_setup = sem("pool_setup")
        psum_done = sem("psum_done")
        pt3_copied = sem("pt3_copied")
        pterm_ready = sem("pterm_ready")
        pv0_ready = sem("pv0_ready")
        pv3_ready = sem("pv3_ready")
        q3_copied = sem("q3_copied")
        q_copied = sem("q_copied")
        q_ready = sem("q_ready")
        q_stacked = sem("q_stacked")
        qc_ready = sem("qc_ready")
        qk3_ready = sem("qk3_ready")
        qk_mean_ready = sem("qk_mean_ready")
        qk_n_ready = sem("qk_n_ready")
        qk_rstd_ready = sem("qk_rstd_ready")
        qk_sq_ready = sem("qk_sq_ready")
        qk_sum_ready = sem("qk_sum_ready")
        qkt3_ready = sem("qkt3_ready")
        qkv3_ready = sem("qkv3_ready")
        qr0_ready = sem("qr0_ready")
        qs_ready = sem("qs_ready")
        ready = sem("ready")
        rinit0 = sem("rinit0")
        rinit_a = sem("rinit_a")
        rinit_b = sem("rinit_b")
        rs3_ready = sem("rs3_ready")
        rs_done = sem("rs_done")
        rs_rows_ready = sem("rs_rows_ready")
        rsb3_ready = sem("rsb3_ready")
        rst3_ready = sem("rst3_ready")
        rsum3_ready = sem("rsum3_ready")
        s0_ready = sem("s0_ready")
        s3_ready = sem("s3_ready")
        semaphore = sem("semaphore")
        seq_loaded = sem("seq_loaded")
        splits_ready = sem("splits_ready")
        sq3_ready = sem("sq3_ready")
        sq_done = sem("sq_done")
        stacked = sem("stacked")
        t0_ready = sem("t0_ready")
        t3_ready = sem("t3_ready")
        t_ready = sem("t_ready")
        terms0 = sem("terms0")
        terms1 = sem("terms1")
        terms2 = sem("terms2")
        terms3 = sem("terms3")
        terms4 = sem("terms4")
        terms5 = sem("terms5")
        th_ready = sem("th_ready")
        tl_ready = sem("tl_ready")
        trz_ready = sem("trz_ready")
        v0_ready = sem("v0_ready")
        v3_copied = sem("v3_copied")
        v_hi_ready = sem("v_hi_ready")
        v_lo_ready = sem("v_lo_ready")
        weights_loaded = sem("weights_loaded")
        x2_done = sem("x2_done")
        x3_done = sem("x3_done")
        x3_taken = sem("x3_taken")
        x_loaded = sem("x_loaded")
        xg_ready = sem("xg_ready")
        xn_ready = sem("xn_ready")
        y0_added = sem("y0_added")
        zh_done = sem("zh_done")
        a, Rc, Pc = rk4_coefficients()

        def at_least(engine, semaphore, value):
            if not isinstance(value, int) or value > 0:
                engine.wait_ge(semaphore, value)

        def head_before(b, h, back):
            return (b, h - back) if h >= back else (b - 1, h - back + HEADS)

        def l3_batches(engine_type, body):
            body(0)
            with nc.Fori(0, B - 2, engines=(engine_type,)) as u:
                body(u + 1)
            body(B - 1)

        def has_next(b):
            return not (isinstance(b, int) and b == B - 1)

        def l0_slots(engine_type, slot):
            for h in range(HEADS):
                slot(0, 0, h)
            with nc.Fori(0, B // 2 - 1, engines=(engine_type,)) as u:
                for half in range(2):
                    for h in range(HEADS):
                        slot(u * 2 + half + 1, 1 - half, h)
            for h in range(HEADS + L0_DRAIN):
                slot(B - 1, 1, h)

        def C(s):
            return bank[s % 2][:, 0:32]
        Grz = bank[2][:, 0:128].rearrange("p (j w b) -> p j w b", j=4, w=2)
        Gn = bank[3][:, 0:32]

        def QP(s):
            return bank[4 + s % 2][:, 0:32]
        th_ps = bank[6][:, 0:64].rearrange("p (s n) -> p s n", s=2)

        with nc.Block() as block:
            @block.sync
            def _(sp):
                sp.dma_start(row_consts[:], row_consts_in).then_inc(first_loaded, 16)
                sp.dma_start(b0_sb[:], b0.broadcast_to([128, 1])).then_inc(first_loaded, 16)
                sp.dma_start(wq_sb[:], wq_pad).then_inc(first_loaded, 16)
                sp.dma_start(wk_sb[:], wk_pad).then_inc(first_loaded, 16)
                sp.dma_start(wv_sb[:], wv_t).then_inc(first_loaded, 16)
                sp.dma_start(identity[:], identity_in).then_inc(first_loaded, 16)
                sp.dma_start(select_sb[:], select_in).then_inc(first_loaded, 16)
                sp.dma_start(x_b0[:], x_cbn[:, 0]).then_inc(x_loaded, 16)
                for i in range(4):
                    sp.dma_start(mask_rows[:, 4 * i:4 * i + 4], cond_rows[:, 4 * i:4 * i + 4].broadcast_to([128, 4, N])).then_inc(mask_loaded, 16)
                sp.dma_start(SEQ[:, SLOT:], x_seq).then_inc(seq_loaded, 16)
                for tile, source in ((condT, cond_t), (biasT, bias_t), (bhn, b_hn), (b_ih_sb, b_ih), (b_hh_sb, b_hh),
                                     (b_emb_sb, b_emb), (g_norm_sb, g_norm)):
                    sp.dma_start(tile[:], source).then_inc(weights_loaded, 16)
                for tile, source in ((WHHf, w_hh), (WCf, coupling_t), (w_ih_sb, w_ih), (w_emb_sb, w_emb), (w_qkv_sb, w_qkv), (w_out_sb, w_out)):
                    sp.dma_start(tile[:], source).then_inc(weights_loaded, 16)
                for i, gain in enumerate((g_q, g_k)):
                    sp.dma_start(g_qk_sb[:, i], gain.broadcast_to([128, HEADS, D3])).then_inc(weights_loaded, 16)
                with nc.Fori(0, B - 1, engines=(mybir.EngineType.SP,)) as b:
                    sp.wait_ge(v0_ready, b + 1)
                    sp.dma_start(x_b0[:].unsqueeze(1), x_cbn[:, bass.ds(b + 1, 1)]).then_inc(x_loaded, 16)
                sp.wait_ge(pool_setup, 16)
                sp.dma_start(bhn3[0:3, :], bhnp[:].rearrange("p w n -> p (w n)")).then_inc(bias3, 16)
                with nc.Fori(0, B, engines=(mybir.EngineType.SP,)) as b:
                    sp.wait_ge(out_ready, b + 1)
                    sp.dma_start(out[:, bass.ds(b, 1), :], out_sb[:].unsqueeze(1)).then_inc(out_stored, 16)
                sp.wait_ge(out_stored, 16 * B)

            @block.tensor
            def _(pe):
                mm = nc.tensor.matmul
                pe.wait_ge(first_loaded, 112)

                def l0_project(b, pair):
                    at_least(pe, q_copied, b * 2 + pair)
                    at_least(pe, k_copied, b * 2 + pair)
                    if pair == 0:
                        pe.wait_ge(x_loaded, (b + 1) * 16)
                        at_least(pe, v_lo_ready, b)
                    for w_sb, to, ready in ((wq_sb, 4, qr0_ready), (wk_sb, 5, kr0_ready)):
                        for i in range(2):
                            product = mm(bank[to][:, i * N:(i + 1) * N], w_sb[:, 2 * pair + i], x_b0[:], start=(i == 0), stop=True, skip_group_check=True)
                        product.then_inc(ready, 1)

                def l0_project_v(b):
                    pe.wait_ge(q_copied, b * 2 + 2)
                    for kc in range(KC):
                        i = mm(bank[4][:, kc * T:kc * T + T], x_b0[:, kc * 128:kc * 128 + 128], wv_sb[:], start=(kc == 0), stop=True, skip_group_check=True)
                    i.then_inc(v0_ready, 1)

                def l0_pe_slot(b, parity, h):
                    n = b * HEADS + h
                    if h < HEADS:
                        if h % 8 == 0:
                            pe.wait_ge(q_stacked, b * 2 + h // 8 + 1)
                            pe.wait_ge(k_stacked, b * 2 + h // 8 + 1)
                        at_least(pe, p0_ready, n - 1)
                        rows = slice(32 * (h % 4), 32 * (h % 4) + 32)
                        for qc in range(KC):
                            i = mm(bank[h % 2][:, qc * N:(qc + 1) * N], q_stack[rows, parity, h // 4, qc * 128:(qc + 1) * 128], k_stack[rows, parity, h // 4], start=(qc == 0), stop=True, skip_group_check=True)
                        i.then_inc(s0_ready, 1)
                    if not isinstance(n, int) or 2 <= n < B * HEADS + 2:
                        pe.wait_ge(p0_ready, n - 1)
                        at_least(pe, p_lo_ready, n - 3)
                        for kc in range(KC):
                            for qc in range(KC):
                                i = nc.tensor.transpose(bank[2 + h % 2][:, kc * N + qc * 128:kc * N + qc * 128 + 128], probs0[:, (h - 2) % 4, qc, kc * 128:kc * 128 + 128], identity[:])
                        i.then_inc(t0_ready, 1)
                    if not isinstance(n, int) or 4 <= n < B * HEADS + 4:
                        hv = (h - 4) % HEADS
                        vp = parity if h >= 4 else 1 - parity
                        bv = b if h >= 4 else b - 1
                        pe.wait_ge(p_lo_ready, n - 3)
                        if hv == 0:
                            pe.wait_ge(v_lo_ready, bv + 1)
                            at_least(pe, y0_added, bv - 1)
                        for qc in range(KC):
                            for kc in range(KC):
                                for part in range(2):
                                    first, last = kc == 0 and part == 0, kc == KC - 1 and part == 1
                                    i = mm(bank[6 + vp][:, (qc * HEADS + hv) * 16:(qc * HEADS + hv) * 16 + 16], probs0_t[:, (h - 4) % 4, part, kc, qc * 128:qc * 128 + 128],
                                           v_parts[:, vp, kc, hv].rearrange("p w d -> p (w d)"), start=(hv == 0 and qc == 0 and first), stop=last, skip_group_check=True)
                        i.then_inc(pv0_ready, 1)
                    if not (isinstance(b, int) and b == B - 1):
                        if h in (2, 7):
                            l0_project(b + 1, h // 7)
                        if h == 10:
                            l0_project_v(b + 1)

                l0_project(0, 0)
                l0_project(0, 1)
                l0_project_v(0)
                l0_slots(mybir.EngineType.PE, l0_pe_slot)

                pe.wait_ge(weights_loaded, 15 * 16)
                pe.wait_ge(y0_added, B)
                for j in range(4):
                    for k in range(KC):
                        i = mm(bank[6][:, j * B:(j + 1) * B], w_emb_sb[:, k, j * 128:(j + 1) * 128], condT[:, k * B:(k + 1) * B], start=(j == 0 and k == 0), stop=(k == KC - 1), skip_group_check=True)
                i.then_inc(emb_ready, 1)
                pe.wait_ge(y0_added, B)
                with nc.Fori(0, 4, engines=(mybir.EngineType.PE,)) as c:
                    for j in range(6):
                        pe.wait_ge(gi_a if j % 2 == 0 else gi_d, c * 3)
                        for k in range(KC):
                            i = mm(bank[j][:].rearrange("p (t b) -> p t b", b=B), w_ih_sb[:, k, j * 128:(j + 1) * 128], seq[:, bass.ds(c * 32 + 1, 32), k, :], start=(k == 0), stop=(k == KC - 1), skip_group_check=True)
                        i.then_inc(gi_ready, 1)

                pe.wait_ge(splits_ready, 1)
                pe.wait_ge(gi_a, 12)
                pe.wait_ge(gi_d, 12)
                def coupling(t,s,parts,src,first,last):
                    i=0; n=len(parts)*4
                    for w in parts:
                        for m in range(2):
                            for k in range(2):
                                mm=nc.tensor.matmul(bank[s%2][:,m*16:m*16+16],WC[:,w,k,m*128:m*128+128],src[:,s%2,k*16:k*16+16],
                                    start=(first and i==0),stop=(last and i==n-1),skip_group_check=True)
                                i+=1
                    return mm
                def gru_products(dst,chunks,j0):
                    i=0
                    for j in chunks:
                        for w in range(3):
                            for k in range(2):
                                mm=nc.tensor.matmul(dst[:,j-j0],WHH[:,w,k,j*128:j*128+128],h_split[:,k],start=(i==0),stop=(i==len(chunks)*6-1),skip_group_check=True)
                                i+=1
                    return mm
                def gru(tau):
                    pe.wait_ge(hs_ready,tau+1)
                    gru_products(Grz,range(4),0).then_inc(grz_ready,1)
                def gru_n(tau):
                    for j in range(2):
                        dst=Gn[:,j*16:j*16+16]
                        nc.tensor.matmul(dst,bhn3[:,j*128:j*128+128],ones16[:],start=(j==0),stop=False,skip_group_check=True)
                        for w,half in ((0,0),(1,0),(2,0),(0,1),(1,1)):
                            for k in range(2):
                                mm=nc.tensor.matmul(dst,WHH[:,w,k,(4+j)*128:(5+j)*128],h_split[:,k,half],start=False,stop=(j==1 and k==1 and w==1 and half==1),skip_group_check=True)
                    mm.then_inc(gn_ready,1)
                def step(t,g):
                    for s in range(4):
                        pe.wait_ge(th_ready,t*4+s+1)
                        coupling(t,s,(0,1,2),th_hi,True,False)
                        pe.wait_ge(tl_ready,t*4+s+1)
                        coupling(t,s,(0,1),th_lo,False,True).then_inc(c_ready,1)
                        if g and s==0: gru(t+2)
                        if g and s==1: gru_n(t+2)
                pe.wait_ge(bias3,16)
                for tau in range(2):
                    gru(tau); gru_n(tau)
                for t in range(2): step(t,True)
                with nc.Fori(1,(T-2)//2,engines=(mybir.EngineType.PE,)) as t:
                    for uu in range(2): step(t*2+uu,True)
                step(T-2,False); step(T-1,False)
                pe.wait_ge(qc_ready, T + 1)

                for g in range(T // 8):
                    if g % 4 == 0:
                        pe.wait_ge(sq3_ready, g // 4 + 1)
                    for k in range(KC):
                        i = mm(bank[0][:, g:g + 1], sq3[:, k, 8 * g:8 * g + 8].rearrange("p t b -> p (t b)"), mean_ones[:, 0:1], start=(g == 0 and k == 0), stop=(k == KC - 1), skip_group_check=True)
                i.then_inc(ms3_ready, 1)
                pe.wait_ge(rs3_ready, 1)
                nc.tensor.transpose(bank[1][0:T // 8, 0:128], rstd3[:], identity[:]).then_inc(rst3_ready, 1)
                pe.wait_ge(rs_rows_ready, 1)
                for g in range(T // 8):
                    i = mm(bank[2 + g // 4][:, (g % 4) * 128:(g % 4) * 128 + 128], select_sb[:, g], rstd_rows[:], start=(g % 4 == 0), stop=True, skip_group_check=True)
                    if g % 4 == 3:
                        i.then_inc(rsb3_ready, 1)
                pe.wait_ge(xg_ready, 1)

                def l3_project(b):
                    pe.wait_ge(xn_ready, b + 1)
                    at_least(pe, v3_copied, b)
                    for k in range(KC):
                        mm(bank[1][:], xn[:, k], w_qkv_sb[:, k, 0:2 * N], start=(k == 0), stop=(k == KC - 1), skip_group_check=True)
                    for k in range(KC):
                        i = mm(bank[0][:, 0:N], xn[:, k], w_qkv_sb[:, k, 2 * N:], start=(k == 0), stop=(k == KC - 1), skip_group_check=True)
                    i.then_inc(qkv3_ready, 1)

                def l3_head_rows(b):
                    pe.wait_ge(qk3_ready, b + 1)
                    at_least(pe, q3_copied, b)
                    at_least(pe, k3_copied, b)
                    for w in range(2):
                        for g in range(GROUPS):
                            i = nc.tensor.transpose(bank[2 + w][:, g * T:(g + 1) * T], qk_pad[:, w, 4 * g:4 * g + 4].rearrange("p h d -> p (h d)"), identity[:])
                        i.then_inc(qkt3_ready, 1)

                def l3_scores(b, g):
                    at_least(pe, p3_ready, b * GROUPS + g - 1)
                    rows = slice(32 * g, 32 * g + 32)
                    for j in range(4):
                        i = mm(bank[4 + g % 2][:, j * T:(j + 1) * T], q3_rows[rows, j], k3_rows[rows, j], start=(j == 0), stop=True, skip_group_check=True)
                    i.then_inc(s3_ready, 1)

                def l3_transposes(b, g):
                    pe.wait_ge(p3_ready, b * GROUPS + g + 1)
                    at_least(pe, pt3_copied, b * GROUPS + g)
                    if g == 0:
                        at_least(pe, ot3_copied, b)
                    for j in range(4):
                        i = nc.tensor.transpose(bank[6][:, j * T:(j + 1) * T], probs3[:, g % 2, j], identity[:])
                    i.then_inc(t3_ready, 1)

                def l3_values(b, g):
                    pe.wait_ge(pt3_copied, b * GROUPS + g + 1)
                    if g == 0:
                        pe.wait_ge(v3_copied, b + 1)
                        at_least(pe, out_ready, b)
                    for j in range(4):
                        h = 4 * j + g
                        i = mm(bank[7][:, h * D3:(h + 1) * D3], probs3_t[:, g % 2, j], v3_sb[:, h * D3:(h + 1) * D3], start=(h == 0), stop=True, skip_group_check=True)
                    i.then_inc(pv3_ready, 1)

                def l3_pe_body(b):
                    pe.wait_ge(q3_copied, b + 1)
                    pe.wait_ge(k3_copied, b + 1)
                    l3_scores(b, 0)
                    l3_scores(b, 1)
                    if has_next(b):
                        l3_project(b + 1)
                    l3_transposes(b, 0)
                    l3_scores(b, 2)
                    l3_transposes(b, 1)
                    l3_values(b, 0)
                    l3_scores(b, 3)
                    l3_transposes(b, 2)
                    l3_values(b, 1)
                    l3_transposes(b, 3)
                    l3_values(b, 2)
                    l3_values(b, 3)
                    if has_next(b):
                        l3_head_rows(b + 1)
                    pe.wait_ge(o3_ready, b + 1)
                    for k in range(KC):
                        i = nc.tensor.transpose(bank[6][:, k * 128:(k + 1) * 128], o_sb[:, k * 128:(k + 1) * 128], identity[:])
                    i.then_inc(ot3_ready, 1)
                    pe.wait_ge(x3_taken, b + 1)
                    for k in range(KC):
                        mm(bank[7][:, N + k * 128:N + (k + 1) * 128], x3_b[:, k], identity[:], start=(k == 0), stop=False, skip_group_check=True)
                    pe.wait_ge(ot3_copied, b + 1)
                    for k in range(KC):
                        i = mm(bank[7][:, N:], o_t[:, k], w_out_sb[:, k], start=False, stop=(k == KC - 1), skip_group_check=True)
                    i.then_inc(final_ready, 1)

                l3_project(0)
                l3_head_rows(0)
                l3_batches(mybir.EngineType.PE, l3_pe_body)

            @block.scalar
            def _(act):
                def l0_prepare_q(b, pair):
                    pe_count = b * 2 + pair
                    act.wait_ge(qr0_ready, pe_count + 1)
                    at_least(act, q_stacked, pe_count)
                    nc.scalar.activation(q_full[:], bank[4][:], ACT.Identity, scale=1.0 / float(np.sqrt(D0)), bias=row_consts[:, 0:1])
                    nc.scalar.activation(q_hi_part[:], bank[4][:], ACT.Identity, scale=row_consts[:, 1:2], bias=row_consts[:, 2:3]).then_inc(q_copied, 1)

                def l0_prepare_k(b, pair):
                    act.wait_ge(k_copied, b * 2 + pair + 1)
                    at_least(act, k_stacked, b * 2 + pair)
                    nc.scalar.activation(k_hi_part[:], k_full[:], ACT.Copy, scale=row_consts[:, 3:4]).then_inc(k_hi_ready, 1)

                def l0_prepare_v(b, parity):
                    act.wait_ge(v0_ready, b + 1)
                    at_least(act, pv0_ready, (b - 1) * HEADS)
                    for kc in range(KC):
                        i = nc.scalar.activation(v_parts[:, parity, kc, :, 0], bank[4][:, kc * T:(kc + 1) * T].rearrange("p (h d) -> p h d", d=D0), ACT.Copy)
                    i.then_inc(v_hi_ready, 1)

                def l0_act_slot(b, parity, h):
                    n = b * HEADS + h
                    if h < HEADS:
                        act.wait_ge(m0_ready, n + 1)
                        at_least(act, t0_ready, n - 3)
                        if h == 0:
                            at_least(act, y0_added, b - 1)
                        for qc in range(KC):
                            i = nc.scalar.activation(probs0[:, h % 4, qc], bank[h % 2][:, qc * N:(qc + 1) * N], ACT.Exp, bias=negmax0[:, h % 4, qc:qc + 1], accum_out=esum0[:, parity, qc, h:h + 1])
                        i.then_inc(p0_ready, 1)
                    if not isinstance(n, int) or 2 <= n < B * HEADS + 2:
                        act.wait_ge(t0_ready, n - 1)
                        at_least(act, pv0_ready, n - 5)
                        nc.scalar.activation(probs0_t[:, (h - 2) % 4, 0].rearrange("p c k -> p (c k)"), bank[2 + h % 2][:], ACT.Copy).then_inc(p_hi_ready, 1)
                    if not (isinstance(b, int) and b == B - 1):
                        if h in (3, 8):
                            l0_prepare_q(b + 1, h // 8)
                            l0_prepare_k(b + 1, h // 8)
                        if h == 11:
                            l0_prepare_v(b + 1, 1 - parity)

                act.wait_ge(first_loaded, 112)
                for pair in range(2):
                    l0_prepare_q(0, pair)
                    l0_prepare_k(0, pair)
                l0_prepare_v(0, 0)
                l0_slots(mybir.EngineType.Activation, l0_act_slot)

                act.wait_ge(gate_bias_ready, 1)
                with nc.Fori(0, 4, engines=(mybir.EngineType.Activation,)) as c:
                    for j in (0, 2, 4):
                        act.wait_ge(gi_ready, c * 6 + j + 1)
                        nc.scalar.activation(gi4[:, bass.ds(c * 32, 32), j, :], bank[j][:].rearrange("p (t b) -> p t b", b=B), ACT.Identity, bias=gate_bias[:, j:j + 1]).then_inc(gi_a, 1)

                A=nc.scalar.activation
                def gates(tau):
                    act.wait_ge(a2_ready,tau+1)
                    A(trz[:],gsum[:,1],ACT.Tanh,scale=0.5).then_inc(trz_ready,1)
                def omzs(tau):
                    act.wait_ge(trz_ready,tau+1)
                    A(omz[:],trz[:,32:64],ACT.Copy,scale=-0.5,bias=0.5).then_inc(omz_ready,1)
                def cand(tau):
                    act.wait_ge(npre_ready,tau+1)
                    A(ncand[:],npre[:],ACT.Tanh).then_inc(n_ready,1)
                def hhi(tau):
                    act.wait_ge(h_ready,tau+2)
                    A(h_split[:,:,0,:],h_tile[:],ACT.Copy).then_inc(hh_ready,1)
                def drives(t):
                    act.wait_ge(drive_ready,t+1)
                    for i,c in enumerate((a[0],a[2],a[3])):
                        x=A(dscaled[:,i],drive[:],ACT.Copy,scale=c)
                    x.then_inc(dsc_ready,1)
                def step(t,g,prep):
                    for s in range(4):
                        act.wait_ge(q_ready,t*4+s+1)
                        A(th_hi[:,s%2],QP(s),ACT.Tanh).then_inc(th_ready,1)
                        A(th_ps[:,s%2],QP(s),ACT.Tanh).then_inc(t_ready,1)
                        if s==0:
                            if g: hhi(t+1)
                            act.wait_ge(qc_ready,t+1)
                            qv=q_clip[:]
                        else: qv=QP(s)
                        A(qsq[:,s%2],qv,ACT.Square).then_inc(sq_done,1)
                        if s==0:
                            act.wait_ge(p_ready,t+1)
                            A(kp[:,1],p_tile[:],ACT.Copy,scale=Rc[1][0]).then_inc(kp_ready,1)
                            A(kp[:,2],p_tile[:],ACT.Copy,scale=Rc[2][0])
                            A(kp[:,3],p_tile[:],ACT.Copy,scale=Rc[3][0]).then_inc(kp_ready,1)
                            A(kp[:,4],p_tile[:],ACT.Copy,scale=Pc[0])
                        if s==3 and g: cand(t+2)
                        A(pterm[:,s],qv,ACT.Copy,scale=Pc[s+1]).then_inc(pterm_ready,1)
                        if s==2 and g:
                            gates(t+2)
                            omzs(t+2)
                        if s==3 and prep: drives(t+1)
                act.wait_ge(init,1)
                for tau in range(2):
                    hhi(tau-1); gates(tau); omzs(tau); cand(tau)
                drives(0)
                for t in range(2): step(t,True,True)
                with nc.Fori(1,(T-2)//2,engines=(mybir.EngineType.Activation,)) as t:
                    for uu in range(2): step(t*2+uu,True,True)
                step(T-2,False,True); step(T-1,False,False)
                act.wait_ge(rst3_ready, 1)
                nc.scalar.activation(rstd_rows[:], bank[1][0:T // 8, 0:128], ACT.Copy).then_inc(rs_rows_ready, 1)

                def l3_norm(b):
                    act.wait_ge(xg_ready, 1)
                    at_least(act, qkv3_ready, b)
                    for k in range(KC):
                        i = nc.scalar.activation(xn[:, k], xg[:, :, k, bass.ds(b, 1)].rearrange("p t o -> p (t o)"), ACT.Identity, scale=gain_shift[:, k, bass.ds(b, 1)], bias=gain_shift[:, 2 + k, bass.ds(b, 1)])
                    i.then_inc(xn_ready, 1)

                def l3_squares(b):
                    act.wait_ge(qkv3_ready, b + 1)
                    at_least(act, qk_sum_ready, b)
                    nc.scalar.activation(qk_sq[:].rearrange("p w h d -> p (w h d)"), bank[1][:], ACT.Square).then_inc(qk_sq_ready, 1)

                def l3_copy_v(b):
                    act.wait_ge(qkv3_ready, b + 1)
                    act.wait_ge(qk_n_ready, b + 1)
                    at_least(act, pv3_ready, b * GROUPS)
                    nc.scalar.activation(v3_sb[:], bank[0][:, 0:N], ACT.Copy).then_inc(v3_copied, 1)

                def l3_copy_q(b):
                    act.wait_ge(qkt3_ready, 2 * b + 1)
                    at_least(act, s3_ready, b * GROUPS)
                    nc.scalar.activation(q3_rows[:].rearrange("p g t -> p (g t)"), bank[2][:], ACT.Copy).then_inc(q3_copied, 1)

                def l3_exponentials(b, g):
                    n = b * GROUPS + g
                    act.wait_ge(m3_ready, n + 1)
                    at_least(act, t3_ready, n - 1)
                    if g == 0:
                        at_least(act, o3_ready, b)
                    for j in range(4):
                        i = nc.scalar.activation(probs3[:, g % 2, j], bank[4 + g % 2][:, j * T:(j + 1) * T], ACT.Exp, bias=negmax3[:, g % 2, j:j + 1], accum_out=esum3[:, 4 * j + g:4 * j + g + 1])
                    i.then_inc(p3_ready, 1)

                def l3_act_body(b):
                    if has_next(b):
                        l3_norm(b + 1)
                    l3_exponentials(b, 0)
                    l3_exponentials(b, 1)
                    if has_next(b):
                        l3_squares(b + 1)
                    l3_exponentials(b, 2)
                    l3_exponentials(b, 3)
                    if has_next(b):
                        l3_copy_v(b + 1)
                        l3_copy_q(b + 1)
                    act.wait_ge(ot3_ready, b + 1)
                    nc.scalar.activation(o_t[:].rearrange("p k t -> p (k t)"), bank[6][:, 0:N], ACT.Copy).then_inc(ot3_copied, 1)

                l3_norm(0)
                l3_squares(0)
                l3_copy_v(0)
                l3_copy_q(0)
                l3_batches(mybir.EngineType.Activation, l3_act_body)

            @block.gpsimd
            def _(pool):
                def l0_stack(b, parity):
                    for pair in range(2):
                        for full, hi_part, stack, ready, stacked in ((q_full, q_hi_part, q_stack, q_copied, q_stacked), (k_full, k_hi_part, k_stack, k_hi_ready, k_stacked)):
                            pool.wait_ge(ready, b * 2 + pair + 1)
                            at_least(pool, s0_ready, (b - 1) * HEADS)
                            nc.gpsimd.tensor_tensor(stack[:, parity, 2 * pair:2 * pair + 2].rearrange("p g n -> p (g n)"), full[:], hi_part[:], ALU.subtract).then_inc(stacked, 1)

                l0_stack(0, 0)
                l0_stack(1, 1)
                nc.gpsimd.memset(SEQ[:, 0:SLOT], 0.0)
                nc.gpsimd.memset(ones16[:], 1.0)
                nc.gpsimd.memset(bhn3[:], 0.0)
                nc.gpsimd.memset(mean_ones[:], 1.0 / N)
                nc.gpsimd.memset(minus_half[:], -0.5)
                nc.gpsimd.memset(qk_pad[:], 0.0).then_inc(pool_setup, 1)
                pool.wait_ge(weights_loaded, 15 * 16)
                pool.wait_ge(pool_setup, 1)
                done = 1
                for source, parts in ((WHHf, WHH), (WCf, WC), (bhn, bhnp)):
                    for w in range(3):
                        part = parts[:, w]
                        nc.gpsimd.tensor_copy(part, source[:]).then_inc(pool_setup, 1)
                        done += 1
                        pool.wait_ge(pool_setup, done)
                        if w < 2:
                            nc.gpsimd.tensor_tensor(source[:], source[:], part, ALU.subtract).then_inc(pool_setup, 1)
                            done += 1
                            pool.wait_ge(pool_setup, done)
                nc.gpsimd.tensor_scalar(biasT[:], biasT[:], P_SHIFT, None, ALU.subtract)
                pool.wait_ge(first_loaded, 112)
                for k in range(KC):
                    diagonal = w_out_sb[:, k, k * 128:(k + 1) * 128]
                    i = nc.gpsimd.tensor_tensor(diagonal, diagonal, identity[:], ALU.add)
                i.then_inc(splits_ready, 1)
                nc.gpsimd.tensor_tensor(gate_bias[:, 0:4], b_ih_sb[:, 0:4], b_hh_sb[:, 0:4], ALU.add)
                nc.gpsimd.tensor_copy(gate_bias[:, 4:6], b_ih_sb[:, 4:6]).then_inc(gate_bias_ready, 1)
                with nc.Fori(0, B // 2 - 1, engines=(mybir.EngineType.Pool,)) as u:
                    for half in range(2):
                        l0_stack(u * 2 + 2 + half, half)
                pool.wait_ge(y0_added, B)
                pool.wait_ge(gi_ready, 24)

                G=nc.gpsimd.tensor_tensor
                def xs(t):
                    return SEQ[:,bass.ds((t+1)*32,32)]
                def hlo(tau):
                    pool.wait_ge(hh_ready,tau+2)
                    G(h_split[:,:,1,:],h_tile[:],h_split[:,:,0,:],ALU.subtract).then_inc(hs_ready,1)
                def ncomb(tau):
                    pool.wait_ge(omz_ready,tau+1); pool.wait_ge(n_ready,tau+1)
                    G(hz[:],ncand[:],omz[:],ALU.mult).then_inc(hz_done,1)
                def addh(tau):
                    G(xs(tau),xs(tau),h_tile[:],ALU.add).then_inc(x2_done,1)
                def mkdrive(t):
                    G(drive[:],xs(t),biasT[:],ALU.add).then_inc(drive_ready,1)
                def step(t,g,prep):
                    for s in range(4):
                        if s==3 and g: ncomb(t+2)
                        if s==0:
                            if g: hlo(t+1)
                            pool.wait_ge(kp_ready,t*2+1)
                            G(rinit[:,1],kp[:,1],dscaled[:,0],ALU.add).then_inc(rinit_a,1)
                            pool.wait_ge(kp_ready,t*2+2)
                            G(rinit[:,2],kp[:,2],dscaled[:,1],ALU.add)
                            G(rinit[:,3],kp[:,3],dscaled[:,2],ALU.add).then_inc(rinit_b,1)
                        pool.wait_ge(pterm_ready,t*4+s+1)
                        if s>0: pool.wait_ge(psum_done,t*4+s)
                        if s==2 and prep: pool.wait_ge(x2_done,t+2)
                        G(pacc[:,s],(kp[:,4] if s==0 else pacc[:,s-1]),pterm[:,s],ALU.add).then_inc(psum_done,1)
                        if s==1:
                            if prep: addh(t+1)
                        if s==2:
                            if prep: mkdrive(t+1)
                            G(xs(t-1),xs(t-1),q_clip[:],ALU.add).then_inc(x3_done,1)
                hlo(-1)
                ncomb(0); hlo(0); addh(0); ncomb(1)
                pool.wait_ge(x2_done,1)
                mkdrive(0)
                for t in range(2): step(t,True,True)
                with nc.Fori(1,(T-2)//2,engines=(mybir.EngineType.Pool,)) as t:
                    for uu in range(2): step(t*2+uu,True,True)
                step(T-2,False,True); step(T-1,False,False)
                pool.wait_ge(qc_ready,T+1)
                G(xs(T-1),xs(T-1),q_clip[:],ALU.add).then_inc(x3_done,1)
                pool.wait_ge(me3_ready, 1)
                nc.gpsimd.tensor_tensor(rstd3[:], mean_eps[:], minus_half[:, 0:T // 8], ALU.pow).then_inc(rs3_ready, 1)

                def l3_head_norms(b):
                    pool.wait_ge(qk_mean_ready, b + 1)
                    nc.gpsimd.tensor_tensor(qk_rstd[:].rearrange("p w h -> p (w h)"), qk_mean[:].rearrange("p w h -> p (w h)"), minus_half[:, 0:2 * HEADS], ALU.pow).then_inc(qk_rstd_ready, 1)
                    pool.wait_ge(qk_n_ready, b + 1)
                    at_least(pool, qkt3_ready, 2 * b)
                    nc.gpsimd.tensor_tensor(qk_pad[:, :, :, 0:D3].rearrange("p w h d -> p (w h) d"), qk_n[:].rearrange("p w h d -> p (w h) d"), g_qk_sb[:].rearrange("p w h d -> p (w h) d"), ALU.mult).then_inc(qk3_ready, 1)

                def l3_pool_body(b):
                    at_least(pool, final_ready, b)
                    pool.wait_ge(x3_done, T + 1)
                    nc.gpsimd.tensor_copy(x3_b[:], seq[:, 1:, :, bass.ds(b, 1)].rearrange("p t k o -> p k (t o)")).then_inc(x3_taken, 1)
                    if has_next(b):
                        l3_head_norms(b + 1)

                l3_head_norms(0)
                l3_batches(mybir.EngineType.Pool, l3_pool_body)

            @block.vector
            def _(dve):
                dve.wait_ge(first_loaded, 112)
                nc.vector.tensor_scalar(k_const[:], b0_sb[:], row_consts[:, 4:5], row_consts[:, 5:6], ALU.mult, ALU.add).then_inc(dve_setup, 1)
                dve.wait_ge(mask_loaded, 64)
                for b in range(4):
                    i = nc.vector.tensor_scalar(mask_rows[:, 4 * b:4 * b + 4], mask_rows[:, 4 * b:4 * b + 4], row_consts[:, 6:7], row_consts[:, 7:8], ALU.mult, ALU.add)
                i.then_inc(dve_setup, 1)
                dve.wait_ge(dve_setup, 2)

                def l0_mask_k(b, pair):
                    dve.wait_ge(kr0_ready, b * 2 + pair + 1)
                    at_least(dve, k_stacked, b * 2 + pair)
                    nc.vector.scalar_tensor_tensor(out=k_full[:].rearrange("p (g n) -> p g n", g=2), in0=bank[5][:].rearrange("p (g n) -> p g n", g=2), scalar=k_const[:],
                                                   in1=mask_rows[:, bass.ds(b, 1), :].broadcast_to([128, 2, N]), op0=ALU.add, op1=ALU.mult).then_inc(k_copied, 1)

                def l0_value_lows(b, parity):
                    dve.wait_ge(v_hi_ready, b + 1)
                    for kc in range(KC):
                        i = nc.vector.tensor_tensor(v_parts[:, parity, kc, :, 1], bank[4][:, kc * T:(kc + 1) * T].rearrange("p (h d) -> p h d", d=D0), v_parts[:, parity, kc, :, 0], ALU.subtract)
                    i.then_inc(v_lo_ready, 1)

                def l0_finish(b, parity):
                    dve.wait_ge(pv0_ready, (b + 1) * HEADS)
                    at_least(dve, y0_added, b)
                    nc.vector.reciprocal(rsum0[:], esum0[:, parity])
                    nc.vector.tensor_reduce(y_sum[:].rearrange("p c t -> p (c t)"), bank[6 + parity][:].rearrange("p (h w d) -> p h d w", w=2, d=D0), AXIS_X, ALU.add).then_inc(l0_tail, 1)
                    dve.wait_ge(l0_tail, b * 2 + 1)
                    nc.vector.tensor_tensor(y_sb[:].rearrange("p c (h d) -> p (c h) d", d=D0), y_sum[:].rearrange("p c (h d) -> p (c h) d", d=D0),
                                            rsum0[:].rearrange("p c h -> p (c h)").unsqueeze(2).broadcast_to([128, KC * HEADS, D0]), ALU.mult).then_inc(l0_tail, 1)
                    dve.wait_ge(l0_tail, b * 2 + 2)
                    dve.wait_ge(seq_loaded, 16)
                    x_b = seq[:, 1:, :, bass.ds(b, 1)].rearrange("p t k o -> p k (t o)")
                    nc.vector.tensor_tensor(x_b, x_b, y_sb[:], ALU.add).then_inc(y0_added, 1)

                def l0_dve_slot(b, parity, h):
                    n = b * HEADS + h
                    if h < HEADS:
                        dve.wait_ge(s0_ready, n + 1)
                        nc.vector.tensor_reduce(negmax0[:, h % 4], bank[h % 2][:].rearrange("p (c k) -> p c k", c=KC), AXIS_X, ALU.max, negate=True).then_inc(m0_ready, 1)
                    if not isinstance(n, int) or 3 <= n < B * HEADS + 3:
                        dve.wait_ge(p_hi_ready, n - 2)
                        m = (h - 3) % 4
                        nc.vector.tensor_tensor(probs0_t[:, m, 1].rearrange("p c k -> p (c k)"), bank[2 + m % 2][:], probs0_t[:, m, 0].rearrange("p c k -> p (c k)"), ALU.subtract).then_inc(p_lo_ready, 1)
                    if h == 4 and not (isinstance(b, int) and b == 0):
                        l0_finish(b - 1, 1 - parity)
                    if h == HEADS + 4:
                        l0_finish(b, parity)
                    if not (isinstance(b, int) and b == B - 1):
                        if h in (3, 8):
                            l0_mask_k(b + 1, h // 8)
                        if h == 11:
                            l0_value_lows(b + 1, 1 - parity)

                for pair in range(2):
                    l0_mask_k(0, pair)
                l0_value_lows(0, 0)
                l0_slots(mybir.EngineType.DVE, l0_dve_slot)

                dve.wait_ge(weights_loaded, 15 * 16)
                dve.wait_ge(emb_ready, 1)
                nc.vector.tensor_scalar(b_emb1[:], b_emb_sb[:], 1.0, None, ALU.add).then_inc(dve_setup, 1)
                dve.wait_ge(dve_setup, 3)
                for j in range(4):
                    if j < 2:
                        i = nc.vector.tensor_scalar(gain_shift[:, j], bank[6][:, j * B:(j + 1) * B], b_emb1[:, j:j + 1], g_norm_sb[:, j:j + 1], ALU.add, ALU.mult)
                    else:
                        i = nc.vector.tensor_scalar(gain_shift[:, j], bank[6][:, j * B:(j + 1) * B], b_emb_sb[:, j:j + 1], None, ALU.add)
                i.then_inc(dve_setup, 1)
                dve.wait_ge(gate_bias_ready, 1)
                with nc.Fori(0, 4, engines=(mybir.EngineType.DVE,)) as c:
                    for j in (1, 3, 5):
                        dve.wait_ge(gi_ready, c * 6 + j + 1)
                        nc.vector.tensor_scalar(gi4[:, bass.ds(c * 32, 32), j, :], bank[j][:].rearrange("p (t b) -> p t b", b=B), gate_bias[:, j:j + 1], None, ALU.add).then_inc(gi_d, 1)

                V=nc.vector
                stt=lambda o,i0,sc,i1,op0=ALU.mult,op1=ALU.add: V.scalar_tensor_tensor(out=o,in0=i0,scalar=sc,in1=i1,op0=op0,op1=op1)
                def gis(tau,j0,n): return GI[:,bass.ds(tau*96+j0*16,n*16)]
                def g_rz(tau):
                    dve.wait_ge(grz_ready,tau+1)
                    V.tensor_tensor(gsum[:,0].rearrange("p (j b)->p j b",b=16),Grz[:,:,0,:],gis(tau,0,4).rearrange("p (j b)->p j b",b=16),ALU.add).then_inc(ga_done,1)
                def g_rz2(tau):
                    dve.wait_ge(ga_done,tau+1)
                    V.tensor_tensor(gsum[:,1].rearrange("p (j b)->p j b",b=16),Grz[:,:,1,:],gsum[:,0].rearrange("p (j b)->p j b",b=16),ALU.add).then_inc(a2_ready,1)
                v3=lambda ap: ap.rearrange("p (j b)->p j b",b=16)
                def g_m(tau):
                    dve.wait_ge(gn_ready,tau+1); dve.wait_ge(trz_ready,tau+1)
                    stt(nmul[:],trz[:,0:32],1.0,Gn,ALU.add,ALU.mult).then_inc(nmul_done,1)
                def g_npre(tau):
                    dve.wait_ge(nmul_done,tau+1)
                    stt(npre[:],nmul[:],0.5,gis(tau,4,2)).then_inc(npre_ready,1)
                hv=h_tile[:].rearrange("p k b -> p (k b)")
                def g_zh(tau):
                    stt(hdiff[:],trz[:,32:64],1.0,hv,ALU.add,ALU.mult).then_inc(zh_done,1)
                def g_h(tau,first=False):
                    dve.wait_ge(zh_done,tau+1); dve.wait_ge(hz_done,tau+1)
                    if not first: dve.wait_ge(x2_done,tau)
                    stt(hv,hdiff[:],0.5,hz[:]).then_inc(h_ready,1)
                def r0init(t):
                    dve.wait_ge(p_ready,t+1); dve.wait_ge(dsc_ready,t+1)
                    stt(rinit[:,0],p_tile[:],Rc[0][0],dscaled[:,0]).then_inc(rinit0,1)
                def step(t,g,prep):
                    def tl(s):
                        dve.wait_ge(t_ready,t*4+s+1)
                        V.tensor_tensor(th_lo[:,s%2],th_ps[:,s%2],th_hi[:,s%2],ALU.subtract).then_inc(tl_ready,1)
                    def mkbase(s):
                        dve.wait_ge(rs_done,t*4+s+1); dve.wait_ge(cube_ready,t*4+s+1)
                        stt(base[:,s%2],qcube[:,s%2],-a[s]/3,rlin[:,s]).then_inc(base_done,1)
                    def cube(s):
                        dve.wait_ge(sq_done,t*4+s+1)
                        V.tensor_tensor(qcube[:,s%2],qsq[:,s%2],(q_clip[:] if s==0 else q_tile[:,s]),ALU.mult).then_inc(cube_ready,1)
                    def upd(s):
                        dve.wait_ge(base_done,t*4+s+1); dve.wait_ge(c_ready,t*4+s+1)
                        stt(QP(s+1),C(s),a[s],base[:,s%2]).then_inc(q_ready,1)
                        stt(q_tile[:,(s+1)%4],C(s),a[s],base[:,s%2]).then_inc(qs_ready,1)
                    def rt(j,i,src):
                        return stt(rlin[:,j],q_clip[:] if i==0 else q_tile[:,i],Rc[j][i+1],src[:,j])
                    dve.wait_ge(psum_done,t*4)
                    V.tensor_scalar(p_tile[:],pacc[:,3],20.-.875,-20.-.875,ALU.min,ALU.max).then_inc(p_ready,1)
                    dve.wait_ge(x3_done,t)
                    dve.wait_ge(qs_ready,t*4+1)
                    V.tensor_scalar(q_clip[:],q_tile[:,0],20.,-20.,ALU.min,ALU.max).then_inc(qc_ready,1)
                    r0init(t)
                    tl(0)
                    dve.wait_ge(qc_ready,t+1); dve.wait_ge(rinit0,t+1)
                    rt(0,0,rinit).then_inc(rs_done,1)
                    cube(0)
                    mkbase(0)
                    upd(0)
                    dve.wait_ge(rinit_a,t+1)
                    rt(1,0,rinit).then_inc(terms0,1)
                    tl(1)
                    dve.wait_ge(qs_ready,t*4+2); dve.wait_ge(terms0,t+1)
                    rt(1,1,rlin).then_inc(rs_done,1)
                    cube(1)
                    dve.wait_ge(rinit_b,t+1)
                    rt(2,0,rinit).then_inc(terms1,1)
                    mkbase(1)
                    rt(3,0,rinit).then_inc(terms2,1)
                    if g: g_rz(t+2)
                    upd(1)
                    if g: g_rz2(t+2)
                    dve.wait_ge(terms1,t+1)
                    rt(2,1,rlin).then_inc(terms3,1)
                    tl(2)
                    dve.wait_ge(qs_ready,t*4+3)
                    dve.wait_ge(terms3,t+1)
                    rt(2,2,rlin).then_inc(rs_done,1)
                    cube(2)
                    dve.wait_ge(terms2,t+1)
                    rt(3,1,rlin).then_inc(terms4,1)
                    mkbase(2)
                    if g: g_m(t+2)
                    upd(2)
                    if g: g_npre(t+2)
                    dve.wait_ge(terms4,t+1)
                    rt(3,2,rlin).then_inc(terms5,1)
                    if g: g_zh(t+2)
                    tl(3)
                    dve.wait_ge(qs_ready,t*4+4); dve.wait_ge(terms5,t+1)
                    rt(3,3,rlin).then_inc(rs_done,1)
                    cube(3)
                    mkbase(3)
                    if g: g_h(t+2)
                    upd(3)
                dve.wait_ge(gi_a, 12)
                dve.wait_ge(gi_d, 12)
                V.tensor_copy(QP(0),condT[:])
                V.tensor_scalar(pacc[:,3],condT[:],P_SHIFT,None,ALU.subtract)
                V.tensor_copy(q_tile[:,0],condT[:]).then_inc(qs_ready,1)
                V.tensor_copy(hv,condT[:]).then_inc(h_ready,1)
                dve.wait_ge(h_ready,1)
                V.tensor_copy(r1[:,0:1],condT[:,0:1]).then_inc(init,1)
                V.tensor_copy(r1[:,1:2],condT[:,0:1]).then_inc(q_ready,1)
                for tau in range(2):
                    g_rz(tau); g_rz2(tau); g_m(tau); g_npre(tau); g_zh(tau); g_h(tau,tau==0)
                for t in range(14): step(t,True,True)
                with nc.Fori(1,(T-2)//14,engines=(mybir.EngineType.DVE,)) as t:
                    for uu in range(14): step(t*14+uu,True,True)
                step(T-2,False,True); step(T-1,False,False)
                dve.wait_ge(x3_done,T)
                dve.wait_ge(qs_ready,4*T+1)
                V.tensor_scalar(q_clip[:],q_tile[:,0],20.,-20.,ALU.min,ALU.max).then_inc(qc_ready,1)
                dve.wait_ge(x3_done, T + 1)
                for c in range(4):
                    part = seq[:, 1 + 32 * c:33 + 32 * c]
                    nc.vector.tensor_tensor(sq3[:, :, 32 * c:32 * c + 32].rearrange("p k t b -> p t k b"), part, part, ALU.mult).then_inc(sq3_ready, 1)
                dve.wait_ge(ms3_ready, 1)
                nc.vector.tensor_scalar(mean_eps[:], bank[0][:, 0:T // 8], EPS, None, ALU.add).then_inc(me3_ready, 1)
                for c in range(4):
                    dve.wait_ge(rsb3_ready, c + 1)
                    for k in range(KC):
                        i = nc.vector.tensor_tensor(xg[:, 32 * c:32 * c + 32, k], seq[:, 1 + 32 * c:33 + 32 * c, k], bank[2 + c][:].rearrange("p (t b) -> p t b", b=B), ALU.mult)
                i.then_inc(xg_ready, 1)

                def l3_head_means(b):
                    dve.wait_ge(qk_sq_ready, b + 1)
                    nc.vector.tensor_reduce(qk_sum[:].rearrange("p w h -> p (w h)"), qk_sq[:].rearrange("p w h d -> p (w h) d"), AXIS_X, ALU.add).then_inc(qk_sum_ready, 1)
                    dve.wait_ge(qk_sum_ready, b + 1)
                    nc.vector.tensor_scalar(qk_mean[:], qk_sum[:], 1.0 / D3, EPS, ALU.mult, ALU.add).then_inc(qk_mean_ready, 1)

                def l3_head_scale(b):
                    dve.wait_ge(qk_rstd_ready, b + 1)
                    at_least(dve, qk3_ready, b)
                    nc.vector.tensor_tensor(qk_n[:].rearrange("p w h d -> p (w h) d"), bank[1][:].rearrange("p (h d) -> p h d", d=D3),
                                            qk_rstd[:].rearrange("p w h -> p (w h)").unsqueeze(2).broadcast_to([128, 2 * HEADS, D3]), ALU.mult).then_inc(qk_n_ready, 1)

                def l3_copy_k(b):
                    dve.wait_ge(qkt3_ready, 2 * b + 2)
                    at_least(dve, s3_ready, b * GROUPS)
                    nc.vector.tensor_scalar(k3_rows[:].rearrange("p g t -> p (g t)"), bank[3][:], float(D3 ** -0.5), None, ALU.mult).then_inc(k3_copied, 1)

                def l3_maxima(b, g):
                    n = b * GROUPS + g
                    dve.wait_ge(s3_ready, n + 1)
                    nc.vector.tensor_reduce(negmax3[:, g % 2], bank[4 + g % 2][:].rearrange("p (c k) -> p c k", c=4), AXIS_X, ALU.max, negate=True).then_inc(m3_ready, 1)

                def l3_copy_probs(b, g):
                    n = b * GROUPS + g
                    dve.wait_ge(t3_ready, n + 1)
                    at_least(dve, pv3_ready, n - 1)
                    nc.vector.tensor_copy(probs3_t[:, g % 2].rearrange("p j t -> p (j t)"), bank[6][:]).then_inc(pt3_copied, 1)

                def l3_dve_body(b):
                    l3_maxima(b, 0)
                    l3_maxima(b, 1)
                    l3_copy_probs(b, 0)
                    if has_next(b):
                        l3_head_means(b + 1)
                    l3_maxima(b, 2)
                    l3_copy_probs(b, 1)
                    l3_maxima(b, 3)
                    l3_copy_probs(b, 2)
                    l3_copy_probs(b, 3)
                    if has_next(b):
                        l3_head_scale(b + 1)
                    dve.wait_ge(p3_ready, (b + 1) * GROUPS)
                    nc.vector.reciprocal(rsum3[:], esum3[:]).then_inc(rsum3_ready, 1)
                    dve.wait_ge(rsum3_ready, b + 1)
                    dve.wait_ge(pv3_ready, (b + 1) * GROUPS)
                    nc.vector.tensor_tensor(o_sb[:].rearrange("p (h d) -> p h d", d=D3), bank[7][:, 0:N].rearrange("p (h d) -> p h d", d=D3),
                                            rsum3[:].unsqueeze(2).broadcast_to([128, HEADS, D3]), ALU.mult).then_inc(o3_ready, 1)
                    if has_next(b):
                        l3_copy_k(b + 1)
                    dve.wait_ge(final_ready, b + 1)
                    at_least(dve, out_stored, b * 16)
                    nc.vector.tensor_copy(out_sb[:], bank[7][:, N:]).then_inc(out_ready, 1)

                l3_head_means(0)
                l3_head_scale(0)
                l3_copy_k(0)
                l3_batches(mybir.EngineType.DVE, l3_dve_body)


def kernel(**inputs):
    import concourse.bacc as bacc
    from concourse.bass_utils import run_bass_kernel_spmd

    def by_feature(v):
        return v.reshape(KC, 128, -1).transpose(1, 0, 2)

    def padded(w):
        p = np.zeros((T, GROUPS, 4, 32), w.dtype)
        for i in range(3):
            p[..., i * D0:(i + 1) * D0] = w.T.reshape(T, GROUPS, 4, D0)
        return p.reshape(T, GROUPS, 128)

    v = {k: np.asarray(x) for k, x in inputs.items()}
    x, cond = v["x"], v["cond_2048"]
    mask_row = 3 * D0 + 2
    low_q, low_k, consts = np.zeros(32), np.zeros(32), np.zeros((32, 8))
    low_q[D0:2 * D0] = 1.0
    low_k[2 * D0:3 * D0] = 1.0
    low_k[3 * D0 + 1] = 1.0
    consts[3 * D0:3 * D0 + 2, 0] = 1.0
    consts[mask_row, 0] = NEG
    consts[:, 1] = low_q / np.sqrt(D0)
    consts[:, 3] = low_k
    consts[3 * D0:3 * D0 + 2, 4] = 1.0
    consts[mask_row, 5] = -NEG
    consts[:, 6] = 1.0
    consts[mask_row, 6] = -1.0
    consts[mask_row, 7] = 1.0
    rows = np.tile(consts, (4, 1)).astype(np.float32)
    arrays = {
        "x_cbn": x.transpose(1, 0, 2),
        "x_seq": x.reshape(B, T, KC, 128).transpose(3, 1, 2, 0).reshape(128, T * SLOT),
        "cond_rows": cond[None],
        "cond_t": by_feature(cond.T).reshape(128, SLOT),
        "wq_pad": padded(v["L0_cond_Wq"]), "wk_pad": padded(v["L0_cond_Wk"]), "wv_t": v["L0_cond_Wv"].T,
        "b0": v["L0_cond_b"].reshape(1, 1),
        "w_ih": by_feature(v["L1_cond_W_ih"]), "w_hh": by_feature(v["L1_cond_W_hh"]),
        "b_ih": v["L1_cond_b_ih"].reshape(6, 128).T, "b_hh": v["L1_cond_b_hh"].reshape(6, 128).T,
        "b_hn": v["L1_cond_b_hh"][None, 2 * N:],
        "coupling_t": by_feature(v["L2_cond_coupling"].T),
        "bias_t": np.repeat(v["L2_cond_bias"].reshape(KC, 128).T, B, axis=1),
        "w_emb": by_feature(v["L3_cond_W_emb"]), "b_emb": v["L3_cond_b_emb"].reshape(4, 128).T,
        "g_norm": v["L3_cond_g_norm"].reshape(KC, 128).T,
        "w_qkv": by_feature(v["L3_cond_W_qkv"]),
        "g_q": v["L3_cond_g_q"].reshape(1, 1, D3), "g_k": v["L3_cond_g_k"].reshape(1, 1, D3),
        "w_out": by_feature(v["L3_cond_W_out"]),
        "identity_in": np.eye(128, dtype=np.float32), "row_consts_in": rows, "select_in": np.repeat(np.eye(T // 8, dtype=np.float32)[:, :, None], 128, axis=2),
    }
    nc = bacc.Bacc("TRN2", target_bir_lowering=False, num_devices=1)
    args, ins = {}, {}
    for name, a in arrays.items():
        ins[f"in_{name}_dram"] = np.ascontiguousarray(a)
        args[name] = nc.dram_tensor(f"in_{name}_dram", a.shape, mybir.dt.from_np(a.dtype), kind="ExternalInput").ap()
    out = nc.dram_tensor("out_0_dram", [B, T, N], FP32, kind="ExternalOutput").ap()
    cond_resid_kernel(nc, **args, out=out.rearrange("b t n -> t b n"))
    r = run_bass_kernel_spmd(nc, [ins], core_ids=[0])
    return r.results[0]["out_0_dram"]
```

```python
import numpy as np
import concourse.bass as bass
import concourse.mybir as mybir
from contextlib import ExitStack

FP32 = mybir.dt.float32
BF16 = mybir.dt.bfloat16
FP16 = mybir.dt.float16
ALU = mybir.AluOpType
ACT = mybir.ActivationFunctionType
AXIS_X = mybir.AxisListType.X

B = 16
T = 128
N = 256
KC = N // 128
SLOT = KC * B
HEADS = 16
D0 = T // HEADS
V0 = 2 * D0 + 1
D3 = N // HEADS
V3 = D3 + 1
GROUPS = 4
NEG = 60000.0
EPS = 1e-6
CLAMP = 20.0
S0_BANK = [(0, 1, 5)[h % 3] for h in range(HEADS - 1)] + [1]
S0_DISTANCE = [4, 2, 4] + [3] * (HEADS - 4) + [2]
S3_BANK = (4, 5, 3, 4)
FIRST_LOADS = 7
WEIGHT_LOADS = 15
L0_DRAIN = 7
P_SHIFT = 0.7 / 0.8


def rk4_coefficients():
    dt, eps, beta = 0.01, 0.08, 0.8
    a = [dt / 2, dt / 2, dt, dt / 6]

    def unit(i):
        return [1.0 if j == i else 0.0 for j in range(5)]

    p_stage = [unit(0)]
    for s in range(3):
        c = a[s] * eps
        p_stage.append([unit(0)[i] + c * (unit(s + 1)[i] - beta * p_stage[s][i]) for i in range(5)])
    p_next = unit(0)
    for s, w in enumerate((1, 2, 2, 1)):
        p_next = [p_next[i] + dt * eps / 6 * w * (unit(s + 1)[i] - beta * p_stage[s][i]) for i in range(5)]
    rows = []
    for s in range(4):
        if s < 3:
            own = unit(1)
        else:
            own = [(-unit(1)[i] + unit(2)[i] + 2 * unit(3)[i] + unit(4)[i]) / 3 for i in range(5)]
        rows.append([own[i] - a[s] * p_stage[s][i] + a[s] * unit(s + 1)[i] for i in range(5)])
    return a, rows, p_next


def cond_resid_kernel(nc, x_cbn, x_seq, cond_rows, cond_t, wq_pad, wk_pad, wv_t, b0, w_ih, w_hh, b_ih, b_hh, b_hn,
                      coupling_t, bias_t, w_emb, b_emb, g_norm, w_qkv, g_q, g_k, w_out, identity_in, row_consts_in, select_in, out):
    ctx = ExitStack()
    with ctx:
        def sb(name, shape, dtype=FP32):
            return ctx.enter_context(nc.sbuf_tensor(name, shape, dtype))

        def sem(name):
            return ctx.enter_context(nc.semaphore(name))

        bank = [ctx.enter_context(nc.psum_tensor(f"bank{i}", [128, 512], FP32)) for i in range(8)]

        SEQ = sb("SEQ", [128, (T + 1) * SLOT])
        GI = sb("GI", [128, T * 96])
        seq = SEQ[:].rearrange("p (s k b) -> p s k b", k=KC, b=B)
        gi4 = GI[:].rearrange("p (t j b) -> p t j b", j=6, b=B)
        x_b0 = sb("x_b0", [128, N])
        identity = sb("identity", [128, 128])
        row_consts = sb("row_consts", [128, 9])
        wq_sb = sb("wq_sb", [128, GROUPS, 128])
        wk_sb = sb("wk_sb", [128, GROUPS, 128])
        wv_sb = sb("wv_sb", [128, T])
        select_sb = sb("select_sb", [T // 8, T // 8, 128])
        b0_sb = sb("b0_sb", [128, 1])
        k_const = sb("k_const", [128, 1])
        mask_rows = sb("mask_rows", [128, B, N])
        w_ih_sb = sb("w_ih_sb", [128, KC, 3 * N])
        b_ih_sb = sb("b_ih_sb", [128, 6])
        b_hh_sb = sb("b_hh_sb", [128, 6])
        gate_bias = sb("gate_bias", [128, 6])
        w_hh_sb = sb("w_hh_sb", [128, KC, 3 * N])
        coupling_sb = sb("coupling_sb", [128, KC, N])
        w_hh_parts = sb("w_hh_parts", [128, 3, KC, 3 * N], BF16)
        coupling_parts = sb("coupling_parts", [128, 3, KC, N], BF16)
        cond_sb = sb("cond_sb", [128, SLOT])
        bias_sb = sb("bias_sb", [128, SLOT])
        b_hn_sb = sb("b_hn_sb", [1, N])
        b_hn_parts = sb("b_hn_parts", [1, 3, N], BF16)
        b_hn_rows = sb("b_hn_rows", [128, N], BF16)
        ones16 = sb("ones16", [128, B], BF16)
        w_emb_sb = sb("w_emb_sb", [128, KC, 2 * N])
        b_emb_sb = sb("b_emb_sb", [128, 4])
        b_emb1 = sb("b_emb1", [128, 4])
        g_norm_sb = sb("g_norm_sb", [128, KC])
        gain_shift = sb("gain_shift", [128, 4, B])
        w_qkv_sb = sb("w_qkv_sb", [128, KC, 3 * N])
        g_qk_sb = sb("g_qk_sb", [128, 2, HEADS, D3])
        w_out_sb = sb("w_out_sb", [128, KC, N])
        mean_ones = sb("mean_ones", [128, 128])
        minus_half = sb("minus_half", [128, 128])

        q_full = sb("q_full", [128, 2 * N])
        q_hi_part = sb("q_hi_part", [128, 2 * N], FP16)
        k_full = sb("k_full", [128, 2 * N])
        k_hi_part = sb("k_hi_part", [128, 2 * N], FP16)
        q_stack = sb("q_stack", [128, 2, GROUPS, N], FP16)
        k_stack = sb("k_stack", [128, 2, GROUPS, N], FP16)
        v_parts = sb("v_parts", [128, 2, KC, HEADS, V0], FP16)
        negmax0 = sb("negmax0", [128, 4, KC])
        rsum0 = sb("rsum0", [128, KC, HEADS])
        probs0 = sb("probs0", [128, 4, KC, N])
        probs0_t = sb("probs0_t", [128, 4, 2, KC, N], FP16)
        y_sum = sb("y_sum", [128, KC, HEADS, D0])
        y_sb = sb("y_sb", [128, KC, T])

        q_state = sb("q_state", [128, 4, 32])
        q_clipped = sb("q_clipped", [128, 32])
        tanh_hi = sb("tanh_hi", [128, 2, 32], FP16)
        tanh_lo = sb("tanh_lo", [128, 2, 32], FP16)
        q_squared = sb("q_squared", [128, 2, 32])
        cubic = sb("cubic", [128, 2, 32])
        stage_base = sb("stage_base", [128, 2, 32])
        linear = sb("linear", [128, 4, 32])
        linear_start = sb("linear_start", [128, 4, 32])
        p_scaled = sb("p_scaled", [128, 5, 32])
        p_sum = sb("p_sum", [128, 4, 32])
        p_term = sb("p_term", [128, 4, 32])
        p_state = sb("p_state", [128, 32])
        drive = sb("drive", [128, 32])
        drive_scaled = sb("drive_scaled", [128, 3, 32])
        h_tile = sb("h_tile", [128, 2, 16])
        h_split = sb("h_split", [128, 2, 2, 16], FP16)
        gate_sum = sb("gate_sum", [128, 2, 64])
        gate_tanh = sb("gate_tanh", [128, 64])
        reset_times = sb("reset_times", [128, 32])
        cand_in = sb("cand_in", [128, 32])
        cand_tile = sb("cand_tile", [128, 32])
        kept_part = sb("kept_part", [128, 32])
        new_part = sb("new_part", [128, 32])
        one_minus_z = sb("one_minus_z", [128, 32])

        start_marks = sb("start_marks", [128, 2])
        mean_eps = sb("mean_eps", [128, T // 8])
        rstd3 = sb("rstd3", [128, T // 8])
        rstd_rows = sb("rstd_rows", [T // 8, 128])
        sq3 = GI[:, 0:T * SLOT].rearrange("p (k t b) -> p k t b", k=KC, b=B)
        xg = GI[:, T * SLOT:2 * T * SLOT].rearrange("p (t k b) -> p t k b", k=KC, b=B)
        x3_b = sb("x3_b", [128, KC, T])
        xn = sb("xn", [128, KC, T])
        qk_sq = sb("qk_sq", [128, 2, HEADS, D3])
        qk_sum = sb("qk_sum", [128, 2, HEADS])
        qk_mean = sb("qk_mean", [128, 2, HEADS])
        qk_rstd = sb("qk_rstd", [128, 2, HEADS])
        qk_g = sb("qk_g", [128, 2, HEADS, D3])
        qk_pad = sb("qk_pad", [128, 2, HEADS, 32])
        v3_parts = sb("v3_parts", [128, 2, HEADS, V3], FP16)
        q3_hi_part = sb("q3_hi_part", [128, GROUPS, T], FP16)
        q3_stack = sb("q3_stack", [128, GROUPS, T], FP16)
        k3_parts = sb("k3_parts", [128, 2, GROUPS, T], FP16)
        negmax3 = sb("negmax3", [128, 4, 4])
        rsum3 = sb("rsum3", [128, HEADS])
        probs3 = probs0[:].rearrange("p a c (j t) -> p a (c j) t", t=T)
        probs3_t = probs0_t[:, 0:2].rearrange("p a w c (j t) -> p a w (c j) t", t=T)
        o_sb = sb("o_sb", [128, N])
        o_t = sb("o_t", [128, KC, T])
        out_sb = sb("out_sb", [128, N])

        gate_sum_ready = sem("gate_sum_ready")
        stage_base_ready = sem("stage_base_ready")
        b_hn_rows_ready = sem("b_hn_rows_ready")
        coupling_ready = sem("coupling_ready")
        cubic_ready = sem("cubic_ready")
        drive_ready = sem("drive_ready")
        drive_scaled_ready = sem("drive_scaled_ready")
        dve_setup = sem("dve_setup")
        emb_ready = sem("emb_ready")
        final_ready = sem("final_ready")
        first_loaded = sem("first_loaded")
        gate_sum_hi_ready = sem("gate_sum_hi_ready")
        gate_bias_ready = sem("gate_bias_ready")
        gi_even_copied = sem("gi_even_copied")
        gi_odd_copied = sem("gi_odd_copied")
        gi_ready = sem("gi_ready")
        cand_products_ready = sem("cand_products_ready")
        gate_products_ready = sem("gate_products_ready")
        h_ready = sem("h_ready")
        h_hi_ready = sem("h_hi_ready")
        h_split_ready = sem("h_split_ready")
        new_part_ready = sem("new_part_ready")
        gru_start_ready = sem("gru_start_ready")
        k3_copied = sem("k3_copied")
        k3_hi_ready = sem("k3_hi_ready")
        k_copied = sem("k_copied")
        k_hi_ready = sem("k_hi_ready")
        k_stacked = sem("k_stacked")
        p_scaled_ready = sem("p_scaled_ready")
        k0_products_ready = sem("k0_products_ready")
        y0_scaled = sem("y0_scaled")
        max0_ready = sem("max0_ready")
        max3_ready = sem("max3_ready")
        mask_loaded = sem("mask_loaded")
        mean_eps_ready = sem("mean_eps_ready")
        mean_square_ready = sem("mean_square_ready")
        cand_ready = sem("cand_ready")
        reset_times_ready = sem("reset_times_ready")
        cand_in_ready = sem("cand_in_ready")
        o_ready = sem("o_ready")
        one_minus_z_ready = sem("one_minus_z_ready")
        ones_ready = sem("ones_ready")
        o_t_ready = sem("o_t_ready")
        o_transposed = sem("o_transposed")
        out_ready = sem("out_ready")
        out_stored = sem("out_stored")
        probs0_ready = sem("probs0_ready")
        probs3_t_hi_ready = sem("probs3_t_hi_ready")
        probs3_t_lo_ready = sem("probs3_t_lo_ready")
        probs3_ready = sem("probs3_ready")
        probs0_t_hi_ready = sem("probs0_t_hi_ready")
        probs0_t_lo_ready = sem("probs0_t_lo_ready")
        p_state_ready = sem("p_state_ready")
        pool_done = sem("pool_done")
        pool_setup = sem("pool_setup")
        p_sum_ready = sem("p_sum_ready")
        p_term_ready = sem("p_term_ready")
        outputs0_ready = sem("outputs0_ready")
        outputs3_ready = sem("outputs3_ready")
        q3_copied = sem("q3_copied")
        q3_hi_ready = sem("q3_hi_ready")
        q_copied = sem("q_copied")
        q_psum_ready = sem("q_psum_ready")
        q_stacked = sem("q_stacked")
        q_clipped_ready = sem("q_clipped_ready")
        qk3_ready = sem("qk3_ready")
        qk_g_ready = sem("qk_g_ready")
        qk_mean_ready = sem("qk_mean_ready")
        qk_rstd_ready = sem("qk_rstd_ready")
        qk_sq_ready = sem("qk_sq_ready")
        qk_sum_ready = sem("qk_sum_ready")
        head_rows_transposed = sem("head_rows_transposed")
        qkv3_ready = sem("qkv3_ready")
        q0_products_ready = sem("q0_products_ready")
        q_state_ready = sem("q_state_ready")
        ready = sem("ready")
        start0_ready = sem("start0_ready")
        start1_ready = sem("start1_ready")
        start23_ready = sem("start23_ready")
        rstd_ready = sem("rstd_ready")
        rstd_rows_ready = sem("rstd_rows_ready")
        rstd_broadcast_ready = sem("rstd_broadcast_ready")
        rstd_transposed = sem("rstd_transposed")
        rsum3_ready = sem("rsum3_ready")
        scores0_ready = sem("scores0_ready")
        scores3_ready = sem("scores3_ready")
        semaphore = sem("semaphore")
        seq_loaded = sem("seq_loaded")
        splits_ready = sem("splits_ready")
        squares_ready = sem("squares_ready")
        q_squared_ready = sem("q_squared_ready")
        stacked = sem("stacked")
        transposed0_ready = sem("transposed0_ready")
        transposed3_ready = sem("transposed3_ready")
        tanh_full_ready = sem("tanh_full_ready")
        linear1_ready = sem("linear1_ready")
        linear2_q0_ready = sem("linear2_q0_ready")
        linear3_q0_ready = sem("linear3_q0_ready")
        linear2_ready = sem("linear2_ready")
        linear3_q1_ready = sem("linear3_q1_ready")
        linear3_ready = sem("linear3_ready")
        tanh_hi_ready = sem("tanh_hi_ready")
        tanh_lo_ready = sem("tanh_lo_ready")
        gate_tanh_ready = sem("gate_tanh_ready")
        v0_products_ready = sem("v0_products_ready")
        v3_copied = sem("v3_copied")
        v3_hi_ready = sem("v3_hi_ready")
        v0_hi_ready = sem("v0_hi_ready")
        v0_lo_ready = sem("v0_lo_ready")
        weights_loaded = sem("weights_loaded")
        x2_ready = sem("x2_ready")
        x3_ready = sem("x3_ready")
        x3_taken = sem("x3_taken")
        x_loaded = sem("x_loaded")
        xg_ready = sem("xg_ready")
        xn_ready = sem("xn_ready")
        y0_added = sem("y0_added")
        y0_taken = sem("y0_taken")
        kept_part_ready = sem("kept_part_ready")
        a, stage_rows, p_row = rk4_coefficients()

        def at_least(engine, semaphore, value):
            if not isinstance(value, int) or value > 0:
                engine.wait_ge(semaphore, value)

        def head_before(b, h, back):
            return (b, h - back) if h >= back else (b - 1, h - back + HEADS)

        def l3_batches(engine_type, body):
            body(0)
            with nc.Fori(0, B - 2, engines=(engine_type,)) as u:
                body(u + 1)
            body(B - 1)

        def has_next(b):
            return not (isinstance(b, int) and b == B - 1)

        def l0_slots(engine_type, slot):
            for h in range(HEADS):
                slot(0, 0, h)
            with nc.Fori(0, B // 2 - 1, engines=(engine_type,)) as u:
                for half in range(2):
                    for h in range(HEADS):
                        slot(u * 2 + half + 1, 1 - half, h)
            for h in range(HEADS + L0_DRAIN):
                slot(B - 1, 1, h)

        def coupling_sum(s):
            return bank[s % 2][:, 0:32]
        gate_psum = bank[2][:, 0:128].rearrange("p (j w b) -> p j w b", j=4, w=2)
        cand_psum = bank[3][:, 0:32]

        def q_psum(s):
            return bank[4 + s % 2][:, 0:32]
        tanh_full = bank[6][:, 0:64].rearrange("p (s n) -> p s n", s=2)

        with nc.Block() as block:
            @block.sync
            def _(sp):
                sp.dma_start(row_consts[:], row_consts_in).then_inc(first_loaded, 16)
                sp.dma_start(b0_sb[:], b0.broadcast_to([128, 1])).then_inc(first_loaded, 16)
                sp.dma_start(wq_sb[:], wq_pad).then_inc(first_loaded, 16)
                sp.dma_start(wk_sb[:], wk_pad).then_inc(first_loaded, 16)
                sp.dma_start(wv_sb[:], wv_t).then_inc(first_loaded, 16)
                sp.dma_start(identity[:], identity_in).then_inc(first_loaded, 16)
                sp.dma_start(select_sb[:], select_in).then_inc(first_loaded, 16)
                sp.dma_start(x_b0[:], x_cbn[:, 0]).then_inc(x_loaded, 16)
                for i in range(4):
                    sp.dma_start(mask_rows[:, 4 * i:4 * i + 4], cond_rows[:, 4 * i:4 * i + 4].broadcast_to([128, 4, N])).then_inc(mask_loaded, 16)
                sp.dma_start(SEQ[:, SLOT:], x_seq).then_inc(seq_loaded, 16)
                for tile, source in ((cond_sb, cond_t), (bias_sb, bias_t), (b_hn_sb, b_hn), (b_ih_sb, b_ih), (b_hh_sb, b_hh),
                                     (b_emb_sb, b_emb), (g_norm_sb, g_norm)):
                    sp.dma_start(tile[:], source).then_inc(weights_loaded, 16)
                for tile, source in ((w_hh_sb, w_hh), (coupling_sb, coupling_t), (w_ih_sb, w_ih), (w_emb_sb, w_emb), (w_qkv_sb, w_qkv), (w_out_sb, w_out)):
                    sp.dma_start(tile[:], source).then_inc(weights_loaded, 16)
                for i, gain in enumerate((g_q, g_k)):
                    sp.dma_start(g_qk_sb[:, i], gain.broadcast_to([128, HEADS, D3])).then_inc(weights_loaded, 16)
                with nc.Fori(0, B - 1, engines=(mybir.EngineType.SP,)) as b:
                    sp.wait_ge(v0_products_ready, b + 1)
                    sp.dma_start(x_b0[:].unsqueeze(1), x_cbn[:, bass.ds(b + 1, 1)]).then_inc(x_loaded, 16)
                sp.wait_ge(pool_setup, 16)
                sp.dma_start(b_hn_rows[0:3, :], b_hn_parts[:].rearrange("p w n -> p (w n)")).then_inc(b_hn_rows_ready, 16)
                with nc.Fori(0, B, engines=(mybir.EngineType.SP,)) as b:
                    sp.wait_ge(out_ready, b + 1)
                    sp.dma_start(out[:, bass.ds(b, 1), :], out_sb[:].unsqueeze(1)).then_inc(out_stored, 16)
                sp.wait_ge(out_stored, 16 * B)

            @block.tensor
            def _(pe):
                mm = nc.tensor.matmul
                pe.wait_ge(first_loaded, 16 * FIRST_LOADS)
                pe.wait_ge(ones_ready, 1)

                def l0_project(b, pair, w_sb, ready, i):
                    if i == 0 and w_sb is wq_sb:
                        at_least(pe, k_copied, b * 2 + pair)
                        if pair == 0:
                            at_least(pe, v0_lo_ready, b)
                            pe.wait_ge(x_loaded, (b + 1) * 16)
                    if i == 0 and w_sb is wk_sb:
                        pe.wait_ge(q_copied, b * 2 + pair + 1)
                    product = mm(bank[4][:, i * N:(i + 1) * N], w_sb[:, 2 * pair + i], x_b0[:], start=(i == 0), stop=True, skip_group_check=True)
                    if i == 1:
                        product.then_inc(ready, 1)

                def l0_project_v(b):
                    pe.wait_ge(k_copied, b * 2 + 2)
                    for kc in range(KC):
                        i = mm(bank[4][:, kc * T:kc * T + T], x_b0[:, kc * 128:kc * 128 + 128], wv_sb[:], start=(kc == 0), stop=True, skip_group_check=True)
                    i.then_inc(v0_products_ready, 1)

                def l0_pe_slot(b, parity, h):
                    n = b * HEADS + h
                    if h < HEADS:
                        if h % 8 == 0:
                            pe.wait_ge(q_stacked, b * 2 + h // 8 + 1)
                            pe.wait_ge(k_stacked, b * 2 + h // 8 + 1)
                        at_least(pe, probs0_ready, n + 1 - S0_DISTANCE[h])
                        rows = slice(32 * (h % 4), 32 * (h % 4) + 32)
                        for qc in range(KC):
                            i = mm(bank[S0_BANK[h]][:, qc * N:(qc + 1) * N], q_stack[rows, parity, h // 4, qc * 128:(qc + 1) * 128], k_stack[rows, parity, h // 4], start=(qc == 0), stop=True, skip_group_check=True)
                        i.then_inc(scores0_ready, 1)
                    if h == 0:
                        l0_project_v(b)
                    if not isinstance(n, int) or 4 <= n < B * HEADS + 4:
                        pe.wait_ge(probs0_ready, n - 3)
                        at_least(pe, probs0_t_lo_ready, n - 5)
                        for kc in range(KC):
                            for qc in range(KC):
                                i = nc.tensor.transpose(bank[2 + h % 2][:, kc * N + qc * 128:kc * N + qc * 128 + 128], probs0[:, h % 4, qc, kc * 128:kc * 128 + 128], identity[:])
                        i.then_inc(transposed0_ready, 1)
                    if not isinstance(n, int) or 6 <= n < B * HEADS + 6:
                        h_flat = (h - 6) % HEADS
                        vp = parity if h >= 6 else 1 - parity
                        bv = b if h >= 6 else b - 1
                        pe.wait_ge(probs0_t_lo_ready, n - 5)
                        if h_flat == 0:
                            pe.wait_ge(v0_lo_ready, bv + 1)
                            at_least(pe, y0_taken, bv)
                        for qc in range(KC):
                            for kc in range(KC):
                                for part in range(2):
                                    first, last = kc == 0 and part == 0, kc == KC - 1 and part == 1
                                    i = mm(bank[6 + qc][:, h_flat * V0:(h_flat + 1) * V0], probs0_t[:, (h - 6) % 4, part, kc, qc * 128:qc * 128 + 128],
                                           v_parts[:, vp, kc, h_flat], start=(h_flat == 0 and first), stop=last, skip_group_check=True)
                        i.then_inc(outputs0_ready, 1)
                    if not (isinstance(b, int) and b == B - 1):
                        for pair in range(2):
                            if h in (4 + 6 * pair, 5 + 6 * pair):
                                l0_project(b + 1, pair, wq_sb, q0_products_ready, h % 2)
                            if h in (7 + 6 * pair, 8 + 6 * pair):
                                l0_project(b + 1, pair, wk_sb, k0_products_ready, 1 - h % 2)

                for pair in range(2):
                    for i in range(2):
                        l0_project(0, pair, wq_sb, q0_products_ready, i)
                    for i in range(2):
                        l0_project(0, pair, wk_sb, k0_products_ready, i)
                l0_slots(mybir.EngineType.PE, l0_pe_slot)

                pe.wait_ge(weights_loaded, 16 * WEIGHT_LOADS)
                pe.wait_ge(y0_added, B)
                for j in range(4):
                    for k in range(KC):
                        i = mm(bank[6][:, j * B:(j + 1) * B], w_emb_sb[:, k, j * 128:(j + 1) * 128], cond_sb[:, k * B:(k + 1) * B], start=(j == 0 and k == 0), stop=(k == KC - 1), skip_group_check=True)
                i.then_inc(emb_ready, 1)
                pe.wait_ge(y0_added, B)

                def l1_input_products(c):
                    for j in range(6):
                        at_least(pe, gi_even_copied if j % 2 == 0 else gi_odd_copied, c * 3)
                        for k in range(KC):
                            i = mm(bank[j][:].rearrange("p (t b) -> p t b", b=B), w_ih_sb[:, k, j * 128:(j + 1) * 128], seq[:, bass.ds(c * 32 + 1, 32), k, :], start=(k == 0), stop=(k == KC - 1), skip_group_check=True)
                        i.then_inc(gi_ready, 1)

                l1_input_products(0)
                with nc.Fori(1, 4, engines=(mybir.EngineType.PE,)) as c:
                    l1_input_products(c)

                pe.wait_ge(splits_ready, 1)
                pe.wait_ge(gi_even_copied, 12)
                pe.wait_ge(gi_odd_copied, 12)
                def coupling(t, s, parts, src, first, last):
                    i = 0
                    n = len(parts)*4
                    for w in parts:
                        for m in range(2):
                            for k in range(2):
                                mm = nc.tensor.matmul(bank[s%2][:, m*16:m*16+16], coupling_parts[:, w, k, m*128:m*128+128], src[:, s%2, k*16:k*16+16],
                                    start = (first and i==0), stop=(last and i==n-1), skip_group_check=True)
                                i+=1
                    return mm

                def gru_products(dst, chunks, j0):
                    i = 0
                    for j in chunks:
                        for w in range(3):
                            for k in range(2):
                                mm = nc.tensor.matmul(dst[:, j-j0], w_hh_parts[:, w, k, j*128:j*128+128], h_split[:, k], start=(i==0), stop=(i==len(chunks)*6-1), skip_group_check=True)
                                i+=1
                    return mm

                def gru_gates(tau):
                    pe.wait_ge(h_split_ready, tau+1)
                    gru_products(gate_psum, range(4), 0).then_inc(gate_products_ready, 1)

                def gru_candidate(tau):
                    for j in range(2):
                        dst = cand_psum[:, j*16:j*16+16]
                        nc.tensor.matmul(dst, b_hn_rows[:, j*128:j*128+128], ones16[:], start=(j==0), stop=False, skip_group_check=True)
                        for w, half in ((0, 0), (1, 0), (2, 0), (0, 1), (1, 1)):
                            for k in range(2):
                                mm = nc.tensor.matmul(dst, w_hh_parts[:, w, k, (4+j)*128:(5+j)*128], h_split[:, k, half], start=False, stop=(j==1 and k==1 and w==1 and half==1), skip_group_check=True)
                    mm.then_inc(cand_products_ready, 1)

                def step(t, g):
                    for s in range(4):
                        pe.wait_ge(tanh_hi_ready, t*4+s+1)
                        coupling(t, s, (0, 1, 2), tanh_hi, True, False)
                        pe.wait_ge(tanh_lo_ready, t*4+s+1)
                        coupling(t, s, (0, 1), tanh_lo, False, True).then_inc(coupling_ready, 1)
                        if g and s==0: gru_gates(t+2)
                        if g and s==1: gru_candidate(t+2)
                pe.wait_ge(b_hn_rows_ready, 16)
                for tau in range(2):
                    gru_gates(tau)
                    gru_candidate(tau)
                for t in range(2): step(t, True)
                with nc.Fori(1, (T-2)//2, engines=(mybir.EngineType.PE,)) as t:
                    for i in range(2): step(t*2+i, True)
                step(T-2, False)
                step(T-1, False)
                pe.wait_ge(q_clipped_ready, T + 1)

                for g in range(T // 8):
                    if g % 4 == 0:
                        pe.wait_ge(squares_ready, g // 4 + 1)
                    for k in range(KC):
                        i = mm(bank[0][:, g:g + 1], sq3[:, k, 8 * g:8 * g + 8].rearrange("p t b -> p (t b)"), mean_ones[:, 0:1], start=(g == 0 and k == 0), stop=(k == KC - 1), skip_group_check=True)
                i.then_inc(mean_square_ready, 1)
                pe.wait_ge(rstd_ready, 1)
                nc.tensor.transpose(bank[1][0:T // 8, 0:128], rstd3[:], identity[:]).then_inc(rstd_transposed, 1)
                pe.wait_ge(rstd_rows_ready, 1)
                for g in range(T // 8):
                    i = mm(bank[2 + g // 4][:, (g % 4) * 128:(g % 4) * 128 + 128], select_sb[:, g], rstd_rows[:], start=(g % 4 == 0), stop=True, skip_group_check=True)
                    if g % 4 == 3:
                        i.then_inc(rstd_broadcast_ready, 1)
                pe.wait_ge(xg_ready, 1)

                def l3_project(b):
                    pe.wait_ge(xn_ready, b + 1)
                    at_least(pe, v3_copied, b)
                    for k in range(KC):
                        mm(bank[1][:], xn[:, k], w_qkv_sb[:, k, 0:2 * N], start=(k == 0), stop=(k == KC - 1), skip_group_check=True)
                    for k in range(KC):
                        i = mm(bank[0][:, 0:N], xn[:, k], w_qkv_sb[:, k, 2 * N:], start=(k == 0), stop=(k == KC - 1), skip_group_check=True)
                    i.then_inc(qkv3_ready, 1)

                def l3_head_rows(b):
                    pe.wait_ge(qk3_ready, b + 1)
                    at_least(pe, q3_copied, b)
                    at_least(pe, k3_copied, b)
                    for w in range(2):
                        for g in range(GROUPS):
                            i = nc.tensor.transpose(bank[2 + w][:, g * T:(g + 1) * T], qk_pad[:, w, 4 * g:4 * g + 4].rearrange("p h d -> p (h d)"), identity[:])
                        i.then_inc(head_rows_transposed, 1)

                def l3_scores(b, g):
                    at_least(pe, probs3_ready, b * GROUPS + (1 if g == 3 else 0))
                    rows = slice(32 * g, 32 * g + 32)
                    for j in range(4):
                        for part in range(2):
                            i = mm(bank[S3_BANK[g]][:, j * T:(j + 1) * T], q3_stack[rows, j], k3_parts[rows, part, j], start=(j == 0 and part == 0), stop=(part == 1), skip_group_check=True)
                    i.then_inc(scores3_ready, 1)

                def l3_transposes(b, g):
                    pe.wait_ge(probs3_ready, b * GROUPS + g + 1)
                    at_least(pe, probs3_t_lo_ready, b * GROUPS + g - 1)
                    if g == 0:
                        at_least(pe, out_ready, b)
                    for j in range(4):
                        i = nc.tensor.transpose(bank[(6, 2)[g % 2]][:, j * T:(j + 1) * T], probs3[:, g, j], identity[:])
                    i.then_inc(transposed3_ready, 1)

                def l3_values(b, g):
                    pe.wait_ge(probs3_t_lo_ready, b * GROUPS + g + 1)
                    if g == 0:
                        pe.wait_ge(v3_copied, b + 1)
                        at_least(pe, o_ready, b)
                    for j in range(4):
                        h = 4 * j + g
                        for part in range(2):
                            for w in range(2):
                                i = mm(bank[7][:, h * V3:(h + 1) * V3], probs3_t[:, g % 2, part, j], v3_parts[:, w, h], start=(h == 0 and part == 0 and w == 0), stop=(part == 1 and w == 1), skip_group_check=True)
                    i.then_inc(outputs3_ready, 1)

                def l3_pe_body(b):
                    pe.wait_ge(q3_copied, b + 1)
                    pe.wait_ge(k3_copied, b + 1)
                    l3_scores(b, 0)
                    l3_scores(b, 1)
                    l3_scores(b, 2)
                    if has_next(b):
                        l3_project(b + 1)
                    l3_scores(b, 3)
                    l3_transposes(b, 0)
                    l3_transposes(b, 1)
                    l3_transposes(b, 2)
                    l3_values(b, 0)
                    l3_transposes(b, 3)
                    l3_values(b, 1)
                    l3_values(b, 2)
                    l3_values(b, 3)
                    if has_next(b):
                        l3_head_rows(b + 1)
                    if has_next(b):
                        pe.wait_ge(v3_copied, b + 2)
                    pe.wait_ge(o_ready, b + 1)
                    for k in range(KC):
                        i = nc.tensor.transpose(bank[0][:, k * 128:(k + 1) * 128], o_sb[:, k * 128:(k + 1) * 128], identity[:])
                    i.then_inc(o_transposed, 1)
                    pe.wait_ge(x3_taken, b + 1)
                    for k in range(KC):
                        mm(bank[6][:, k * 128:(k + 1) * 128], x3_b[:, k], identity[:], start=(k == 0), stop=False, skip_group_check=True)
                    pe.wait_ge(o_t_ready, b + 1)
                    for k in range(KC):
                        i = mm(bank[6][:, 0:N], o_t[:, k], w_out_sb[:, k], start=False, stop=(k == KC - 1), skip_group_check=True)
                    i.then_inc(final_ready, 1)

                l3_project(0)
                l3_head_rows(0)
                l3_batches(mybir.EngineType.PE, l3_pe_body)

            @block.scalar
            def _(act):
                def l0_prepare_q(b, pair):
                    pe_count = b * 2 + pair
                    act.wait_ge(q0_products_ready, pe_count + 1)
                    at_least(act, q_stacked, pe_count)
                    nc.scalar.activation(q_full[:], bank[4][:], ACT.Identity, scale=1.0 / float(np.sqrt(D0)), bias=row_consts[:, 0:1])
                    nc.scalar.activation(q_hi_part[:], bank[4][:], ACT.Identity, scale=row_consts[:, 1:2], bias=row_consts[:, 2:3]).then_inc(q_copied, 1)

                def l0_prepare_k(b, pair):
                    act.wait_ge(k_copied, b * 2 + pair + 1)
                    at_least(act, k_stacked, b * 2 + pair)
                    nc.scalar.activation(k_hi_part[:], k_full[:], ACT.Copy, scale=row_consts[:, 3:4]).then_inc(k_hi_ready, 1)

                def l0_prepare_v(b, parity):
                    act.wait_ge(v0_products_ready, b + 1)
                    at_least(act, outputs0_ready, (b - 1) * HEADS)
                    for kc in range(KC):
                        i = nc.scalar.activation(v_parts[:, parity, kc, :, 0:D0], bank[4][:, kc * T:(kc + 1) * T].rearrange("p (h d) -> p h d", d=D0), ACT.Copy)
                    i.then_inc(v0_hi_ready, 1)

                def l0_act_slot(b, parity, h):
                    n = b * HEADS + h
                    if h < HEADS:
                        act.wait_ge(max0_ready, n + 1)
                        at_least(act, transposed0_ready, n - 3)
                        for qc in range(KC):
                            i = nc.scalar.activation(probs0[:, h % 4, qc], bank[S0_BANK[h]][:, qc * N:(qc + 1) * N], ACT.Exp, bias=negmax0[:, h % 4, qc:qc + 1])
                        i.then_inc(probs0_ready, 1)
                    if h == 0:
                        l0_prepare_v(b, parity)
                    if not isinstance(n, int) or 4 <= n < B * HEADS + 4:
                        act.wait_ge(transposed0_ready, n - 3)
                        at_least(act, outputs0_ready, n - 7)
                        nc.scalar.activation(probs0_t[:, h % 4, 0].rearrange("p c k -> p (c k)"), bank[2 + h % 2][:], ACT.Copy).then_inc(probs0_t_hi_ready, 1)
                    if not (isinstance(b, int) and b == B - 1):
                        if h in (5, 11):
                            l0_prepare_q(b + 1, h // 11)
                        if h in (9, 15):
                            l0_prepare_k(b + 1, h // 15)

                act.wait_ge(first_loaded, 16 * FIRST_LOADS)
                for pair in range(2):
                    l0_prepare_q(0, pair)
                    l0_prepare_k(0, pair)
                l0_slots(mybir.EngineType.Activation, l0_act_slot)

                act.wait_ge(gate_bias_ready, 1)
                with nc.Fori(0, 4, engines=(mybir.EngineType.Activation,)) as c:
                    for j in (0, 2, 4):
                        act.wait_ge(gi_ready, c * 6 + j + 1)
                        nc.scalar.activation(gi4[:, bass.ds(c * 32, 32), j, :], bank[j][:].rearrange("p (t b) -> p t b", b=B), ACT.Identity, bias=gate_bias[:, j:j + 1]).then_inc(gi_even_copied, 1)

                activation = nc.scalar.activation

                def gates(tau):
                    act.wait_ge(gate_sum_ready, tau+1)
                    activation(gate_tanh[:], gate_sum[:, 1], ACT.Tanh, scale=0.5).then_inc(gate_tanh_ready, 1)

                def minus_z(tau):
                    act.wait_ge(gate_tanh_ready, tau+1)
                    activation(one_minus_z[:], gate_tanh[:, 32:64], ACT.Copy, scale=-0.5, bias=0.5).then_inc(one_minus_z_ready, 1)

                def candidate(tau):
                    act.wait_ge(cand_in_ready, tau+1)
                    activation(cand_tile[:], cand_in[:], ACT.Tanh).then_inc(cand_ready, 1)

                def h_high(tau):
                    act.wait_ge(h_ready, tau+2)
                    activation(h_split[:, :, 0, :], h_tile[:], ACT.Copy).then_inc(h_hi_ready, 1)

                def scale_drive(t):
                    act.wait_ge(drive_ready, t+1)
                    for i, c in enumerate((a[0], a[2], a[3])):
                        x = activation(drive_scaled[:, i], drive[:], ACT.Copy, scale=c)
                    x.then_inc(drive_scaled_ready, 1)

                def step(t, g, prep):
                    for s in range(4):
                        act.wait_ge(q_psum_ready, t*4+s+1)
                        activation(tanh_hi[:, s%2], q_psum(s), ACT.Tanh).then_inc(tanh_hi_ready, 1)
                        activation(tanh_full[:, s%2], q_psum(s), ACT.Tanh).then_inc(tanh_full_ready, 1)
                        if s==0:
                            if g: h_high(t+1)
                            act.wait_ge(q_clipped_ready, t+1)
                            qv = q_clipped[:]
                        else: qv=q_psum(s)
                        activation(q_squared[:, s%2], qv, ACT.Square).then_inc(q_squared_ready, 1)
                        if s==0:
                            act.wait_ge(p_state_ready, t+1)
                            activation(p_scaled[:, 1], p_state[:], ACT.Copy, scale=stage_rows[1][0]).then_inc(p_scaled_ready, 1)
                            activation(p_scaled[:, 2], p_state[:], ACT.Copy, scale=stage_rows[2][0])
                            activation(p_scaled[:, 3], p_state[:], ACT.Copy, scale=stage_rows[3][0]).then_inc(p_scaled_ready, 1)
                            activation(p_scaled[:, 4], p_state[:], ACT.Copy, scale=p_row[0])
                        if s==3 and g: candidate(t+2)
                        activation(p_term[:, s], qv, ACT.Copy, scale=p_row[s+1]).then_inc(p_term_ready, 1)
                        if s==2 and g:
                            gates(t+2)
                            minus_z(t+2)
                        if s==3 and prep: scale_drive(t+1)
                act.wait_ge(gru_start_ready, 1)
                for tau in range(2):
                    h_high(tau-1)
                    gates(tau)
                    minus_z(tau)
                    candidate(tau)
                scale_drive(0)
                for t in range(2): step(t, True, True)
                with nc.Fori(1, (T-2)//2, engines=(mybir.EngineType.Activation,)) as t:
                    for i in range(2): step(t*2+i, True, True)
                step(T-2, False, True)
                step(T-1, False, False)
                act.wait_ge(rstd_transposed, 1)
                nc.scalar.activation(rstd_rows[:], bank[1][0:T // 8, 0:128], ACT.Copy).then_inc(rstd_rows_ready, 1)

                def l3_norm(b):
                    act.wait_ge(xg_ready, 1)
                    at_least(act, qkv3_ready, b)
                    for k in range(KC):
                        i = nc.scalar.activation(xn[:, k], xg[:, :, k, bass.ds(b, 1)].rearrange("p t o -> p (t o)"), ACT.Identity, scale=gain_shift[:, k, bass.ds(b, 1)], bias=gain_shift[:, 2 + k, bass.ds(b, 1)])
                    i.then_inc(xn_ready, 1)

                def l3_squares(b):
                    act.wait_ge(qkv3_ready, b + 1)
                    at_least(act, qk_sum_ready, b)
                    nc.scalar.activation(qk_sq[:].rearrange("p w h d -> p (w h d)"), bank[1][:], ACT.Square).then_inc(qk_sq_ready, 1)

                def l3_copy_v(b):
                    act.wait_ge(qkv3_ready, b + 1)
                    act.wait_ge(qk_g_ready, b + 1)
                    at_least(act, outputs3_ready, b * GROUPS)
                    nc.scalar.activation(v3_parts[:, 0, :, 0:D3], bank[0][:, 0:N].rearrange("p (h d) -> p h d", d=D3), ACT.Copy).then_inc(v3_hi_ready, 1)

                def l3_row_highs(b):
                    act.wait_ge(head_rows_transposed, 2 * b + 1)
                    nc.scalar.activation(q3_hi_part[:].rearrange("p g t -> p (g t)"), bank[2][:], ACT.Copy, scale=row_consts[:, 8:9]).then_inc(q3_hi_ready, 1)
                    act.wait_ge(head_rows_transposed, 2 * b + 2)
                    nc.scalar.activation(k3_parts[:, 0].rearrange("p g t -> p (g t)"), bank[3][:], ACT.Copy, scale=float(D3 ** -0.5)).then_inc(k3_hi_ready, 1)

                def l3_exponentials(b, g):
                    n = b * GROUPS + g
                    act.wait_ge(max3_ready, n + 1)
                    at_least(act, transposed3_ready, n - 3)
                    for j in range(4):
                        i = nc.scalar.activation(probs3[:, g, j], bank[S3_BANK[g]][:, j * T:(j + 1) * T], ACT.Exp, bias=negmax3[:, g, j:j + 1])
                    i.then_inc(probs3_ready, 1)

                def l3_prob_highs(b, g):
                    n = b * GROUPS + g
                    act.wait_ge(transposed3_ready, n + 1)
                    at_least(act, outputs3_ready, n - 1)
                    nc.scalar.activation(probs3_t[:, g % 2, 0].rearrange("p j t -> p (j t)"), bank[(6, 2)[g % 2]][:], ACT.Copy).then_inc(probs3_t_hi_ready, 1)

                def l3_act_body(b):
                    if has_next(b):
                        l3_norm(b + 1)
                    l3_exponentials(b, 0)
                    l3_exponentials(b, 1)
                    if has_next(b):
                        l3_squares(b + 1)
                    l3_exponentials(b, 2)
                    l3_prob_highs(b, 0)
                    l3_exponentials(b, 3)
                    l3_prob_highs(b, 1)
                    l3_prob_highs(b, 2)
                    l3_prob_highs(b, 3)
                    if has_next(b):
                        l3_copy_v(b + 1)
                        l3_row_highs(b + 1)
                    act.wait_ge(o_transposed, b + 1)
                    nc.scalar.activation(o_t[:].rearrange("p k t -> p (k t)"), bank[0][:, 0:N], ACT.Copy).then_inc(o_t_ready, 1)

                l3_norm(0)
                l3_squares(0)
                l3_copy_v(0)
                l3_row_highs(0)
                l3_batches(mybir.EngineType.Activation, l3_act_body)

            @block.gpsimd
            def _(pool):
                nc.gpsimd.memset(v_parts[:, :, :, :, 2 * D0:], 1.0).then_inc(ones_ready, 1)
                def l0_stack(b, parity):
                    for pair in range(2):
                        for full, hi_part, stack, ready, stacked in ((q_full, q_hi_part, q_stack, q_copied, q_stacked), (k_full, k_hi_part, k_stack, k_hi_ready, k_stacked)):
                            pool.wait_ge(ready, b * 2 + pair + 1)
                            at_least(pool, scores0_ready, (b - 1) * HEADS)
                            nc.gpsimd.tensor_tensor(stack[:, parity, 2 * pair:2 * pair + 2].rearrange("p g n -> p (g n)"), full[:], hi_part[:], ALU.subtract).then_inc(stacked, 1)

                l0_stack(0, 0)
                l0_stack(1, 1)
                with nc.Fori(0, B // 2 - 1, engines=(mybir.EngineType.Pool,)) as u:
                    for half in range(2):
                        l0_stack(u * 2 + 2 + half, half)
                pool.wait_ge(weights_loaded, 16 * WEIGHT_LOADS)
                nc.gpsimd.tensor_tensor(gate_bias[:, 0:4], b_ih_sb[:, 0:4], b_hh_sb[:, 0:4], ALU.add)
                nc.gpsimd.tensor_copy(gate_bias[:, 4:6], b_ih_sb[:, 4:6]).then_inc(gate_bias_ready, 1)
                nc.gpsimd.memset(SEQ[:, 0:SLOT], 0.0)
                nc.gpsimd.memset(ones16[:], 1.0)
                nc.gpsimd.memset(b_hn_rows[:], 0.0)
                nc.gpsimd.memset(mean_ones[:], 1.0 / N)
                nc.gpsimd.memset(v3_parts[:, 0, :, D3:], 1.0)
                nc.gpsimd.memset(v3_parts[:, 1, :, D3:], 0.0)
                nc.gpsimd.memset(minus_half[:], -0.5).then_inc(pool_setup, 1)
                pool.wait_ge(pool_setup, 1)
                done = 1
                for source, parts in ((w_hh_sb, w_hh_parts), (coupling_sb, coupling_parts), (b_hn_sb, b_hn_parts)):
                    for w in range(3):
                        part = parts[:, w]
                        nc.gpsimd.tensor_copy(part, source[:]).then_inc(pool_setup, 1)
                        done += 1
                        pool.wait_ge(pool_setup, done)
                        if w < 2:
                            nc.gpsimd.tensor_tensor(source[:], source[:], part, ALU.subtract).then_inc(pool_setup, 1)
                            done += 1
                            pool.wait_ge(pool_setup, done)
                nc.gpsimd.tensor_scalar(bias_sb[:], bias_sb[:], P_SHIFT, None, ALU.subtract)
                pool.wait_ge(first_loaded, 16 * FIRST_LOADS)
                for k in range(KC):
                    diagonal = w_out_sb[:, k, k * 128:(k + 1) * 128]
                    i = nc.gpsimd.tensor_tensor(diagonal, diagonal, identity[:], ALU.add)
                i.then_inc(splits_ready, 1)
                pool.wait_ge(y0_added, B)
                pool.wait_ge(gi_ready, 24)

                tensor_tensor = nc.gpsimd.tensor_tensor

                def slot(t):
                    return SEQ[:, bass.ds((t+1)*32, 32)]

                def h_low(tau):
                    pool.wait_ge(h_hi_ready, tau+2)
                    tensor_tensor(h_split[:, :, 1, :], h_tile[:], h_split[:, :, 0, :], ALU.subtract).then_inc(h_split_ready, 1)

                def add_candidate(tau):
                    pool.wait_ge(one_minus_z_ready, tau+1)
                    pool.wait_ge(cand_ready, tau+1)
                    tensor_tensor(new_part[:], cand_tile[:], one_minus_z[:], ALU.mult).then_inc(new_part_ready, 1)

                def add_h(tau):
                    tensor_tensor(slot(tau), slot(tau), h_tile[:], ALU.add).then_inc(x2_ready, 1)

                def make_drive(t):
                    tensor_tensor(drive[:], slot(t), bias_sb[:], ALU.add).then_inc(drive_ready, 1)

                def step(t, g, prep):
                    for s in range(4):
                        if s==3 and g: add_candidate(t+2)
                        if s==0:
                            if g: h_low(t+1)
                            pool.wait_ge(p_scaled_ready, t*2+1)
                            tensor_tensor(linear_start[:, 1], p_scaled[:, 1], drive_scaled[:, 0], ALU.add).then_inc(start1_ready, 1)
                            pool.wait_ge(p_scaled_ready, t*2+2)
                            tensor_tensor(linear_start[:, 2], p_scaled[:, 2], drive_scaled[:, 1], ALU.add)
                            tensor_tensor(linear_start[:, 3], p_scaled[:, 3], drive_scaled[:, 2], ALU.add).then_inc(start23_ready, 1)
                        pool.wait_ge(p_term_ready, t*4+s+1)
                        if s>0: pool.wait_ge(p_sum_ready, t*4+s)
                        if s==2 and prep: pool.wait_ge(x2_ready, t+2)
                        tensor_tensor(p_sum[:, s], (p_scaled[:, 4] if s==0 else p_sum[:, s-1]), p_term[:, s], ALU.add).then_inc(p_sum_ready, 1)
                        if s==1:
                            if prep: add_h(t+1)
                        if s==2:
                            if prep: make_drive(t+1)
                            tensor_tensor(slot(t-1), slot(t-1), q_clipped[:], ALU.add).then_inc(x3_ready, 1)
                h_low(-1)
                add_candidate(0)
                h_low(0)
                add_h(0)
                add_candidate(1)
                pool.wait_ge(x2_ready, 1)
                make_drive(0)
                for t in range(2): step(t, True, True)
                with nc.Fori(1, (T-2)//2, engines=(mybir.EngineType.Pool,)) as t:
                    for i in range(2): step(t*2+i, True, True)
                step(T-2, False, True)
                step(T-1, False, False)
                pool.wait_ge(q_clipped_ready, T+1)
                tensor_tensor(slot(T-1), slot(T-1), q_clipped[:], ALU.add).then_inc(x3_ready, 1)
                pool.wait_ge(mean_eps_ready, 1)
                nc.gpsimd.tensor_tensor(rstd3[:], mean_eps[:], minus_half[:, 0:T // 8], ALU.pow).then_inc(rstd_ready, 1)

                def l3_head_norms(b):
                    pool.wait_ge(qk_mean_ready, b + 1)
                    nc.gpsimd.tensor_tensor(qk_rstd[:].rearrange("p w h -> p (w h)"), qk_mean[:].rearrange("p w h -> p (w h)"), minus_half[:, 0:2 * HEADS], ALU.pow).then_inc(qk_rstd_ready, 1)

                def l3_pool_body(b):
                    at_least(pool, final_ready, b)
                    pool.wait_ge(x3_ready, T + 1)
                    nc.gpsimd.tensor_copy(x3_b[:], seq[:, 1:, :, bass.ds(b, 1)].rearrange("p t k o -> p k (t o)")).then_inc(x3_taken, 1)
                    if has_next(b):
                        l3_head_norms(b + 1)

                l3_head_norms(0)
                l3_batches(mybir.EngineType.Pool, l3_pool_body)

            @block.vector
            def _(dve):
                dve.wait_ge(first_loaded, 16 * FIRST_LOADS)
                nc.vector.tensor_scalar(k_const[:], b0_sb[:], row_consts[:, 4:5], row_consts[:, 5:6], ALU.mult, ALU.add).then_inc(dve_setup, 1)
                dve.wait_ge(mask_loaded, 64)
                for b in range(4):
                    i = nc.vector.tensor_scalar(mask_rows[:, 4 * b:4 * b + 4], mask_rows[:, 4 * b:4 * b + 4], row_consts[:, 6:7], row_consts[:, 7:8], ALU.mult, ALU.add)
                i.then_inc(dve_setup, 1)
                dve.wait_ge(dve_setup, 2)

                def l0_mask_k(b, pair):
                    dve.wait_ge(k0_products_ready, b * 2 + pair + 1)
                    at_least(dve, k_stacked, b * 2 + pair)
                    nc.vector.scalar_tensor_tensor(out=k_full[:].rearrange("p (g n) -> p g n", g=2), in0=bank[4][:].rearrange("p (g n) -> p g n", g=2), scalar=k_const[:],
                                                   in1 = mask_rows[:, bass.ds(b, 1), :].broadcast_to([128, 2, N]), op0=ALU.add, op1=ALU.mult).then_inc(k_copied, 1)

                def l0_value_lows(b, parity):
                    dve.wait_ge(v0_hi_ready, b + 1)
                    for kc in range(KC):
                        i = nc.vector.tensor_tensor(v_parts[:, parity, kc, :, D0:2 * D0], bank[4][:, kc * T:(kc + 1) * T].rearrange("p (h d) -> p h d", d=D0), v_parts[:, parity, kc, :, 0:D0], ALU.subtract)
                    i.then_inc(v0_lo_ready, 1)

                def l0_take(b):
                    dve.wait_ge(outputs0_ready, (b + 1) * HEADS)
                    at_least(dve, y0_added, b)
                    for qc in range(KC):
                        out_cols = bank[6 + qc][:, 0:HEADS * V0].rearrange("p (h v) -> p h v", v=V0)
                        nc.vector.reciprocal(rsum0[:, qc], out_cols[:, :, 2 * D0])
                        i = nc.vector.tensor_reduce(y_sum[:, qc], out_cols[:, :, 0:2 * D0].rearrange("p h (w d) -> p h d w", w=2), AXIS_X, ALU.add)
                    i.then_inc(y0_taken, 1)

                def l0_add(b):
                    dve.wait_ge(y0_taken, b + 1)
                    nc.vector.tensor_tensor(y_sb[:].rearrange("p c (h d) -> p (c h) d", d=D0), y_sum[:].rearrange("p c h d -> p (c h) d"),
                                            rsum0[:].rearrange("p c h -> p (c h)").unsqueeze(2).broadcast_to([128, KC * HEADS, D0]), ALU.mult).then_inc(y0_scaled, 1)
                    dve.wait_ge(y0_scaled, b + 1)
                    dve.wait_ge(seq_loaded, 16)
                    x_b = seq[:, 1:, :, bass.ds(b, 1)].rearrange("p t k o -> p k (t o)")
                    nc.vector.tensor_tensor(x_b, x_b, y_sb[:], ALU.add).then_inc(y0_added, 1)

                def l0_dve_slot(b, parity, h):
                    n = b * HEADS + h
                    if h < HEADS:
                        dve.wait_ge(scores0_ready, n + 1)
                        nc.vector.tensor_reduce(negmax0[:, h % 4], bank[S0_BANK[h]][:].rearrange("p (c k) -> p c k", c=KC), AXIS_X, ALU.max, negate=True).then_inc(max0_ready, 1)
                    if h == 1:
                        l0_value_lows(b, parity)
                    if h % HEADS == 6 and not (isinstance(n, int) and n == 6):
                        l0_take(b - 1 if h < HEADS else b)
                    if not isinstance(n, int) or 5 <= n < B * HEADS + 5:
                        dve.wait_ge(probs0_t_hi_ready, n - 4)
                        m = (h - 5) % 4
                        nc.vector.tensor_tensor(probs0_t[:, m, 1].rearrange("p c k -> p (c k)"), bank[2 + m % 2][:], probs0_t[:, m, 0].rearrange("p c k -> p (c k)"), ALU.subtract).then_inc(probs0_t_lo_ready, 1)
                    if h == 7 and not (isinstance(b, int) and b == 0):
                        l0_add(b - 1)
                    if h == HEADS + 6:
                        l0_add(b)
                    if not (isinstance(b, int) and b == B - 1):
                        if h in (8, 14):
                            l0_mask_k(b + 1, h // 14)

                for pair in range(2):
                    l0_mask_k(0, pair)
                l0_slots(mybir.EngineType.DVE, l0_dve_slot)

                dve.wait_ge(weights_loaded, 16 * WEIGHT_LOADS)
                dve.wait_ge(emb_ready, 1)
                nc.vector.tensor_scalar(b_emb1[:], b_emb_sb[:], 1.0, None, ALU.add).then_inc(dve_setup, 1)
                dve.wait_ge(dve_setup, 3)
                for j in range(4):
                    if j < 2:
                        i = nc.vector.tensor_scalar(gain_shift[:, j], bank[6][:, j * B:(j + 1) * B], b_emb1[:, j:j + 1], g_norm_sb[:, j:j + 1], ALU.add, ALU.mult)
                    else:
                        i = nc.vector.tensor_scalar(gain_shift[:, j], bank[6][:, j * B:(j + 1) * B], b_emb_sb[:, j:j + 1], None, ALU.add)
                i.then_inc(dve_setup, 1)
                dve.wait_ge(gate_bias_ready, 1)
                with nc.Fori(0, 4, engines=(mybir.EngineType.DVE,)) as c:
                    for j in (1, 3, 5):
                        dve.wait_ge(gi_ready, c * 6 + j + 1)
                        nc.vector.tensor_scalar(gi4[:, bass.ds(c * 32, 32), j, :], bank[j][:].rearrange("p (t b) -> p t b", b=B), gate_bias[:, j:j + 1], None, ALU.add).then_inc(gi_odd_copied, 1)

                V=nc.vector
                stt = lambda o, i0, sc, i1, op0=ALU.mult, op1=ALU.add: V.scalar_tensor_tensor(out=o, in0=i0, scalar=sc, in1=i1, op0=op0, op1=op1)

                def input_products(tau, j0, n): return GI[:, bass.ds(tau*96+j0*16, n*16)]

                def gates_high(tau):
                    dve.wait_ge(gate_products_ready, tau+1)
                    V.tensor_tensor(gate_sum[:, 0].rearrange("p (j b) -> p j b", b=16), gate_psum[:, :, 0, :], input_products(tau, 0, 4).rearrange("p (j b) -> p j b", b=16), ALU.add).then_inc(gate_sum_hi_ready, 1)

                def gates_low(tau):
                    dve.wait_ge(gate_sum_hi_ready, tau+1)
                    V.tensor_tensor(gate_sum[:, 1].rearrange("p (j b) -> p j b", b=16), gate_psum[:, :, 1, :], gate_sum[:, 0].rearrange("p (j b) -> p j b", b=16), ALU.add).then_inc(gate_sum_ready, 1)

                def times_reset(tau):
                    dve.wait_ge(cand_products_ready, tau+1)
                    dve.wait_ge(gate_tanh_ready, tau+1)
                    stt(reset_times[:], gate_tanh[:, 0:32], 1.0, cand_psum, ALU.add, ALU.mult).then_inc(reset_times_ready, 1)

                def candidate_input(tau):
                    dve.wait_ge(reset_times_ready, tau+1)
                    stt(cand_in[:], reset_times[:], 0.5, input_products(tau, 4, 2)).then_inc(cand_in_ready, 1)
                h_flat = h_tile[:].rearrange("p k b -> p (k b)")

                def keep_part(tau):
                    stt(kept_part[:], gate_tanh[:, 32:64], 1.0, h_flat, ALU.add, ALU.mult).then_inc(kept_part_ready, 1)

                def new_h(tau, first=False):
                    dve.wait_ge(kept_part_ready, tau+1)
                    dve.wait_ge(new_part_ready, tau+1)
                    if not first: dve.wait_ge(x2_ready, tau)
                    stt(h_flat, kept_part[:], 0.5, new_part[:]).then_inc(h_ready, 1)

                def start_stage0(t):
                    dve.wait_ge(p_state_ready, t+1)
                    dve.wait_ge(drive_scaled_ready, t+1)
                    stt(linear_start[:, 0], p_state[:], stage_rows[0][0], drive_scaled[:, 0]).then_inc(start0_ready, 1)

                def step(t, g, prep):
                    def tanh_low(s):
                        dve.wait_ge(tanh_full_ready, t*4+s+1)
                        V.tensor_tensor(tanh_lo[:, s%2], tanh_full[:, s%2], tanh_hi[:, s%2], ALU.subtract).then_inc(tanh_lo_ready, 1)
                    def make_stage_base(s):
                        dve.wait_ge((start0_ready, linear1_ready, linear2_ready, linear3_ready)[s], t+1)
                        dve.wait_ge(cubic_ready, t*4+s+1)
                        stt(stage_base[:, s%2], cubic[:, s%2], -a[s]/3, linear[:, s] if s else linear_start[:, 0]).then_inc(stage_base_ready, 1)
                    def cubic_term(s):
                        dve.wait_ge(q_squared_ready, t*4+s+1)
                        if s: dve.wait_ge(q_state_ready, t*4+s+1)
                        else: dve.wait_ge(q_clipped_ready, t+1)
                        stt(cubic[:, s%2], q_squared[:, s%2], -3*stage_rows[s][s+1]/a[s], (q_clipped[:] if s==0 else q_state[:, s]), ALU.add, ALU.mult).then_inc(cubic_ready, 1)
                    def update_q(s):
                        dve.wait_ge(stage_base_ready, t*4+s+1)
                        dve.wait_ge(coupling_ready, t*4+s+1)
                        stt(q_psum(s+1), coupling_sum(s), a[s], stage_base[:, s%2]).then_inc(q_psum_ready, 1)
                        stt(q_state[:, (s+1)%4], coupling_sum(s), a[s], stage_base[:, s%2]).then_inc(q_state_ready, 1)
                    def add_linear(j, i, src):
                        return stt(linear[:, j], q_clipped[:] if i==0 else q_state[:, i], stage_rows[j][i+1], src[:, j])
                    dve.wait_ge(p_sum_ready, t*4)
                    V.tensor_scalar(p_state[:], p_sum[:, 3], CLAMP - P_SHIFT, -CLAMP - P_SHIFT, ALU.min, ALU.max).then_inc(p_state_ready, 1)
                    dve.wait_ge(x3_ready, t)
                    dve.wait_ge(q_state_ready, t*4+1)
                    V.tensor_scalar(q_clipped[:], q_state[:, 0], CLAMP, -CLAMP, ALU.min, ALU.max).then_inc(q_clipped_ready, 1)
                    start_stage0(t)
                    tanh_low(0)
                    cubic_term(0)
                    make_stage_base(0)
                    update_q(0)
                    dve.wait_ge(start1_ready, t+1)
                    add_linear(1, 0, linear_start).then_inc(linear1_ready, 1)
                    tanh_low(1)
                    cubic_term(1)
                    dve.wait_ge(start23_ready, t+1)
                    add_linear(2, 0, linear_start).then_inc(linear2_q0_ready, 1)
                    make_stage_base(1)
                    add_linear(3, 0, linear_start).then_inc(linear3_q0_ready, 1)
                    update_q(1)
                    if g: gates_high(t+2)
                    dve.wait_ge(linear2_q0_ready, t+1)
                    add_linear(2, 1, linear).then_inc(linear2_ready, 1)
                    tanh_low(2)
                    if g: gates_low(t+2)
                    cubic_term(2)
                    dve.wait_ge(linear3_q0_ready, t+1)
                    add_linear(3, 1, linear).then_inc(linear3_q1_ready, 1)
                    make_stage_base(2)
                    if g: times_reset(t+2)
                    update_q(2)
                    if g: candidate_input(t+2)
                    dve.wait_ge(linear3_q1_ready, t+1)
                    add_linear(3, 2, linear).then_inc(linear3_ready, 1)
                    if g: keep_part(t+2)
                    tanh_low(3)
                    cubic_term(3)
                    make_stage_base(3)
                    if g: new_h(t+2)
                    update_q(3)
                dve.wait_ge(gi_even_copied, 12)
                dve.wait_ge(gi_odd_copied, 12)
                V.tensor_copy(q_psum(0), cond_sb[:])
                V.tensor_scalar(p_sum[:, 3], cond_sb[:], P_SHIFT, None, ALU.subtract)
                V.tensor_copy(q_state[:, 0], cond_sb[:]).then_inc(q_state_ready, 1)
                V.tensor_copy(h_flat, cond_sb[:]).then_inc(h_ready, 1)
                dve.wait_ge(h_ready, 1)
                V.tensor_copy(start_marks[:, 0:1], cond_sb[:, 0:1]).then_inc(gru_start_ready, 1)
                V.tensor_copy(start_marks[:, 1:2], cond_sb[:, 0:1]).then_inc(q_psum_ready, 1)
                for tau in range(2):
                    gates_high(tau)
                    gates_low(tau)
                    times_reset(tau)
                    candidate_input(tau)
                    keep_part(tau)
                    new_h(tau, tau==0)
                for t in range(14): step(t, True, True)
                with nc.Fori(1, (T-2)//14, engines=(mybir.EngineType.DVE,)) as t:
                    for i in range(14): step(t*14+i, True, True)
                step(T-2, False, True)
                step(T-1, False, False)
                dve.wait_ge(x3_ready, T)
                dve.wait_ge(q_state_ready, 4*T+1)
                V.tensor_scalar(q_clipped[:], q_state[:, 0], CLAMP, -CLAMP, ALU.min, ALU.max).then_inc(q_clipped_ready, 1)
                dve.wait_ge(x3_ready, T + 1)
                for c in range(4):
                    part = seq[:, 1 + 32 * c:33 + 32 * c]
                    nc.vector.tensor_tensor(sq3[:, :, 32 * c:32 * c + 32].rearrange("p k t b -> p t k b"), part, part, ALU.mult).then_inc(squares_ready, 1)
                dve.wait_ge(mean_square_ready, 1)
                nc.vector.tensor_scalar(mean_eps[:], bank[0][:, 0:T // 8], EPS, None, ALU.add).then_inc(mean_eps_ready, 1)
                for c in range(4):
                    dve.wait_ge(rstd_broadcast_ready, c + 1)
                    for k in range(KC):
                        i = nc.vector.tensor_tensor(xg[:, 32 * c:32 * c + 32, k], seq[:, 1 + 32 * c:33 + 32 * c, k], bank[2 + c][:].rearrange("p (t b) -> p t b", b=B), ALU.mult)
                i.then_inc(xg_ready, 1)

                def l3_head_means(b):
                    dve.wait_ge(qk_sq_ready, b + 1)
                    nc.vector.tensor_reduce(qk_sum[:].rearrange("p w h -> p (w h)"), qk_sq[:].rearrange("p w h d -> p (w h) d"), AXIS_X, ALU.add).then_inc(qk_sum_ready, 1)
                    dve.wait_ge(qk_sum_ready, b + 1)
                    nc.vector.tensor_scalar(qk_mean[:], qk_sum[:], 1.0 / D3, EPS, ALU.mult, ALU.add).then_inc(qk_mean_ready, 1)

                def l3_head_gain(b):
                    dve.wait_ge(qk_sq_ready, b + 1)
                    at_least(dve, qk3_ready, b)
                    nc.vector.tensor_tensor(qk_g[:].rearrange("p w h d -> p (w h d)"), bank[1][:], g_qk_sb[:].rearrange("p w h d -> p (w h d)"), ALU.mult).then_inc(qk_g_ready, 1)

                def l3_head_scale(b):
                    dve.wait_ge(qk_rstd_ready, b + 1)
                    dve.wait_ge(qk_g_ready, b + 1)
                    at_least(dve, head_rows_transposed, 2 * b)
                    nc.vector.tensor_tensor(qk_pad[:].rearrange("p w h (r d) -> p (w h) r d", d=D3), qk_g[:].rearrange("p w h d -> p (w h) d").unsqueeze(2).broadcast_to([128, 2 * HEADS, 2, D3]),
                                            qk_rstd[:].rearrange("p w h -> p (w h)").unsqueeze(2).unsqueeze(3).broadcast_to([128, 2 * HEADS, 2, D3]), ALU.mult).then_inc(qk3_ready, 1)

                def l3_value_lows(b):
                    dve.wait_ge(v3_hi_ready, b + 1)
                    nc.vector.tensor_tensor(v3_parts[:, 1, :, 0:D3], bank[0][:, 0:N].rearrange("p (h d) -> p h d", d=D3), v3_parts[:, 0, :, 0:D3], ALU.subtract).then_inc(v3_copied, 1)

                def l3_row_lows(b):
                    dve.wait_ge(q3_hi_ready, b + 1)
                    nc.vector.tensor_tensor(q3_stack[:].rearrange("p g t -> p (g t)"), bank[2][:], q3_hi_part[:].rearrange("p g t -> p (g t)"), ALU.subtract).then_inc(q3_copied, 1)
                    dve.wait_ge(k3_hi_ready, b + 1)
                    nc.vector.scalar_tensor_tensor(out=k3_parts[:, 1].rearrange("p g t -> p (g t)"), in0=bank[3][:], scalar=float(D3 ** -0.5), in1=k3_parts[:, 0].rearrange("p g t -> p (g t)"),
                                                   op0 = ALU.mult, op1=ALU.subtract).then_inc(k3_copied, 1)

                def l3_maxima(b, g):
                    n = b * GROUPS + g
                    dve.wait_ge(scores3_ready, n + 1)
                    nc.vector.tensor_reduce(negmax3[:, g], bank[S3_BANK[g]][:].rearrange("p (c k) -> p c k", c=4), AXIS_X, ALU.max, negate=True).then_inc(max3_ready, 1)

                def l3_prob_lows(b, g):
                    n = b * GROUPS + g
                    dve.wait_ge(probs3_t_hi_ready, n + 1)
                    nc.vector.tensor_tensor(probs3_t[:, g % 2, 1].rearrange("p j t -> p (j t)"), bank[(6, 2)[g % 2]][:], probs3_t[:, g % 2, 0].rearrange("p j t -> p (j t)"), ALU.subtract).then_inc(probs3_t_lo_ready, 1)

                def l3_dve_body(b):
                    l3_maxima(b, 0)
                    l3_maxima(b, 1)
                    l3_maxima(b, 2)
                    if has_next(b):
                        l3_head_means(b + 1)
                    l3_maxima(b, 3)
                    if has_next(b):
                        l3_head_gain(b + 1)
                    for g in range(GROUPS):
                        l3_prob_lows(b, g)
                    if has_next(b):
                        l3_head_scale(b + 1)
                    dve.wait_ge(outputs3_ready, (b + 1) * GROUPS)
                    o_cols = bank[7][:, 0:HEADS * V3].rearrange("p (h v) -> p h v", v=V3)
                    nc.vector.reciprocal(rsum3[:], o_cols[:, :, D3]).then_inc(rsum3_ready, 1)
                    dve.wait_ge(rsum3_ready, b + 1)
                    nc.vector.tensor_tensor(o_sb[:].rearrange("p (h d) -> p h d", d=D3), o_cols[:, :, 0:D3],
                                            rsum3[:].unsqueeze(2).broadcast_to([128, HEADS, D3]), ALU.mult).then_inc(o_ready, 1)
                    if has_next(b):
                        l3_value_lows(b + 1)
                        l3_row_lows(b + 1)
                    dve.wait_ge(final_ready, b + 1)
                    at_least(dve, out_stored, b * 16)
                    nc.vector.tensor_copy(out_sb[:], bank[6][:, 0:N]).then_inc(out_ready, 1)

                l3_head_means(0)
                l3_head_gain(0)
                l3_head_scale(0)
                l3_value_lows(0)
                l3_row_lows(0)
                l3_batches(mybir.EngineType.DVE, l3_dve_body)


def kernel(**inputs):
    import concourse.bacc as bacc
    from concourse.bass_utils import run_bass_kernel_spmd

    def by_feature(v):
        return v.reshape(KC, 128, -1).transpose(1, 0, 2)

    def padded(w):
        p = np.zeros((T, GROUPS, 4, 32), w.dtype)
        for i in range(3):
            p[..., i * D0:(i + 1) * D0] = w.T.reshape(T, GROUPS, 4, D0)
        return p.reshape(T, GROUPS, 128)

    v = {k: np.asarray(x) for k, x in inputs.items()}
    x, cond = v["x"], v["cond_2048"]
    mask_row = 3 * D0 + 2
    low_q, low_k, consts = np.zeros(32), np.zeros(32), np.zeros((32, 9))
    low_q[D0:2 * D0] = 1.0
    low_k[2 * D0:3 * D0] = 1.0
    low_k[3 * D0 + 1] = 1.0
    consts[3 * D0:3 * D0 + 2, 0] = 1.0
    consts[mask_row, 0] = NEG
    consts[:, 1] = low_q / np.sqrt(D0)
    consts[:, 3] = low_k
    consts[3 * D0:3 * D0 + 2, 4] = 1.0
    consts[mask_row, 5] = -NEG
    consts[:, 6] = 1.0
    consts[mask_row, 6] = -1.0
    consts[mask_row, 7] = 1.0
    consts[D3:, 8] = 1.0
    rows = np.tile(consts, (4, 1)).astype(np.float32)
    arrays = {
        "x_cbn": x.transpose(1, 0, 2),
        "x_seq": x.reshape(B, T, KC, 128).transpose(3, 1, 2, 0).reshape(128, T * SLOT),
        "cond_rows": cond[None],
        "cond_t": by_feature(cond.T).reshape(128, SLOT),
        "wq_pad": padded(v["L0_cond_Wq"]), "wk_pad": padded(v["L0_cond_Wk"]), "wv_t": v["L0_cond_Wv"].T,
        "b0": v["L0_cond_b"].reshape(1, 1),
        "w_ih": by_feature(v["L1_cond_W_ih"]), "w_hh": by_feature(v["L1_cond_W_hh"]),
        "b_ih": v["L1_cond_b_ih"].reshape(6, 128).T, "b_hh": v["L1_cond_b_hh"].reshape(6, 128).T,
        "b_hn": v["L1_cond_b_hh"][None, 2 * N:],
        "coupling_t": by_feature(v["L2_cond_coupling"].T),
        "bias_t": np.repeat(v["L2_cond_bias"].reshape(KC, 128).T, B, axis=1),
        "w_emb": by_feature(v["L3_cond_W_emb"]), "b_emb": v["L3_cond_b_emb"].reshape(4, 128).T,
        "g_norm": v["L3_cond_g_norm"].reshape(KC, 128).T,
        "w_qkv": by_feature(v["L3_cond_W_qkv"]),
        "g_q": v["L3_cond_g_q"].reshape(1, 1, D3), "g_k": v["L3_cond_g_k"].reshape(1, 1, D3),
        "w_out": by_feature(v["L3_cond_W_out"]),
        "identity_in": np.eye(128, dtype=np.float32), "row_consts_in": rows, "select_in": np.repeat(np.eye(T // 8, dtype=np.float32)[:, :, None], 128, axis=2),
    }
    nc = bacc.Bacc("TRN2", target_bir_lowering=False, num_devices=1)
    args, ins = {}, {}
    for name, a in arrays.items():
        ins[f"in_{name}_dram"] = np.ascontiguousarray(a)
        args[name] = nc.dram_tensor(f"in_{name}_dram", a.shape, mybir.dt.from_np(a.dtype), kind="ExternalInput").ap()
    out = nc.dram_tensor("out_0_dram", [B, T, N], FP32, kind="ExternalOutput").ap()
    cond_resid_kernel(nc, **args, out=out.rearrange("b t n -> t b n"))
    r = run_bass_kernel_spmd(nc, [ins], core_ids=[0])
    return r.results[0]["out_0_dram"]
```
